# Optimizing a Trainium2 kernel written in Bass

```python
import numpy as np
import jax
import jax.numpy as jnp

def _softmax(x, axis=-1):
    return jax.nn.softmax(x, axis=axis)

def _gelu(x):
    return jax.nn.gelu(x, approximate=True)

def _silu(x):
    return jax.nn.silu(x)

def _sigmoid(x):
    return jax.nn.sigmoid(x)

def _layernorm(x, axis=-1, eps=1e-05):
    m = jnp.mean(x, axis=axis, keepdims=True)
    v = jnp.var(x, axis=axis, keepdims=True)
    return (x - m) / jnp.sqrt(v + eps)

def _scatter_add(tgt, idx, src, axis=0):
    return tgt.at[idx].add(src)

def _segment_sum(src, seg, n):
    return jax.ops.segment_sum(src, seg, n)
kernel_name = 'mk_decoder_preln_d1_seqx_r8_9f9217'

def setup_inputs(seed: int=0):
    np.random.seed(seed)
    _w = jnp.asarray

    def _rec_inputs():
        import jax
        import jax.numpy as jnp
        _rk = jax.random.key(seed)
        x = -0.0002928 + 1 * jax.random.normal(jax.random.fold_in(_rk, 1), (128, 64, 128), jnp.float32)
        _lenS = 64 - jax.random.randint(jax.random.fold_in(_rk, 7), (128,), 0, max(1, 64 // 4) + 1, jnp.int32)
        _lenS2 = 64 - jax.random.randint(jax.random.fold_in(_rk, 8), (128,), 0, max(1, 64 // 4) + 1, jnp.int32)
        _ctx_1024P = jax.random.normal(jax.random.fold_in(_rk, 11), (128, 16, 128), jnp.float32)
        _ctx_1024c = jax.random.dirichlet(jax.random.fold_in(_rk, 511), 0.3 * jnp.ones((16,), jnp.float32), (128, 64))
        _ctx_1024t = jnp.einsum('bsk,bkd->bsd', _ctx_1024c, _ctx_1024P)
        _ctx_1024t = _ctx_1024t * jax.lax.rsqrt(jnp.mean(jnp.square(_ctx_1024t)) + 1e-12) * 0.953939
        ctx_1024 = -1.39393e-06 + 0.999914 * (_ctx_1024t + 0.3 * jax.random.normal(jax.random.fold_in(_rk, 611), (128, 64, 128), jnp.float32))
        _validS = jnp.arange(64)[None, :] < _lenS[:, None]
        _validS2 = jnp.arange(64)[None, :] < _lenS2[:, None]
        _causal = jnp.tril(jnp.ones((64, 64), dtype=bool))
        mask_Bx1xSxS2_bf0 = jnp.logical_not(jnp.ones((128, 1, 64, 64), dtype=bool))
        return (x, ctx_1024, mask_Bx1xSxS2_bf0)
    x, ctx_1024, mask_Bx1xSxS2_bf0 = _rec_inputs()

    def _L0_attn_setup():
        import math
        import jax, jax.numpy as jnp
        import numpy as np
        D_MODEL = 128
        N_HEADS = 16
        HEAD_DIM = D_MODEL // N_HEADS

        def build_rope_cache(seq_len, head_dim):
            half = head_dim // 2
            inv_freq = 1.0 / 10000.0 ** (jnp.arange(half, dtype=jnp.float32) / half)
            pos = jnp.arange(seq_len, dtype=jnp.float32)
            angles = jnp.outer(pos, inv_freq)
            return (jnp.cos(angles)[None, None], jnp.sin(angles)[None, None])

        def apply_rope(x, cos, sin):
            half = x.shape[-1] // 2
            x1, x2 = (x[..., :half], x[..., half:])
            return jnp.concatenate((x1 * cos - x2 * sin, x1 * sin + x2 * cos), axis=-1)
        key = jax.random.key(seed)
        ks = jax.random.split(key, 5)
        B, S = (2, 256)
        bound = 1.0 / math.sqrt(D_MODEL)
        x = jax.random.normal(ks[0], (B, S, D_MODEL), dtype=jnp.float32)
        qkv_w = jax.random.uniform(ks[1], (3 * D_MODEL, D_MODEL), minval=-bound, maxval=bound, dtype=jnp.float32)
        qkv_b = jax.random.uniform(ks[2], (3 * D_MODEL,), minval=-bound, maxval=bound, dtype=jnp.float32)
        out_w = jax.random.uniform(ks[3], (D_MODEL, D_MODEL), minval=-bound, maxval=bound, dtype=jnp.float32)
        out_b = jax.random.uniform(ks[4], (D_MODEL,), minval=-bound, maxval=bound, dtype=jnp.float32)
        return {'x': x, 'qkv_w': qkv_w, 'qkv_b': qkv_b, 'out_w': out_w, 'out_b': out_b}
    _L0_attn_all = _L0_attn_setup()
    _L0_attn_in = {k: v for k, v in _L0_attn_all.items() if k in ('qkv_w', 'qkv_b', 'out_w', 'out_b')}
    del _L0_attn_all

    def _L0_xattn_setup():
        import jax, jax.numpy as jnp
        import numpy as np
        B, S, D, H = (2, 256, 128, 16)
        HD = D // H
        LN_EPS = 1e-05

        def _linear(x, w, b):
            return jnp.einsum('bsd,od->bso', x, w) + b

        def _split_heads(x):
            b, s, _ = x.shape
            return x.reshape(b, s, H, HD).transpose(0, 2, 1, 3)
        key = jax.random.key(seed)
        ks = jax.random.split(key, 14)
        w = 0.02
        return {'q': jax.random.normal(ks[0], (B, S, D), jnp.float32), 'k': jax.random.normal(ks[1], (B, S, D), jnp.float32), 'v': jax.random.normal(ks[2], (B, S, D), jnp.float32), 'mask': jnp.zeros((B, 1, S, S), dtype=bool), 'training': 0, 'wq_w': jax.random.normal(ks[3], (D, D), jnp.float32) * w, 'wq_b': jnp.zeros((D,), jnp.float32), 'wk_w': jax.random.normal(ks[4], (D, D), jnp.float32) * w, 'wk_b': jnp.zeros((D,), jnp.float32), 'wv_w': jax.random.normal(ks[5], (D, D), jnp.float32) * w, 'wv_b': jnp.zeros((D,), jnp.float32), 'wo_w': jax.random.normal(ks[6], (D, D), jnp.float32) * w, 'wo_b': jnp.zeros((D,), jnp.float32), 'ln_g': jnp.ones((D,), jnp.float32), 'ln_b': jnp.zeros((D,), jnp.float32)}
    _L0_xattn_all = _L0_xattn_setup()
    _L0_xattn_in = {k: v for k, v in _L0_xattn_all.items() if k in ('wq_w', 'wq_b', 'wk_w', 'wk_b', 'wv_w', 'wv_b', 'wo_w', 'wo_b', 'ln_g', 'ln_b')}
    del _L0_xattn_all

    def _L0_ffn_setup():
        import jax, jax.numpy as jnp
        import numpy as np
        E, D, F = (8, 128, 512)
        LN_EPS = 1e-05
        key = jax.random.key(seed)
        k = jax.random.split(key, 8)
        x = jax.random.normal(k[0], (4, 256, D), jnp.float32)
        centroids = jax.random.normal(k[1], (E, D), jnp.float32) * 0.1
        ln_g = jnp.ones((E, D), jnp.float32)
        ln_b = jnp.zeros((E, D), jnp.float32)
        w1 = jax.random.normal(k[2], (E, F, D), jnp.float32) * (1.0 / np.sqrt(D))
        b1 = jnp.zeros((E, F), jnp.float32)
        w2 = jax.random.normal(k[3], (E, D, F), jnp.float32) * (1.0 / np.sqrt(F))
        b2 = jnp.zeros((E, D), jnp.float32)
        return {'input_features': x, 'centroids': centroids, 'ln_g': ln_g, 'ln_b': ln_b, 'w1': w1, 'b1': b1, 'w2': w2, 'b2': b2}
    _L0_ffn_all = _L0_ffn_setup()
    _L0_ffn_in = {k: v for k, v in _L0_ffn_all.items() if k in ('centroids', 'ln_g', 'ln_b', 'w1', 'b1', 'w2', 'b2')}
    del _L0_ffn_all
    return {'x': x, 'ctx_1024': ctx_1024, 'mask_Bx1xSxS2_bf0': mask_Bx1xSxS2_bf0, 'L0_attn_qkv_w': _L0_attn_in['qkv_w'], 'L0_attn_qkv_b': _L0_attn_in['qkv_b'], 'L0_attn_out_w': _L0_attn_in['out_w'], 'L0_attn_out_b': _L0_attn_in['out_b'], 'L0_xattn_wq_w': _L0_xattn_in['wq_w'], 'L0_xattn_wq_b': _L0_xattn_in['wq_b'], 'L0_xattn_wk_w': _L0_xattn_in['wk_w'], 'L0_xattn_wk_b': _L0_xattn_in['wk_b'], 'L0_xattn_wv_w': _L0_xattn_in['wv_w'], 'L0_xattn_wv_b': _L0_xattn_in['wv_b'], 'L0_xattn_wo_w': _L0_xattn_in['wo_w'], 'L0_xattn_wo_b': _L0_xattn_in['wo_b'], 'L0_xattn_ln_g': _L0_xattn_in['ln_g'], 'L0_xattn_ln_b': _L0_xattn_in['ln_b'], 'L0_ffn_centroids': _L0_ffn_in['centroids'], 'L0_ffn_ln_g': _L0_ffn_in['ln_g'], 'L0_ffn_ln_b': _L0_ffn_in['ln_b'], 'L0_ffn_w1': _L0_ffn_in['w1'], 'L0_ffn_b1': _L0_ffn_in['b1'], 'L0_ffn_w2': _L0_ffn_in['w2'], 'L0_ffn_b2': _L0_ffn_in['b2']}

def reference(x, ctx_1024, mask_Bx1xSxS2_bf0, L0_attn_qkv_w, L0_attn_qkv_b, L0_attn_out_w, L0_attn_out_b, L0_xattn_wq_w, L0_xattn_wq_b, L0_xattn_wk_w, L0_xattn_wk_b, L0_xattn_wv_w, L0_xattn_wv_b, L0_xattn_wo_w, L0_xattn_wo_b, L0_xattn_ln_g, L0_xattn_ln_b, L0_ffn_centroids, L0_ffn_ln_g, L0_ffn_ln_b, L0_ffn_w1, L0_ffn_b1, L0_ffn_w2, L0_ffn_b2):
    import jax
    import jax.numpy as jnp

    def _L0_attn_ref(x, qkv_w, qkv_b, out_w, out_b):
        import math
        import jax, jax.numpy as jnp
        import numpy as np
        D_MODEL = 128
        N_HEADS = 16
        HEAD_DIM = D_MODEL // N_HEADS

        def build_rope_cache(seq_len, head_dim):
            half = head_dim // 2
            inv_freq = 1.0 / 10000.0 ** (jnp.arange(half, dtype=jnp.float32) / half)
            pos = jnp.arange(seq_len, dtype=jnp.float32)
            angles = jnp.outer(pos, inv_freq)
            return (jnp.cos(angles)[None, None], jnp.sin(angles)[None, None])

        def apply_rope(x, cos, sin):
            half = x.shape[-1] // 2
            x1, x2 = (x[..., :half], x[..., half:])
            return jnp.concatenate((x1 * cos - x2 * sin, x1 * sin + x2 * cos), axis=-1)
        B, S, D = x.shape
        H, Hd = (N_HEADS, HEAD_DIM)
        qkv = x @ qkv_w.T + qkv_b
        qkv = qkv.reshape(B, S, 3, H, Hd).transpose(2, 0, 3, 1, 4)
        q, k, v = (qkv[0], qkv[1], qkv[2])
        cos, sin = build_rope_cache(S, Hd)
        q = apply_rope(q, cos, sin)
        k = apply_rope(k, cos, sin)
        scores = jnp.einsum('bhqd,bhkd->bhqk', q, k) / math.sqrt(Hd)
        causal = jnp.triu(jnp.ones((S, S), dtype=bool), k=1)
        scores = jnp.where(causal, jnp.finfo(scores.dtype).min, scores)
        attn = jax.nn.softmax(scores, axis=-1)
        out = jnp.einsum('bhqk,bhkd->bhqd', attn, v)
        out = out.transpose(0, 2, 1, 3).reshape(B, S, D)
        return out @ out_w.T + out_b

    def _L0_xattn_ref(q, k, v, mask, training, wq_w, wq_b, wk_w, wk_b, wv_w, wv_b, wo_w, wo_b, ln_g, ln_b):
        import jax, jax.numpy as jnp
        import numpy as np
        B, S, D, H = (2, 256, 128, 16)
        HD = D // H
        LN_EPS = 1e-05

        def _linear(x, w, b):
            return jnp.einsum('bsd,od->bso', x, w) + b

        def _split_heads(x):
            b, s, _ = x.shape
            return x.reshape(b, s, H, HD).transpose(0, 2, 1, 3)
        residual = q
        Q = _split_heads(_linear(q, wq_w, wq_b))
        K = _split_heads(_linear(k, wk_w, wk_b))
        V = _split_heads(_linear(v, wv_w, wv_b))
        dk = jnp.sqrt(jnp.asarray(HD, jnp.float16)).astype(jnp.float32) + 1e-08
        score = jnp.einsum('bhqd,bhkd->bhqk', Q, K) / dk
        attn = jnp.where(mask, -jnp.inf, score)
        ctx = jnp.einsum('bhqk,bhkd->bhqd', attn, V)
        b, _, s, _ = ctx.shape
        ctx = ctx.transpose(0, 2, 1, 3).reshape(b, s, D)
        o = _linear(ctx, wo_w, wo_b)
        x = residual + o
        mu = jnp.mean(x, axis=-1, keepdims=True)
        var = jnp.mean(jnp.square(x - mu), axis=-1, keepdims=True)
        return ln_g * (x - mu) * jax.lax.rsqrt(var + LN_EPS) + ln_b

    def _L0_ffn_ref(input_features, centroids, ln_g, ln_b, w1, b1, w2, b2):
        import jax, jax.numpy as jnp
        import numpy as np
        E, D, F = (8, 128, 512)
        LN_EPS = 1e-05
        x = input_features.reshape(-1, D)
        aff = jax.lax.stop_gradient(x) @ centroids.T
        assign = jnp.argmax(aff, axis=1)
        onehot = jax.nn.one_hot(assign, E, dtype=x.dtype)
        mu = jnp.mean(x, axis=-1, keepdims=True)
        var = jnp.mean((x - mu) ** 2, axis=-1, keepdims=True)
        xhat = (x - mu) * jax.lax.rsqrt(var + LN_EPS)
        xn = xhat[None, :, :] * ln_g[:, None, :] + ln_b[:, None, :]
        h = jax.nn.relu(jnp.einsum('etd,efd->etf', xn, w1) + b1[:, None, :])
        y = x[None, :, :] + jnp.einsum('etf,edf->etd', h, w2) + b2[:, None, :]
        alpha = jax.nn.sigmoid(x @ centroids.T)
        a = alpha.T[:, :, None]
        gated = a * y + (1.0 - a) * x[None, :, :]
        out = jnp.einsum('te,etd->td', onehot, gated)
        return out.reshape(input_features.shape)
    x = x + _L0_attn_ref(_layernorm(x, axis=-1), L0_attn_qkv_w, L0_attn_qkv_b, L0_attn_out_w, L0_attn_out_b)
    x = x + _L0_xattn_ref(_layernorm(x, axis=-1), ctx_1024, ctx_1024, mask_Bx1xSxS2_bf0, 0, L0_xattn_wq_w, L0_xattn_wq_b, L0_xattn_wk_w, L0_xattn_wk_b, L0_xattn_wv_w, L0_xattn_wv_b, L0_xattn_wo_w, L0_xattn_wo_b, L0_xattn_ln_g, L0_xattn_ln_b)
    x = x + _L0_ffn_ref(_layernorm(x, axis=-1), L0_ffn_centroids, L0_ffn_ln_g, L0_ffn_ln_b, L0_ffn_w1, L0_ffn_b1, L0_ffn_w2, L0_ffn_b2)
    return x

_drawn_inputs = setup_inputs


def setup_inputs(seed=0):
    import zlib

    import numpy as np

    out = dict(_drawn_inputs(seed))
    spreads = {'L0_xattn_wq_b': (0.0, 0.1),
     'L0_xattn_wk_b': (0.0, 0.1),
     'L0_xattn_wv_b': (0.0, 0.1),
     'L0_xattn_wo_b': (0.0, 0.1),
     'L0_xattn_ln_g': (1.0, 0.2),
     'L0_xattn_ln_b': (0.0, 0.1),
     'L0_ffn_ln_g': (1.0, 0.2),
     'L0_ffn_ln_b': (0.0, 0.419),
     'L0_ffn_b1': (0.0, 0.43),
     'L0_ffn_b2': (0.0, 0.311)}
    factors = {}
    for name, (base, spread) in spreads.items():
        noise = np.random.default_rng([zlib.crc32(name.encode()), seed]).standard_normal(out[name].shape)
        drawn = base * np.exp(spread * noise) if base else spread * noise
        out[name] = jnp.asarray(drawn.astype(out[name].dtype))
    for name, factor in factors.items():
        out[name] = (out[name] * factor).astype(out[name].dtype)
    return out
```

```python
from contextlib import ExitStack

import numpy as np

import concourse.bass as bass
from concourse import mybir

FP32 = mybir.dt.float32
F32R = mybir.dt.float32r
BF16 = mybir.dt.bfloat16
I32 = mybir.dt.int32
U32 = mybir.dt.uint32
ALU = mybir.AluOpType
ACT = mybir.ActivationFunctionType
AX = mybir.AxisListType

P = 128
D = 128
H, HD = 16, 8
SQ = 64
J = 2
TG = J * P
E, F = 8, 512
FC = F // P
EPS = 1e-5
NEG = -1.0e30
ROW = 136
C_A, C_B, C_R, C_C, C_AL, C_ID = range(D, D + 6)


class Steps:

    def __init__(self, sem, names, total):
        self.sem, self.names, self.next, self.total = sem, names.split(), 0, total

    def at(self, n, name):
        if isinstance(n, int):
            n = min(n, self.total - 1)
        return n * len(self.names) + (self.names.index(name) + 1)

    def done(self, name):
        assert self.names[self.next] == name, (self.names[self.next], name)
        self.next = (self.next + 1) % len(self.names)
        return self.sem, 1


class Group:

    def __init__(self, c, it=None):
        self.c, self.it = c, it
        self.n = c if it is None else it * 2 + c
        self.half = c // 2 if it is None else it + c // 2
        self.par = c % 2

    def back(self, k):
        return Group(self.c - k, self.it)

    def within(self, total):
        return self.it is not None or 0 <= self.c < total


class Block:

    def __init__(self, c, it=None, step=0):
        self.c, self.it, self.step = c, it, step
        self.n = c if it is None else it * step + c
        self.half = c // 2 if it is None else it * (step // 2) + c // 2
        self.quarter = c // 4 if it is None or step < 4 else it * (step // 4) + c // 4

    def on(self, k):
        return Block(self.c + k, self.it, self.step)


class Waits:
    passed = None


def wait_for(eng, sem, v, alone=False):
    if not isinstance(v, int):
        eng.wait_ge(sem, v)
        if alone or eng.engine in (mybir.EngineType.Pool, mybir.EngineType.SP):
            eng.sem_inc(Waits.passed, 1)
    elif v > 0:
        eng.wait_ge(sem, v)


def wait(eng, steps, n, name, alone=False):
    wait_for(eng, steps.sem, steps.at(n, name), alone)




def wait_freed(eng, g, *steps):
    for st, n, name in steps if g.it is None else steps[:1]:
        wait(eng, st, n, name)


def wait_dma(eng, sems, g, count=1):
    wait_for(eng, sems[g.par], (g.half + 1) * (16 * count))


def decoder_kernel(nc, x, ctx, mask, wself, wcross, bcol, brow, cent, w1t, lngb, b1c, w2t, b2r,
                   consts, negq, negk, padc, out):
    NB = x.shape[0]
    T = NB * SQ
    NT = T // P
    NG = NT // J
    CAP = T + P
    NBLK = NT + E
    x_rows = x.rearrange("b s d -> (b s) d")
    c_rows = ctx.rearrange("b s d -> (b s) d")
    o_rows = out.rearrange("b s d -> (b s) d")
    m_rows = mask.rearrange("b o s k -> (b o s) k").rearrange("(t p) k -> p t k", p=P)
    rows = nc.dram_tensor("expert_rows", [E * CAP + P, ROW], FP32, kind="Internal").ap()

    es = ExitStack()
    with es:
        def sb(name, shape, dt=FP32):
            return es.enter_context(nc.sbuf_tensor(name, shape, dt))

        def two(name, shape, dt=FP32):
            return [sb(f"{name}_{i}", shape, dt) for i in range(2)]

        def sem(name):
            return es.enter_context(nc.semaphore(name))

        ws = sb("ws", [P, 6, D])
        WQ, WQR, WK, WKR, WV, WO = (ws[:, i, :] for i in range(6))
        wc = sb("wc", [P, 4, D])
        bc = sb("bc", [P, 6])
        br = sb("br", [P, 6, D])
        BO, BO2, LNG, LNB, BK2, BV2 = (br[:, i, :] for i in range(6))
        cT = sb("cT", [P, E])
        cf = sb("cf", [P, 4 * SQ + D + P + 4 + 4 + E + 2 + P + NBLK])
        o = 0
        rope = [cf[:, i * SQ:(i + 1) * SQ] for i in range(4)]
        o += 4 * SQ
        headmask = cf[:, o:o + D]
        o += D
        identf = cf[:, o:o + P]
        o += P
        own4, own4s = cf[:, o:o + 4], cf[:, o + 4:o + 8]
        o += 8
        iota8 = cf[:, o:o + E]
        o += E
        tok0 = cf[:, o:o + J]
        o += J
        trif = cf[:, o:o + P]
        o += P
        blkno = cf[:, o:o + NBLK]
        nqf = sb("nqf", [P, 512])
        nkf = sb("nkf", [P, 512])
        negq_b = sb("negq_b", [P, 512], BF16)
        negk_b = sb("negk_b", [P, 512], BF16)
        ident_b = sb("ident_b", [P, P], BF16)
        tri_b = sb("tri_b", [P, P], BF16)
        ones_b = sb("ones_b", [P, P], BF16)
        half = sb("half", [P, J])
        bvx = sb("bvx", [P, P])
        w1 = sb("w1", [P, E, F])
        w2 = sb("w2", [P, E, FC, D])
        gb = sb("gb", [P, 2, E])
        b1 = sb("b1", [P, E, FC])
        b2 = sb("b2", [P, E, D])
        mk = sb("mk", [P, NT, SQ // 4], I32)
        pen = sb("pen", [P, NT])
        tokid = sb("tokid", [P, J])
        xin = two("xin", [P, J, D])
        xn = two("xn", [P, J, D])
        xT = sb("xT", [P, TG])
        t1 = two("t1_", [P, TG])
        t2 = two("t2_", [P, TG])
        qf = sb("qf", [P, TG])
        kf = sb("kf", [P, TG])
        qhi = sb("qhi", [P, TG], F32R)
        qlo = sb("qlo", [P, TG], F32R)
        khi = sb("khi", [P, 2 * J, P], F32R)
        klo = sb("klo", [P, 2 * J, P], F32R)
        qst = two("qst", [P, 4, TG], F32R)
        qex = sb("qex", [P, 4, 4, TG], F32R)
        kst = two("kst", [P, 4, 2 * J, P], F32R)
        qz = two("qz", [P, 4, 2 * J, P], F32R)
        kex = two("kex", [P, 4, TG], F32R)
        vau = two("vau", [P, J, H, 32])
        mx = sb("mx", [P, J, H])
        mt = sb("mt", [P, J, 4, 2, 4], BF16)
        prob = two("prob", [P, 512])
        ot = sb("ot", [P, J, 4, 2, 2, 16])
        rd = sb("rd", [P, J, 4, 2, 2])
        on = sb("on", [P, J, 2, 2, 4, HD])
        ont = two("ont", [P, J, 2, 2, 32])
        xr = two("xr", [P, J, D])
        cin = two("cin", [P, J, D])
        cxT = sb("cxT", [P, TG])
        x1 = sb("x1", [P, J, D])
        xn1 = sb("xn1", [P, J, D])
        xT1 = sb("xT1", [P, TG])
        q2 = sb("q2", [P, TG])
        k2 = sb("k2", [P, J, 2, D])
        v2 = sb("v2", [P, J, D])
        mt2 = sb("mt2", [P, J, 2, D])
        r2s = sb("r2s", [P, J, 2, D])
        y1 = sb("y1", [P, J, D])
        yn = sb("yn", [P, J, D])
        pay = two("pay", [P, J, ROW])
        xp = sb("xp", [P, J, D])
        xpT = sb("xpT", [P, TG])
        stat = {s: sb(f"stat_{s}", [P, J, 6]) for s in "LTURQ"}
        mv = {s: sb(f"mv_{s}", [P, J, 2]) for s in "LTURQ"}
        ve = {s: sb(f"ve_{s}", [P, J]) for s in "LTURQ"}
        rs = {s: sb(f"rs_{s}", [P, J]) for s in "LTURQ"}
        rc = sb("rc", [P, J])
        rm = sb("rm", [P, J])
        aff = sb("aff", [P, J, E])
        mx8 = sb("mx8", [P, J, 8])
        ix8 = sb("ix8", [P, J, 8], U32)
        idf = sb("idf", [P, J])
        ohb = sb("ohb", [P, J, E], BF16)
        ea = sb("ea", [P, J])
        ea1 = sb("ea1", [P, J])
        cnt = sb("cnt", [P, 2, E])
        rk = sb("rk", [P, J, E])
        slf = sb("slf", [P, J])
        sli = two("sli", [P, J], I32)
        ti = sb("ti", [P, E], I32)
        nbf = sb("nbf", [P, E])
        cum = sb("cum", [P, E])
        geb = sb("geb", [P, NBLK, E])
        gnb = sb("gnb", [P, NBLK, E])
        bex = sb("bex", [P, NBLK])
        bst = sb("bst", [P, NBLK])
        btf = sb("btf", [P, 2, NBLK])
        bti = sb("bti", [P, 2, NBLK], I32)
        prf = sb("prf", [P, E])
        pri = sb("pri", [P, E], I32)
        padt = sb("padt", [P, ROW])
        rb = [sb(f"rb{i}", [P, ROW]) for i in range(4)]
        idi = two("idi", [P, 1], I32)
        xh = two("xh", [P, D])
        bs = [sb(f"bs{i}", [P, D]) for i in range(4)]
        xhT = two("xhT", [P, P])
        hs = two("hs", [P, F])
        hT = two("hT", [P, FC, P])
        yb = two("yb", [P, D])
        yo = two("yo", [P, D])

        bank = [es.enter_context(nc.psum_tensor(f"bank{i}", [P, 512], FP32)) for i in range(8)]
        M = bank[0:3]
        B1 = bank[3:5]
        B2 = bank[5:7]
        BO_ = bank[7]

        pe_f = Steps(sem("pe_front"), "xT QQ KK V", NG)
        pe_s = Steps(sem("pe_scores_for_max"), "s0 s1 s2 s3 m0 m1", NG)
        pe_a = Steps(sem("pe_attention"), "s0 s1 p0 s2 p1 s3 p2 p3", NG)
        pe_t = Steps(sem("pe_cross"), "out cT xT KV Q2 gram R o2", NG)
        pe_r = Steps(sem("pe_route"), "xT aff rank", NG)
        ac_f = Steps(sem("act_front"), "xT qhi khi V0 V1", NG)
        ac_s = Steps(sem("act_maxima_rows"), "m0 m1", NG)
        ac_a = Steps(sem("act_exp"), "e0 e1 e2 e3", NG)
        ac_t = Steps(sem("act_cross"), "cT xT Q2 R", NG)
        ac_r = Steps(sem("act_route"), "xT ea", NG)
        dv_l = Steps(sem("dve_norm_x"), "b0 b1 a0 a1 n0 n1", NG)
        dv_f = Steps(sem("dve_front"), "q1 q2 z0 z1 z2 z3 k1 k2 x0 x1 x2 x3", NG)
        dv_s = Steps(sem("dve_maxima"), "m0 m1 m2 m3 hi lo e0 e1", NG)
        dv_a = Steps(sem("dve_attention"), "ot rd n0 n1 n2 n3 tr", NG)
        dv_t = Steps(sem("dve_cross"), "x1 b0 b1 a0 a1 n0 n1 k0 k1 v mt y0 y1 c0 c1 d0 d1 z0 z1 x2", NG)
        dv_r = Steps(sem("dve_route"), "b0 b1 a0 a1 c p0 p1 d0 d1 e0 e1 cm A B R C id aff g0 g1 "
                     "i0 i1 idf idm o0 o1 al1 al c1 rk pr sl s2 si tot nx tok", NG)
        po_l = Steps(sem("pool_norm_x"), "eps pow", NG)
        po_f = Steps(sem("pool_front"), "qf qlo kf klo", NG)
        po_s = Steps(sem("pool_expand"), "e2 e3", NG)
        po_t = Steps(sem("pool_cross"), "xb eps pow xnb x1b eps2 pow2 zg", NG)
        po_r = Steps(sem("pool_route"), "eps pow eps2 pow2", NG)
        d_x = [sem(f"dma_x{i}") for i in range(2)]
        d_xr = [sem(f"dma_x_again{i}") for i in range(2)]
        d_c = [sem(f"dma_ctx{i}") for i in range(2)]
        d_q = [sem(f"dma_q_stack{i}") for i in range(2)]
        d_k = [sem(f"dma_k_stack{i}") for i in range(2)]
        d_s = [sem(f"dma_scatter{i}") for i in range(2)]
        d_const = sem("dma_constants")
        d_weights = sem("dma_ffn_weights")
        d_pad = sem("dma_pad_rows")
        s_vec = sem("setup_vector")
        s_pool = sem("setup_pool")
        s_pe = sem("setup_tensor")
        s_tab = sem("block_table")
        s_zero = sem("setup_vector_zeros")
        s_pz = sem("setup_pool_zeros")
        s_mask = sem("setup_mask")
        s_chain = sem("block_table_chain")
        d_rb = [sem(f"dma_rows{i}") for i in range(4)]
        d_o = [sem(f"dma_out{i}") for i in range(2)]
        ffn = {k: Steps(sem(f"ffn_{k}"), k, NBLK) for k in
               ("pe_xT", "pe_h", "pe_hT", "pe_y", "act_xT", "act_relu", "dve_xh", "dve_h", 
                "dve_yb", "dve_yo", "pool_base", "pool_id")}

        Waits.passed = sem("waits_passed")

        def wait_b(eng, kind, n):
            wait(eng, ffn[kind], n, kind)

        def wait_rows(eng, b):
            wait_for(eng, d_rb[b.c % 4], (b.quarter + 1) * 16)

        def wait_out(eng, b):
            wait_for(eng, d_o[b.c % 2], b.half * 16)

        block = es.enter_context(nc.Block())

        FIRST, TOTAL = 6, NG + 4
        LOOPS = (NG - 1 - FIRST) // 2

        def rounds(eng, one):
            for i in range(FIRST):
                one(Group(i))
            with eng.Fori(0, LOOPS) as it:
                one(Group(FIRST, it))
                one(Group(FIRST + 1, it))
            for i in range(FIRST + 2 * LOOPS, TOTAL):
                one(Group(i))

        N_CONST = 13

        @block.sync
        def _(sp):
            for dst, src in ((ws[:, :, :], wself), (wc[:, :, :], wcross), (bc[:, :], bcol),
                             (cT[:, :], cent), (cf[:, :], consts), (nqf[:, :], negq), (nkf[:, :], negk),
                             (br[:, :, :].rearrange("p a d -> p (a d)"), brow.partition_broadcast(P)),
                             (gb[:, :, :], lngb), (b1[:, :, :], b1c), (padt[:, :], padc),
                             (b2[:, :, :].rearrange("p e d -> p (e d)"), b2r.partition_broadcast(P)),
                             (mk[:, :, :], m_rows)):
                sp.dma_start(dst, src).then_inc(d_const, 16)
            sp.dma_start(w1[:, :, :], w1t).then_inc(d_weights, 16)
            sp.dma_start(w2[:, :, :, :], w2t).then_inc(d_weights, 16)
            sp.wait_ge(d_const, 16 * N_CONST)
            sp.dma_start(rows[E * CAP:E * CAP + P, :], padt[:, :]).then_inc(d_pad, 16)
            sp.wait_ge(s_vec, 1)
            sp.wait_ge(s_pool, 1)

            def load(g):
                wait(sp, dv_l, g.n - 2, "n1")
                sp.dma_start(xin[g.par][:, :, :],
                             x_rows[bass.ds(g.n * TG, TG), :].rearrange("(j p) d -> p j d", j=J)
                             ).then_inc(d_x[g.par], 16)

            def one(g):
                if g.c == 0 and g.it is None:
                    load(Group(0))
                if g.back(-1).within(NG):
                    load(g.back(-1))
                t = g.back(2)
                if t.within(NG):
                    wait(sp, dv_t, t.n - 2, "x1")
                    sp.dma_start(xr[t.par][:, :, :],
                                 x_rows[bass.ds(t.n * TG, TG), :].rearrange("(j p) d -> p j d", j=J)
                                 ).then_inc(d_xr[t.par], 16)
                    wait(sp, pe_t, t.n - 2, "cT")
                    sp.dma_start(cin[t.par][:, :, :],
                                 c_rows[bass.ds(t.n * TG, TG), :].rearrange("(j p) d -> p j d", j=J)
                                 ).then_inc(d_c[t.par], 16)
                if g.within(NG):
                    wait(sp, dv_s, g.n - 2, "e1")
                    wait(sp, po_s, g.n - 2, "e3")
                    wait(sp, ac_f, g.n, "qhi")
                    wait(sp, po_f, g.n, "qlo")
                    for s, src in enumerate((qhi, qhi, qlo)):
                        for r in range(4):
                            sp.dma_start(qst[g.par][32 * s:32 * s + 32, r, :].bitcast(FP32),
                                         src[32 * r:32 * r + 32, :].bitcast(FP32)).then_inc(d_q[g.par], 16)
                    wait(sp, pe_a, g.n - 2, "s3")
                    wait(sp, ac_f, g.n, "khi")
                    wait(sp, po_f, g.n, "klo")
                    for s, src in enumerate((khi, klo, khi)):
                        for r in range(4):
                            sp.dma_start(kst[g.par][32 * s:32 * s + 32, r, :, :].bitcast(FP32),
                                         src[32 * r:32 * r + 32, :, :].bitcast(FP32)).then_inc(d_k[g.par], 16)

            rounds(nc.sync, one)

            sp.wait_ge(s_tab, 1)
            for e in range(E):
                at = nc.sync.value_load(pri[0:1, e:e + 1], min_val=0, max_val=(e + 1) * CAP - P)
                sp.dma_start(rows[bass.ds(at, P), :], padt[:, :]).then_inc(d_pad, 16)
            sp.wait_ge(d_pad, 16 * (E + 1))
            sp.wait_ge(d_s[0], 16 * J * ((NG + 1) // 2))
            sp.wait_ge(d_s[1], 16 * J * (NG // 2))

            def fetch(b):
                wait_b(sp, "pool_id", b.n - 4)
                wait_b(sp, "dve_yo", b.n - 4)
                at = nc.sync.value_load(bti[0:1, 1, bass.ds(b.n, 1)], min_val=0, max_val=E * CAP)
                sp.dma_start(rb[b.c % 4][:, :], rows[bass.ds(at, P), :]).then_inc(d_rb[b.c % 4], 16)

            for c in range(4):
                fetch(Block(c))
            with nc.sync.Fori(1, NBLK // 4) as it:
                for u in range(4):
                    fetch(Block(u, it, 4))
            for i in range(2):
                sp.wait_ge(d_o[i], 16 * NBLK // 2)

        @block.tensor
        def _(pe):
            mm, tr = nc.tensor.matmul, nc.tensor.transpose
            pe.wait_ge(d_const, 16 * N_CONST)
            pe.wait_ge(s_vec, 2)
            mm(M[0][:, 0:D], bvx[:, :], WO, start=True, stop=True).then_inc(s_pe, 1)
            pe.wait_ge(d_weights, 32)
            for e in range(E):
                for c in range(FC):
                    last = mm(M[1][:, e * FC + c:e * FC + c + 1], w1[:, e, c * P:(c + 1) * P],
                              gb[:, 1, e:e + 1], start=True, stop=True)
            last.then_inc(s_pe, 1)
            pe.wait_ge(s_vec, 4)

            def one(g):
                f, s, a, t, r = g, g.back(1), g.back(2), g.back(3), g.back(4)
                F_, S_, A_, T_, R_ = (q.within(NG) for q in (f, s, a, t, r))

                def s2(k):
                    j, c = k // 2, k % 2
                    if k < 2:
                        wait(pe, ac_a, a.n - 1, f"e{k + 2}")
                    else:
                        wait(pe, ac_a, a.n, f"e{k - 2}")
                    mm(B2[c][:, :], ident_b[:, :], negk_b[:, :], start=True, stop=False)
                    for r_ in range(2):
                        for b in range(2):
                            q = 2 * j + b
                            last = mm(B2[c][:, 256 * r_:256 * r_ + 256], kst[a.par][:, 2 * c + r_, q, :],
                                      qex[:, 2 * c + r_, :, q * SQ:(q + 1) * SQ],
                                      start=False, stop=r_ == 1 and b == 1)
                    last.then_inc(*pe_a.done(f"s{k}"))

                def pv(k):
                    j, c = k // 2, k % 2
                    wait(pe, ac_a, a.n, f"e{k}")
                    if k == 0:
                        wait(pe, dv_a, a.n - 1, "ot")
                    for i in range(8):
                        h = 8 * c + i
                        o_ = BO_[32 * (h // 4):32 * (h // 4) + 32,
                                 j * 256 + (h % 4) * SQ:j * 256 + (h % 4 + 1) * SQ]
                        last = mm(o_, vau[a.par][:, j, h, :], prob[k % 2][:, i * SQ:(i + 1) * SQ],
                                  start=True, stop=True, tile_position=(0, 32 * (h // 4)))
                    last.then_inc(*pe_a.done(f"p{k}"))

                def s1(k):
                    j, c = k // 2, k % 2
                    if k < 2:
                        wait(pe, dv_s, s.n - 1, f"m{k + 2}")
                    else:
                        wait(pe, dv_s, s.n, f"m{k - 2}")
                    mm(B1[c][:, :], ident_b[:, :], negq_b[:, :], start=True, stop=False)
                    for r_ in range(2):
                        for b in range(2):
                            q = 2 * j + b
                            last = mm(B1[c][:, 256 * r_:256 * r_ + 256], qz[s.par][:, 2 * c + r_, q, :],
                                      kex[s.par][:, :, q * SQ:(q + 1) * SQ],
                                      start=False, stop=r_ == 1 and b == 1)
                    last.then_inc(*pe_s.done(f"s{k}"))

                if T_:
                    wait(pe, dv_a, t.n, "tr")
                    wait_freed(pe, g, (ac_t, t.n - 1, "R"), (dv_f, f.n - 1, "q2"))
                    for j in range(J):
                        last = mm(M[0][:, j * D:(j + 1) * D],
                                  ont[t.par][:, j, :, :, :].rearrange("p b q t -> p (b q t)"), WO,
                                  start=True, stop=True)
                    last.then_inc(*pe_t.done("out"))
                if F_:
                    wait(pe, dv_l, f.n, "n1")
                    wait_freed(pe, g, (ac_s, s.n - 1, "m1"), (ac_f, f.n - 1, "xT"))
                    for j in range(J):
                        last = tr(M[1][:, j * P:(j + 1) * P], xn[f.par][:, j, :], identf)
                    last.then_inc(*pe_f.done("xT"))
                if A_:
                    wait_dma(pe, d_k, a, 12)
                    wait(pe, dv_s, a.n, "e1")
                    wait(pe, po_s, a.n, "e3")
                    s2(0)
                if T_:
                    wait_dma(pe, d_c, t)
                    wait_freed(pe, g, (dv_t, t.n - 1, "y1"), (ac_f, f.n - 1, "V1"))
                    for j in range(J):
                        last = tr(M[2][:, j * P:(j + 1) * P], cin[t.par][:, j, :], identf)
                    last.then_inc(*pe_t.done("cT"))
                if A_:
                    s2(1)
                if F_:
                    wait(pe, ac_f, f.n, "xT")
                    wait_freed(pe, g, (dv_t, t.n, "x1"), (dv_f, f.n - 1, "q2"))
                    mm(M[0][:, 0:TG], WQ, xT[:, :], start=True, stop=True)
                    mm(M[0][:, TG:2 * TG], WQR, xT[:, :], start=True, stop=True
                       ).then_inc(*pe_f.done("QQ"))
                if A_:
                    pv(0)
                if T_:
                    wait(pe, dv_t, t.n, "n1")
                    wait_freed(pe, g, (ac_f, f.n, "xT"), (ac_s, s.n - 1, "m1"), (dv_r, r.n - 1, "tot"))
                    for j in range(J):
                        last = tr(M[1][:, j * P:(j + 1) * P], xn1[:, j, :], identf)
                    last.then_inc(*pe_t.done("xT"))
                if A_:
                    s2(2)
                if F_:
                    wait_freed(pe, g, (ac_t, t.n, "cT"), (ac_f, f.n - 1, "V1"))
                    mm(M[2][:, 0:TG], WK, xT[:, :], start=True, stop=True)
                    mm(M[2][:, TG:2 * TG], WKR, xT[:, :], start=True, stop=True
                       ).then_inc(*pe_f.done("KK"))
                if A_:
                    pv(1)
                    s2(3)
                if T_:
                    wait(pe, ac_t, t.n, "cT")
                    wait_freed(pe, g, (dv_f, f.n, "q2"), (dv_t, t.n, "x1"))
                    for j in range(J):
                        last = mm(M[0][:, j * 256:(j + 1) * 256], cxT[:, j * P:(j + 1) * P],
                                  wc[:, 1:3, :], start=True, stop=True)
                    last.then_inc(*pe_t.done("KV"))
                    wait(pe, ac_t, t.n, "xT")
                    mm(M[1][:, 0:TG], wc[:, 0, :], xT1[:, :], start=True, stop=True
                       ).then_inc(*pe_t.done("Q2"))
                if A_:
                    pv(2)
                if S_:
                    wait(pe, dv_f, s.n, "x3")
                    s1(0)
                if R_:
                    wait(pe, dv_r, r.n, "p1")
                    wait_freed(pe, g, (dv_f, f.n, "k2"), (ac_t, t.n, "cT"), (dv_t, t.n - 1, "y1"))
                    for j in range(J):
                        last = tr(M[2][:, j * P:(j + 1) * P], xp[:, j, :], identf)
                    last.then_inc(*pe_r.done("xT"))
                if A_:
                    pv(3)
                if S_:
                    s1(1)
                if T_:
                    wait(pe, dv_t, t.n, "v")
                    for j in range(J):
                        last = mm(M[0][:, j * 256:(j + 1) * 256], v2[:, j, :], k2[:, j, :, :],
                                  start=True, stop=True)
                    last.then_inc(*pe_t.done("gram"))
                if R_:
                    wait(pe, ac_r, r.n, "xT")
                    wait_freed(pe, g, (ac_t, t.n, "Q2"), (ac_f, f.n, "xT"), (ac_s, s.n - 1, "m1"))
                    for j in range(J):
                        last = mm(M[1][:, j * E:(j + 1) * E], xpT[:, j * P:(j + 1) * P], cT[:, :],
                                  start=True, stop=True)
                    last.then_inc(*pe_r.done("aff"))
                if S_:
                    s1(2)
                if F_:
                    wait_freed(pe, g, (ac_r, r.n, "xT"), (dv_f, f.n, "k2"))
                    for j in range(J):
                        last = mm(M[2][:, j * D:(j + 1) * D], xT[:, j * P:(j + 1) * P], WV,
                                  start=True, stop=True)
                    last.then_inc(*pe_f.done("V"))
                if T_:
                    wait(pe, dv_t, t.n, "mt")
                    for j in range(J):
                        for b in range(2):
                            last = mm(M[0][:, (2 * j + b) * D:(2 * j + b + 1) * D], mt2[:, j, b, :],
                                      wc[:, 3, :], start=True, stop=True)
                    last.then_inc(*pe_t.done("R"))
                if S_:
                    s1(3)
                if R_:
                    wait(pe, dv_r, r.n, "o1")
                    mm(M[1][:, 0:J * E], tri_b[:, :], ohb[:, :, :], start=True, stop=True)
                    mm(M[1][:, 16:16 + J * E], ones_b[:, :], ohb[:, :, :], start=True, stop=True
                       ).then_inc(*pe_r.done("rank"))
                if T_:
                    wait(pe, ac_t, t.n, "R")
                    wait(pe, ac_t, t.n, "Q2")
                    wait_freed(pe, g, (ac_f, f.n, "V1"), (ac_r, r.n, "xT"))
                    for j in range(J):
                        last = mm(M[2][:, j * 256:(j + 1) * 256], q2[:, j * P:(j + 1) * P],
                                  r2s[:, j, :, :], start=True, stop=True)
                    last.then_inc(*pe_t.done("o2"))
                if S_:
                    wait(pe, dv_s, s.n, "lo")
                    wait_freed(pe, g, (dv_r, r.n, "tot"), (ac_t, t.n, "Q2"), (ac_f, f.n, "xT"))
                    for half_ in range(2):
                        if half_:
                            wait(pe, ac_s, s.n, "m0")
                        for i in range(2):
                            for j in range(J):
                                q = 2 * half_ + i
                                last = mm(M[1][96:104, (2 * i + j) * P:(2 * i + j + 1) * P],
                                          mt[:, j, q, :, :].rearrange("p t h -> p (t h)"),
                                          ident_b[:, :], start=True, stop=True,
                                          tile_position=(0, 96))
                        last.then_inc(*pe_s.done(f"m{half_}"))

            rounds(nc.tensor, one)

            fx, fy = [M[0], M[1]], [M[2], BO_]

            def expert(b):
                return nc.tensor.value_load(bti[0:1, 0, bass.ds(b.n, 1)], min_val=0, max_val=E - 1)

            def transposed(b):
                wait_b(pe, "dve_xh", b.n)
                wait_b(pe, "act_xT", b.n - 2)
                tr(fx[b.c % 2][:, 0:P], xh[b.c % 2][:, :], identf).then_inc(*ffn["pe_xT"].done("pe_xT"))

            def hidden(b, e):
                u = b.c % 2
                wait_b(pe, "act_xT", b.n)
                wait_b(pe, "dve_h", b.n - 2)
                mm(B1[u][:, :], xhT[u][:, :], w1[:, bass.ds(e, 1), :], start=True, stop=True
                   ).then_inc(*ffn["pe_h"].done("pe_h"))

            def turned(b):
                u = b.c % 2
                wait_b(pe, "dve_h", b.n)
                wait_b(pe, "act_relu", b.n - 2)
                for c in range(FC):
                    last = tr(B2[u][:, c * P:(c + 1) * P], hs[u][:, c * P:(c + 1) * P], identf)
                last.then_inc(*ffn["pe_hT"].done("pe_hT"))

            def second(b, e):
                u = b.c % 2
                wait_b(pe, "act_relu", b.n)
                wait_b(pe, "dve_yb", b.n - 2)
                for c in range(FC):
                    last = mm(fy[u][:, 0:D], hT[u][:, c, :], w2[:, bass.ds(e, 1), c, :],
                              start=c == 0, stop=c == FC - 1)
                last.then_inc(*ffn["pe_y"].done("pe_y"))

            pe.wait_ge(s_tab, 1)
            pe.wait_ge(s_pool, 2)
            transposed(Block(0))
            hidden(Block(0), expert(Block(0)))

            def step(b):
                transposed(b.on(1))
                turned(b)
                hidden(b.on(1), expert(b.on(1)))
                second(b, expert(b))

            step(Block(0))
            step(Block(1))
            with nc.tensor.Fori(1, NBLK // 2 - 1) as it:
                step(Block(0, it, 2))
                step(Block(1, it, 2))
            step(Block(NBLK - 2))
            turned(Block(NBLK - 1))
            second(Block(NBLK - 1), expert(Block(NBLK - 1)))

        @block.scalar
        def _(ac):
            act, cp = nc.scalar.activation, nc.scalar.copy

            def one(g):
                f, s, a, t, r = g, g.back(1), g.back(2), g.back(3), g.back(4)
                F_, S_, A_, T_, R_ = (q.within(NG) for q in (f, s, a, t, r))

                def exp(k):
                    wait(ac, pe_a, a.n, f"s{k}")
                    if k < 2:
                        wait(ac, pe_a, a.n - 1, f"p{k + 2}")
                    else:
                        wait(ac, pe_a, a.n, f"p{k - 2}")
                    act(prob[k % 2][:, :], B2[k % 2][:, :], ACT.Exp).then_inc(*ac_a.done(f"e{k}"))

                if F_:
                    wait(ac, pe_f, f.n, "xT")
                    wait(ac, pe_f, f.n - 1, "V")
                    cp(xT[:, :], M[1][:, 0:TG]).then_inc(*ac_f.done("xT"))
                if A_:
                    exp(0)
                if T_:
                    wait(ac, pe_t, t.n, "cT")
                    wait(ac, pe_t, t.n - 1, "KV")
                    cp(cxT[:, :], M[2][:, 0:TG]).then_inc(*ac_t.done("cT"))
                if A_:
                    exp(1)
                if F_:
                    wait(ac, po_f, f.n, "qf")
                    wait_dma(ac, d_q, f.back(1), 12)
                    cp(qhi[:, :], qf[:, :]).then_inc(*ac_f.done("qhi"))
                if T_:
                    wait(ac, pe_t, t.n, "xT")
                    cp(xT1[:, :], M[1][:, 0:TG]).then_inc(*ac_t.done("xT"))
                if A_:
                    exp(2)
                if F_:
                    wait(ac, po_f, f.n, "kf")
                    wait_dma(ac, d_k, f.back(1), 12)
                    diag = khi[:, :, :].rearrange("p (j b) (c k) -> p j b c k", b=2, c=2)
                    for b in range(2):
                        last = cp(diag[:, :, b, b, :],
                                  kf[:, :].rearrange("p (j b k) -> p j b k", j=J, b=2)[:, :, b, :])
                    last.then_inc(*ac_f.done("khi"))
                if A_:
                    exp(3)
                if T_:
                    wait(ac, pe_t, t.n, "Q2")
                    wait(ac, pe_t, t.n - 1, "o2")
                    act(q2[:, :], M[1][:, 0:TG], ACT.Identity, bias=bc[:, 4:5]).then_inc(*ac_t.done("Q2"))
                if R_:
                    wait(ac, pe_r, r.n, "xT")
                    wait(ac, pe_r, r.n - 1, "aff")
                    cp(xpT[:, :], M[2][:, 0:TG]).then_inc(*ac_r.done("xT"))
                if F_:
                    wait(ac, pe_f, f.n, "V")
                    wait(ac, pe_a, f.n - 2, "p3")
                    for b in range(2):
                        cp(vau[f.par][64 * b:64 * b + 64, :, :, 16 * b:16 * b + HD],
                           M[2][64 * b:64 * b + 64, 0:TG].rearrange("p (j h d) -> p j h d", j=J, h=H)
                           ).then_inc(*ac_f.done(f"V{b}"))
                if R_:
                    wait(ac, dv_r, r.n, "g1")
                    wait(ac, dv_r, r.n - 1, "al1")
                    act(ea[:, :], mx8[:, :, 0], ACT.Exp, scale=-1.0).then_inc(*ac_r.done("ea"))
                if T_:
                    wait(ac, pe_t, t.n, "R")
                    wait(ac, pe_t, t.n - 1, "o2")
                    cp(r2s[:, :, :, :].rearrange("p j b d -> p (j b d)"), M[0][:, :]
                       ).then_inc(*ac_t.done("R"))
                if S_:
                    wait_dma(ac, d_q, s, 12)
                    for i in range(2):
                        wait(ac, pe_s, s.n, f"m{i}")
                        cp(qst[s.par][96:104, 2 * i:2 * i + 2, :].rearrange("p r t -> p (r t)"),
                           M[1][96:104, :]).then_inc(*ac_s.done(f"m{i}"))

            ac.wait_ge(d_const, 16 * N_CONST)
            ac.wait_ge(s_vec, 1)
            ac.wait_ge(s_pool, 1)
            rounds(nc.scalar, one)

            ac.wait_ge(s_tab, 1)

            def turned(b):
                u = b.c % 2
                wait_b(ac, "pe_xT", b.n)
                wait_b(ac, "pe_h", b.n - 2)
                cp(xhT[u][:, :], M[u][:, 0:P]).then_inc(*ffn["act_xT"].done("act_xT"))

            def relu(b):
                u = b.c % 2
                e = nc.scalar.value_load(bti[0:1, 0, bass.ds(b.n, 1)], min_val=0, max_val=E - 1)
                wait_b(ac, "pe_hT", b.n)
                wait_b(ac, "pe_y", b.n - 2)
                for c in range(FC):
                    last = act(hT[u][:, c, :], B2[u][:, c * P:(c + 1) * P], ACT.Relu,
                               bias=b1[:, bass.ds(e, 1), c])
                last.then_inc(*ffn["act_relu"].done("act_relu"))

            turned(Block(0))
            turned(Block(1))
            relu(Block(0))
            turned(Block(2))
            relu(Block(1))
            with nc.scalar.Fori(1, NBLK // 2 - 1) as it:
                turned(Block(1, it, 2))
                relu(Block(0, it, 2))
                turned(Block(2, it, 2))
                relu(Block(1, it, 2))
            turned(Block(NBLK - 1))
            relu(Block(NBLK - 2))
            relu(Block(NBLK - 1))

        @block.vector
        def _(dv):
            v = nc.vector

            def bias_norm(eng_steps, n, src, key, b, a):
                for j in range(J):
                    v.bn_stats(stat[key][:, j, :], src(j)).then_inc(*eng_steps.done(f"{b}{j}"))
                wait(dv, eng_steps, n, f"{b}1", alone=True)
                for j in range(J):
                    v.bn_aggr(mv[key][:, j, :], stat[key][:, j, :]).then_inc(*eng_steps.done(f"{a}{j}"))

            def normalise(eng_steps, dst, src, key, nm):
                for j in range(J):
                    v.tensor_scalar(dst(j), src(j), mv[key][:, j, 0:1], rs[key][:, j:j + 1],
                                    ALU.subtract, ALU.mult).then_inc(*eng_steps.done(f"{nm}{j}"))

            def norm_x(g):
                if not g.within(NG):
                    return
                wait_dma(dv, d_x, g)
                wait(dv, po_l, g.n - 1, "eps")
                wait(dv, dv_l, g.n - 1, "n1")
                bias_norm(dv_l, g.n, lambda j: xin[g.par][:, j, :], "L", "b", "a")
                wait(dv, po_l, g.n, "pow")
                wait(dv, pe_f, g.n - 2, "xT")
                normalise(dv_l, lambda j: xn[g.par][:, j, :], lambda j: xin[g.par][:, j, :], "L", "n")

            def one(g):
                f, s, a, t, r = g, g.back(1), g.back(2), g.back(3), g.back(4)
                F_, S_, A_, T_, R_ = (q.within(NG) for q in (f, s, a, t, r))

                def row_max(k):
                    j, c = k // 2, k % 2
                    wait(dv, pe_s, s.n, f"s{k}")
                    wait(dv, dv_s, s.n - 1, "lo")
                    v.tensor_reduce(mx[:, j, 8 * c:8 * c + 8],
                                    B1[c][:, :].rearrange("p (h k) -> p h k", k=SQ), AX.X, ALU.max
                                    ).then_inc(*dv_s.done(f"m{k}"))

                if T_:
                    wait(dv, pe_t, t.n, "out")
                    wait(dv, po_t, t.n, "xb")
                    wait(dv, po_t, t.n - 1, "x1b")
                    wait(dv, dv_t, t.n - 1, "x2")
                    v.tensor_tensor(x1[:, :, :].rearrange("p j d -> p (j d)"), M[0][:, 0:TG],
                                    xr[t.par][:, :, :].rearrange("p j d -> p (j d)"), ALU.add
                                    ).then_inc(*dv_t.done("x1"))
                    wait(dv, dv_t, t.n, "x1")
                    bias_norm(dv_t, t.n, lambda j: x1[:, j, :], "T", "b", "a")
                if R_:
                    px = pay[r.par]
                    wait(dv, dv_t, r.n, "x2")
                    bias_norm(dv_r, r.n, lambda j: px[:, j, 0:D], "R", "b", "a")
                if T_:
                    wait(dv, po_t, t.n, "pow")
                    wait(dv, po_t, t.n - 1, "xnb")
                    wait(dv, dv_t, t.n - 1, "y1")
                    normalise(dv_t, lambda j: xn1[:, j, :], lambda j: x1[:, j, :], "T", "n")
                if R_:
                    wait(dv, po_r, r.n, "pow")
                    v.scalar_tensor_tensor(rc[:, :], mv["R"][:, :, 0], -1.0, rs["R"][:, :],
                                           ALU.mult, ALU.mult).then_inc(*dv_r.done("c"))
                    wait(dv, dv_r, r.n, "c")
                    for j in range(J):
                        v.tensor_scalar(xp[:, j, :], px[:, j, 0:D], rs["R"][:, j:j + 1], rc[:, j:j + 1],
                                        ALU.mult, ALU.add).then_inc(*dv_r.done(f"p{j}"))
                if F_:
                    wait(dv, pe_f, f.n, "QQ")
                    wait(dv, po_f, f.n - 1, "qf")
                    for i, buf in enumerate((t1, t2)):
                        v.scalar_tensor_tensor(
                            buf[0][:, :].rearrange("p (s t) -> p s t", t=SQ),
                            M[0][:, i * TG:(i + 1) * TG].rearrange("p (s t) -> p s t", t=SQ), bc[:, i:i + 1],
                            rope[i].unsqueeze(1).broadcast_to((P, 2 * J, SQ)), ALU.add, ALU.mult
                        ).then_inc(*dv_f.done(f"q{i + 1}"))
                if R_:
                    wait(dv, dv_r, r.n, "p1")
                    bias_norm(dv_r, r.n, lambda j: xp[:, j, :], "Q", "d", "e")
                if F_:
                    wait(dv, po_f, f.n, "qf")
                    wait(dv, pe_s, f.n - 2, "s3")
                    qd = qz[f.par][:, :, :, :].rearrange("p r (j b) (c q) -> p r j b c q", b=2, c=2)
                    qs_ = qf[:, :].rearrange("p (j b q) -> p j b q", j=J, b=2)
                    for r_ in range(4):
                        rows_ = slice(32 * r_, 32 * r_ + 32)
                        for b in range(2):
                            last = v.tensor_copy(qd[rows_, r_, :, b, b, :], qs_[rows_, :, b, :])
                        last.then_inc(*dv_f.done(f"z{r_}"))
                if F_:
                    wait(dv, pe_f, f.n, "KK")
                    wait(dv, po_f, f.n - 1, "kf")
                    for i, buf in enumerate((t1, t2)):
                        v.scalar_tensor_tensor(
                            buf[1][:, :].rearrange("p (s t) -> p s t", t=SQ),
                            M[2][:, i * TG:(i + 1) * TG].rearrange("p (s t) -> p s t", t=SQ), bc[:, 2 + i:3 + i],
                            rope[2 + i].unsqueeze(1).broadcast_to((P, 2 * J, SQ)), ALU.add, ALU.mult
                        ).then_inc(*dv_f.done(f"k{i + 1}"))
                if R_:
                    wait(dv, po_r, r.n, "pow2")
                    v.tensor_tensor(rm[:, :], rc[:, :], mv["Q"][:, :, 0], ALU.subtract
                                    ).then_inc(*dv_r.done("cm"))
                    v.tensor_tensor(px[:, :, C_A], rs["R"][:, :], rs["Q"][:, :], ALU.mult
                                    ).then_inc(*dv_r.done("A"))
                    wait(dv, dv_r, r.n, "cm")
                    v.tensor_tensor(px[:, :, C_B], rm[:, :], rs["Q"][:, :], ALU.mult
                                    ).then_inc(*dv_r.done("B"))
                    v.tensor_scalar(px[:, :, C_R], rs["R"][:, :], 1.0, None, ALU.add
                                    ).then_inc(*dv_r.done("R"))
                    v.tensor_tensor(px[:, :, C_C], rc[:, :], pen[:, bass.ds(r.n * J, J)], ALU.add
                                    ).then_inc(*dv_r.done("C"))
                    wait(dv, dv_r, r.n - 1, "tok")
                    v.tensor_copy(px[:, :, C_ID], tokid[:, :]).then_inc(*dv_r.done("id"))
                if T_:
                    wait(dv, pe_t, t.n, "KV")
                    wait(dv, pe_t, t.n - 1, "gram")
                    kv = M[0][:, :].rearrange("p (j a d) -> p j a d", j=J, a=2)
                    for b in range(2):
                        rows_ = slice(64 * b, 64 * b + 64)
                        v.tensor_tensor(k2[rows_, :, b, :], kv[rows_, :, 0, :],
                                        BK2[rows_].unsqueeze(1).broadcast_to((64, J, D)), ALU.add
                                        ).then_inc(*dv_t.done(f"k{b}"))
                    v.tensor_tensor(v2[:, :, :], kv[:, :, 1, :], BV2.unsqueeze(1).broadcast_to((P, J, D)),
                                    ALU.add).then_inc(*dv_t.done("v"))
                if F_:
                    wait(dv, po_f, f.n, "kf")
                    wait(dv, pe_s, f.n - 2, "s3")
                    for i in range(4):
                        v.tensor_scalar(kex[f.par][:, i, :], kf[:, :], own4[:, i:i + 1], None, ALU.mult
                                        ).then_inc(*dv_f.done(f"x{i}"))
                if S_:
                    row_max(0)
                if A_:
                    wait(dv, pe_a, a.n, "p3")
                    wait(dv, dv_a, a.n - 1, "n3")
                    v.transpose(ot[:, :, :, :, :, :].rearrange("p j g q b t -> p (j g q b t)"),
                                BO_[:, :]).then_inc(*dv_a.done("ot"))
                    wait(dv, dv_a, a.n, "ot")
                    v.reciprocal(rd[:, :, :, :, :], ot[:, :, :, :, :, HD]).then_inc(*dv_a.done("rd"))
                    wait(dv, dv_a, a.n, "rd")
                    wait(dv, dv_a, a.n - 1, "tr")
                    for j in range(J):
                        for b in range(2):
                            v.tensor_tensor(
                                on[:, j, b, :, :, :], ot[:, j, :, :, b, 0:HD].rearrange("p g q d -> p q g d"),
                                rd[:, j, :, :, b].rearrange("p g q -> p q g").unsqueeze(3)
                                .broadcast_to((P, 2, 4, HD)), ALU.mult).then_inc(*dv_a.done(f"n{2 * j + b}"))
                    wait(dv, dv_a, a.n, "n3")
                    wait(dv, pe_t, a.n - 2, "out")
                    v.transpose(ont[a.par][:, :, :, :, :].rearrange("p j b q t -> p (j b q t)"),
                                on[:, :, :, :, :, :].rearrange("p j b q g d -> p (j b q g d)")
                                ).then_inc(*dv_a.done("tr"))
                if S_:
                    row_max(1)
                if T_:
                    wait(dv, pe_t, t.n, "gram")
                    wait(dv, pe_t, t.n - 1, "R")
                    v.tensor_tensor(mt2[:, :, :, :].rearrange("p j b d -> p (j b) d"),
                                    M[0][:, :].rearrange("p (a d) -> p a d", d=D),
                                    headmask.unsqueeze(1).broadcast_to((P, 2 * J, D)), ALU.mult
                                    ).then_inc(*dv_t.done("mt"))
                if R_:
                    wait(dv, pe_r, r.n, "aff")
                    v.tensor_copy(aff[:, :, :].rearrange("p j e -> p (j e)"), M[1][:, 0:J * E]
                                  ).then_inc(*dv_r.done("aff"))
                    wait(dv, dv_r, r.n, "aff")
                    wait(dv, ac_r, r.n - 1, "ea", alone=True)
                    for j in range(J):
                        v.max(mx8[:, j, :], aff[:, j, :]).then_inc(*dv_r.done(f"g{j}"))
                    wait(dv, dv_r, r.n, "g1", alone=True)
                    for j in range(J):
                        v.max_index(ix8[:, j, :], mx8[:, j, :], aff[:, j, :]).then_inc(*dv_r.done(f"i{j}"))
                    wait(dv, dv_r, r.n, "i1")
                    v.tensor_copy(idf[:, :], ix8[:, :, 0]).then_inc(*dv_r.done("idf"))
                    wait(dv, dv_r, r.n, "idf")
                    v.tensor_scalar(idf[:, :], idf[:, :], float(E - 1), None, ALU.min
                                    ).then_inc(*dv_r.done("idm"))
                    wait(dv, dv_r, r.n, "idm")
                    for j in range(J):
                        v.tensor_scalar(ohb[:, j, :], iota8, idf[:, j:j + 1], None, ALU.is_equal
                                        ).then_inc(*dv_r.done(f"o{j}"))
                if S_:
                    row_max(2)
                if R_:
                    wait(dv, ac_r, r.n, "ea")
                    v.tensor_scalar(ea1[:, :], ea[:, :], 1.0, None, ALU.add).then_inc(*dv_r.done("al1"))
                    wait(dv, dv_r, r.n, "al1")
                    v.reciprocal(px[:, :, C_AL], ea1[:, :]).then_inc(*dv_r.done("al"))
                if S_:
                    row_max(3)
                    wait(dv, dv_s, s.n, "m3")
                    wait(dv, pe_s, s.n - 1, "m1")
                    mxv = mx[:, :, :].rearrange("p j (r h) -> p (j r) h", h=4)
                    mtv = mt[:, :, :, :, :].rearrange("p j r t h -> p (j r) t h")
                    v.tensor_scalar(mtv[:, :, 0, :], mxv, -1.0, None, ALU.mult).then_inc(*dv_s.done("hi"))
                    wait(dv, dv_s, s.n, "hi")
                    v.scalar_tensor_tensor(mtv[:, :, 1, :], mxv, -1.0, mtv[:, :, 0, :],
                                           ALU.mult, ALU.subtract).then_inc(*dv_s.done("lo"))
                if R_:
                    wait(dv, pe_r, r.n, "rank")
                    v.tensor_tensor(cnt[:, 1, :], cnt[:, 0, :], M[1][:, 16:16 + E], ALU.add
                                    ).then_inc(*dv_r.done("c1"))
                    wait(dv, dv_r, r.n, "c1")
                    v.tensor_tensor(rk[:, :, :], M[1][:, 0:J * E].rearrange("p (j e) -> p j e", j=J),
                                    cnt[:, :, :], ALU.add).then_inc(*dv_r.done("rk"))
                    wait(dv, dv_r, r.n, "rk")
                    v.tensor_tensor(rk[:, :, :], rk[:, :, :], ohb[:, :, :], ALU.mult
                                    ).then_inc(*dv_r.done("pr"))
                    wait(dv, dv_r, r.n, "pr")
                    v.tensor_reduce(slf[:, :], rk[:, :, :], AX.X, ALU.add).then_inc(*dv_r.done("sl"))
                    wait(dv, dv_r, r.n, "sl")
                    v.scalar_tensor_tensor(slf[:, :], idf[:, :], float(CAP), slf[:, :], ALU.mult, ALU.add
                                           ).then_inc(*dv_r.done("s2"))
                    wait(dv, dv_r, r.n, "s2")
                    wait_dma(dv, d_s, r.back(2), J)
                    v.tensor_copy(sli[r.par][:, :], slf[:, :]).then_inc(*dv_r.done("si"))
                    v.tensor_tensor(cnt[:, 0, :], cnt[:, 1, :], M[1][:, 16 + E:16 + 2 * E], ALU.add
                                    ).then_inc(*dv_r.done("tot"))
                    wait(dv, dv_r, r.n, "tot")
                    v.tensor_copy(cnt[:, 1, :], cnt[:, 0, :]).then_inc(*dv_r.done("nx"))
                    v.tensor_scalar(tokid[:, :], tokid[:, :], float(TG), None, ALU.add
                                    ).then_inc(*dv_r.done("tok"))
                if T_:
                    wait(dv, pe_t, t.n, "o2")
                    wait(dv, po_t, t.n, "xnb")
                    wait(dv, dv_t, t.n - 1, "z1")
                    o2v = M[2][:, :].rearrange("p (j b d) -> p j b d", j=J, b=2)
                    for b in range(2):
                        rows_ = slice(64 * b, 64 * b + 64)
                        v.tensor_tensor(y1[rows_, :, :], o2v[rows_, :, b, :], xn1[rows_, :, :], ALU.add
                                        ).then_inc(*dv_t.done(f"y{b}"))
                    wait(dv, dv_t, t.n, "y1")
                    bias_norm(dv_t, t.n, lambda j: y1[:, j, :], "U", "c", "d")
                norm_x(g.back(-1))
                if T_:
                    wait(dv, po_t, t.n, "pow2")
                    wait(dv, po_t, t.n - 1, "zg")
                    normalise(dv_t, lambda j: yn[:, j, :], lambda j: y1[:, j, :], "U", "z")
                if S_:
                    wait(dv, ac_s, s.n, "m1")
                    wait(dv, pe_a, a.n, "s3")
                    for i in range(2):
                        v.tensor_scalar(qex[:, :, i, :], qst[s.par][:, :, :].bitcast(FP32),
                                        own4s[:, i:i + 1], None, ALU.mult).then_inc(*dv_s.done(f"e{i}"))
                if T_:
                    wait(dv, po_t, t.n, "zg")
                    wait_dma(dv, d_s, t.back(2), J)
                    v.tensor_tensor(pay[t.par][:, :, 0:D], yn[:, :, :], x1[:, :, :], ALU.add
                                    ).then_inc(*dv_t.done("x2"))

            for i in range(2):
                v.memset(qst[i][:, :, :].bitcast(FP32), 0.0)
                v.memset(qz[i][:, :, :, :].bitcast(FP32), 0.0)
                v.memset(vau[i][:, :, :, :], 0.0)
                v.memset(pay[i][:, :, :], 0.0)
            v.memset(khi[:, :, :].bitcast(FP32), 0.0)
            v.memset(klo[:, :, :].bitcast(FP32), 0.0)
            v.memset(cnt[:, :, :], 0.0)
            v.memset(ones_b[:, :], 1.0).then_inc(s_zero, 1)
            dv.wait_ge(s_zero, 1)
            dv.wait_ge(d_const, 16 * N_CONST)
            for i in range(2):
                for b in range(2):
                    v.memset(vau[i][64 * b:64 * b + 64, :, :, 16 * b + HD:16 * b + HD + 1], 1.0)
            v.tensor_copy(tokid[:, :], tok0)
            v.tensor_copy(negq_b[:, :], nqf[:, :])
            v.tensor_copy(negk_b[:, :], nkf[:, :])
            v.tensor_copy(ident_b[:, :], identf)
            v.tensor_copy(tri_b[:, :], trif).then_inc(s_vec, 1)
            v.tensor_copy(bvx[:, :], bc[:, 5:6].broadcast_to((P, P))).then_inc(s_vec, 1)
            dv.wait_ge(s_pe, 1)
            v.tensor_tensor(BO, M[0][:, 0:D], BO, ALU.add).then_inc(s_vec, 1)
            dv.wait_ge(s_vec, 3)
            v.tensor_reduce(pen[:, :], mk[:, :, :], AX.X, ALU.max).then_inc(s_mask, 1)
            dv.wait_ge(s_mask, 1)
            v.tensor_scalar(pen[:, :], pen[:, :], -3.0e38, 1.0e38, ALU.mult, ALU.mult).then_inc(s_mask, 1)
            dv.wait_ge(s_mask, 2)
            v.tensor_scalar(pen[:, :], pen[:, :], 0.0, None, ALU.mult).then_inc(s_mask, 1)
            dv.wait_ge(s_pe, 2)
            v.tensor_tensor(b1[:, :, :].rearrange("p e c -> p (e c)"), M[1][:, 0:E * FC],
                            b1[:, :, :].rearrange("p e c -> p (e c)"), ALU.add).then_inc(s_vec, 1)
            dv.wait_ge(s_vec, 4)
            dv.wait_ge(s_mask, 3)
            dv.wait_ge(s_pool, 1)

            norm_x(Group(0))
            rounds(nc.vector, one)

            cs = [0]

            def link(ins):
                cs[0] += 1
                ins.then_inc(s_chain, 1)
                dv.wait_ge(s_chain, cs[0])

            dv.wait_ge(dv_r.sem, dv_r.at(NG - 1, "nx"))
            link(v.tensor_scalar(nbf[:, :], cnt[:, 0, :], float(P - 1), None, ALU.add))
            link(v.tensor_copy(ti[:, :], nbf[:, :]))
            link(v.tensor_scalar(ti[:, :], ti[:, :], 7, None, ALU.logical_shift_right))
            link(v.tensor_copy(nbf[:, :], ti[:, :]))
            link(v.tensor_copy(cum[:, :], nbf[:, :]))
            for e in range(1, E):
                link(v.tensor_tensor(cum[:, e:e + 1], cum[:, e - 1:e], cum[:, e:e + 1], ALU.add))
            link(v.tensor_tensor(geb[:, :, :], blkno.unsqueeze(2).broadcast_to((P, NBLK, E)),
                                 cum[:, :].unsqueeze(1).broadcast_to((P, NBLK, E)), ALU.is_ge))
            link(v.tensor_tensor(gnb[:, :, :], geb[:, :, :],
                                 nbf[:, :].unsqueeze(1).broadcast_to((P, NBLK, E)), ALU.mult))
            link(v.tensor_reduce(bex[:, :], geb[:, :, :], AX.X, ALU.add))
            link(v.tensor_reduce(bst[:, :], gnb[:, :, :], AX.X, ALU.add))
            link(v.tensor_tensor(bst[:, :], blkno, bst[:, :], ALU.subtract))
            link(v.tensor_scalar(bst[:, :], bst[:, :], float(P), None, ALU.mult))
            link(v.scalar_tensor_tensor(bst[:, :], bex[:, :], float(CAP), bst[:, :], ALU.mult, ALU.add))
            link(v.tensor_scalar(btf[:, 1, :], bst[:, :], float(E * CAP), None, ALU.min))
            link(v.tensor_scalar(btf[:, 0, :], bex[:, :], float(E - 1), None, ALU.min))
            link(v.tensor_copy(bti[:, :, :], btf[:, :, :]))
            link(v.scalar_tensor_tensor(prf[:, :], iota8, float(CAP), cnt[:, 0, :], ALU.mult, ALU.add))
            v.tensor_copy(pri[:, :], prf[:, :]).then_inc(s_tab, 1)

            def rows_in(b):
                q = b.c % 4
                wait_rows(dv, b)
                wait_b(dv, "pe_xT", b.n - 2)
                v.tensor_scalar(xh[b.c % 2][:, :], rb[q][:, 0:D], rb[q][:, C_A:C_A + 1],
                                rb[q][:, C_B:C_B + 1], ALU.mult, ALU.add
                                ).then_inc(*ffn["dve_xh"].done("dve_xh"))

            def hidden(b):
                u = b.c % 2
                wait_b(dv, "pe_h", b.n)
                wait_b(dv, "pe_hT", b.n - 2)
                v.tensor_copy(hs[u][:, :], B1[u][:, :]).then_inc(*ffn["dve_h"].done("dve_h"))

            def finish(b, e):
                u, q = b.c % 2, b.c % 4
                wait_b(dv, "pe_y", b.n)
                v.tensor_tensor(yb[u][:, :], [M[2], BO_][u][:, 0:D], b2[:, bass.ds(e, 1), :], ALU.add
                                ).then_inc(*ffn["dve_yb"].done("dve_yb"))
                wait_b(dv, "dve_yb", b.n)
                wait_b(dv, "pool_base", b.n)
                wait_out(dv, b)
                v.scalar_tensor_tensor(yo[u][:, :], yb[u][:, :], rb[q][:, C_AL:C_AL + 1], bs[q][:, :],
                                       ALU.mult, ALU.add).then_inc(*ffn["dve_yo"].done("dve_yo"))

            def step(b):
                if b.it is not None or b.c + 2 < NBLK:
                    rows_in(b.on(2))
                e = nc.vector.value_load(bti[0:1, 0, bass.ds(b.n, 1)], min_val=0, max_val=E - 1)
                if b.it is not None or b.c + 1 < NBLK:
                    hidden(b.on(1))
                finish(b, e)

            rows_in(Block(0))
            rows_in(Block(1))
            hidden(Block(0))
            for c in range(4):
                step(Block(c))
            with nc.vector.Fori(1, NBLK // 4 - 1) as it:
                for u in range(4):
                    step(Block(u, it, 4))
            for c in range(NBLK - 4, NBLK):
                step(Block(c))

        @block.gpsimd
        def _(po):
            v = nc.gpsimd

            def inv_std(steps, n, key, waits, tail=""):
                waits()
                v.tensor_scalar(ve[key][:, :], mv[key][:, :, 1], EPS, None, ALU.add
                                ).then_inc(*steps.done("eps" + tail))
                wait(po, steps, n, "eps" + tail)
                v.tensor_tensor(rs[key][:, :], ve[key][:, :], half[:, :], ALU.pow
                                ).then_inc(*steps.done("pow" + tail))

            def norm_x(g):
                if not g.within(NG):
                    return

                def waits():
                    wait(po, dv_l, g.n, "a1")
                    wait(po, dv_l, g.n - 1, "n1")
                inv_std(po_l, g.n, "L", waits)

            def one(g):
                f, s, a, t, r = g, g.back(1), g.back(2), g.back(3), g.back(4)
                F_, S_, A_, T_, R_ = (q.within(NG) for q in (f, s, a, t, r))
                if T_:
                    wait_dma(po, d_xr, t)
                    v.tensor_tensor(xr[t.par][:, :, :], xr[t.par][:, :, :],
                                    BO.unsqueeze(1).broadcast_to((P, J, D)), ALU.add
                                    ).then_inc(*po_t.done("xb"))
                    inv_std(po_t, t.n, "T", lambda: wait(po, dv_t, t.n, "a1"))
                if R_:
                    inv_std(po_r, r.n, "R", lambda: (wait(po, dv_r, r.n, "a1"), wait(po, dv_r, r.n - 1, "R")))
                if F_:
                    wait(po, dv_f, f.n, "q2")
                    wait(po, dv_f, f.n - 1, "z3")
                    wait(po, ac_f, f.n - 1, "qhi")
                    v.tensor_tensor(qf[:, :], t1[0][:, :], t2[0][:, :], ALU.add).then_inc(*po_f.done("qf"))
                    wait(po, ac_f, f.n, "qhi")
                    wait_dma(po, d_q, f.back(1), 12)
                    v.tensor_tensor(qlo[:, :], qf[:, :], qhi[:, :].bitcast(FP32), ALU.subtract
                                    ).then_inc(*po_f.done("qlo"))
                    wait(po, dv_f, f.n, "k2")
                    wait(po, dv_f, f.n - 1, "x3")
                    wait(po, ac_f, f.n - 1, "khi")
                    v.tensor_tensor(kf[:, :], t1[1][:, :], t2[1][:, :], ALU.add).then_inc(*po_f.done("kf"))
                    wait(po, ac_f, f.n, "khi")
                    wait_dma(po, d_k, f.back(1), 12)
                    kl = klo[:, :, :].rearrange("p (j b) (c k) -> p j b c k", b=2, c=2)
                    kh = khi[:, :, :].bitcast(FP32).rearrange("p (j b) (c k) -> p j b c k", b=2, c=2)
                    kv = kf[:, :].rearrange("p (j b k) -> p j b k", j=J, b=2)
                    for b in range(2):
                        last = v.tensor_tensor(kl[:, :, b, b, :], kv[:, :, b, :], kh[:, :, b, b, :], ALU.subtract)
                    last.then_inc(*po_f.done("klo"))
                if R_:
                    inv_std(po_r, r.n, "Q", lambda: (wait(po, dv_r, r.n, "e1"), wait(po, dv_r, r.n - 1, "B")), "2")
                if T_:
                    wait(po, pe_t, t.n, "xT")
                    wait(po, dv_t, t.n, "n1")
                    v.tensor_tensor(xn1[:, :, :], xn1[:, :, :], BO2.unsqueeze(1).broadcast_to((P, J, D)),
                                    ALU.add).then_inc(*po_t.done("xnb"))
                    v.tensor_tensor(x1[:, :, :], x1[:, :, :], LNB.unsqueeze(1).broadcast_to((P, J, D)),
                                    ALU.add).then_inc(*po_t.done("x1b"))
                if R_:
                    wait(po, dv_r, r.n, "si")
                    wait(po, dv_r, r.n, "al")
                    wait(po, dv_r, r.n, "id")
                    for j in range(J):
                        v.indirect_dma_start(
                            out=rows, out_offset=bass.IndirectOffsetOnAxis(ap=sli[r.par][:, j:j + 1], axis=0),
                            in_=pay[r.par][:, j, :], in_offset=None).then_inc(d_s[r.par], 16)
                if T_:
                    inv_std(po_t, t.n, "U", lambda: (wait(po, dv_t, t.n, "d1"), wait(po, dv_t, t.n - 1, "z1")), "2")
                norm_x(g.back(-1))
                if T_:
                    wait(po, dv_t, t.n, "z1")
                    v.tensor_tensor(yn[:, :, :], yn[:, :, :], LNG.unsqueeze(1).broadcast_to((P, J, D)),
                                    ALU.mult).then_inc(*po_t.done("zg"))
                if S_:
                    wait(po, ac_s, s.n, "m1")
                    wait(po, pe_a, a.n, "s3")
                    for i in range(2, 4):
                        v.tensor_scalar(qex[:, :, i, :], qst[s.par][:, :, :].bitcast(FP32),
                                        own4s[:, i:i + 1], None, ALU.mult).then_inc(*po_s.done(f"e{i}"))

            v.memset(half[:, :], -0.5)
            for i in range(2):
                v.memset(kst[i][:, :, :, :].bitcast(FP32), 0.0)
            v.memset(k2[:, :, :, :], 0.0).then_inc(s_pz, 1)
            po.wait_ge(s_pz, 1)
            for i in range(2):
                kd = kst[i][96:104, :, :, :].bitcast(FP32).rearrange("p r (j b) (c k) -> p r j b c k", b=2, c=2)
                for r_ in range(4):
                    for b in range(2):
                        last = v.memset(kd[:, r_, :, b, b, :], 1.0)
            last.then_inc(s_pool, 1)
            po.wait_ge(s_pool, 1)
            po.wait_ge(d_weights, 32)
            po.wait_ge(d_const, 16 * N_CONST)
            po.wait_ge(s_pe, 2)
            for e in range(E):
                last = v.tensor_scalar(w1[:, e, :], w1[:, e, :], gb[:, 0, e:e + 1], None, ALU.mult)
            last.then_inc(s_pool, 1)
            po.wait_ge(s_vec, 4)

            norm_x(Group(0))
            rounds(nc.gpsimd, one)

            def step(b):
                u, q = b.c % 2, b.c % 4
                wait_rows(po, b)
                wait_b(po, "dve_yo", b.n - 4)
                v.tensor_scalar(bs[q][:, :], rb[q][:, 0:D], rb[q][:, C_R:C_R + 1], rb[q][:, C_C:C_C + 1],
                                ALU.mult, ALU.add).then_inc(*ffn["pool_base"].done("pool_base"))
                wait_out(po, b)
                v.tensor_copy(idi[u][:, :], rb[q][:, C_ID:C_ID + 1]).then_inc(*ffn["pool_id"].done("pool_id"))

            def scatter(b):
                u = b.c % 2
                wait_b(po, "pool_id", b.n)
                wait_b(po, "dve_yo", b.n)
                v.indirect_dma_start(
                    out=o_rows, out_offset=bass.IndirectOffsetOnAxis(ap=idi[u][:, 0:1], axis=0),
                    in_=yo[u][:, :], in_offset=None, bounds_check=T - 1, oob_is_err=False
                ).then_inc(d_o[u], 16)

            step(Block(0))
            for c in range(4):
                step(Block(c + 1))
                scatter(Block(c))
            with nc.gpsimd.Fori(1, NBLK // 4 - 1) as it:
                for u in range(4):
                    step(Block(u + 1, it, 4))
                    scatter(Block(u, it, 4))
            for c in range(NBLK - 4, NBLK):
                if c + 1 < NBLK:
                    step(Block(c + 1))
                scatter(Block(c))


def _constants(nb):
    t = nb * SQ
    p = np.arange(P)
    half = HD // 2
    inv = (1.0 / np.float32(10000.0) ** (np.arange(half, dtype=np.float32) / half)).astype(np.float32)
    ang = np.outer(np.arange(SQ, dtype=np.float32), inv).astype(np.float32)
    cos = np.cos(ang).T[p % half]
    sin = np.sin(ang).T[p % half] * np.where(p % HD < half, -1.0, 1.0)[:, None]
    scale = 1.0 / np.sqrt(np.float64(HD))
    dk = float(np.float32(np.sqrt(np.float16(HD))) + np.float32(1e-8))
    own = (p[:, None] // HD == p[None, :] // HD) / dk
    own4 = (p[:, None] % 32) // HD == np.arange(4)
    own4s = np.where(p[:, None] < 96, own4, p[:, None] % 4 == np.arange(4))
    nblk = t // P + E
    rep = lambda a: np.broadcast_to(a, (P, len(a)))
    cols = [cos * scale, sin * scale, cos, sin, own, np.eye(P), own4, own4s, rep(np.arange(E)),
            p[:, None] + P * np.arange(J), p[:, None] < p[None, :], rep(np.arange(nblk))]
    consts = np.concatenate([np.asarray(c, np.float32) for c in cols], axis=1)
    q = p % SQ
    later = np.arange(SQ)[None, :] > q[:, None]
    negq = np.tile(np.where(later, NEG, 0.0), (1, 8)).astype(np.float32)
    earlier = np.arange(SQ)[None, :] < q[:, None]
    negk = np.tile(np.where(earlier, NEG, 0.0), (1, 8)).astype(np.float32)
    pad = np.zeros((P, ROW), np.float32)
    pad[:, C_ID] = t + p
    return consts, negq, negk, pad


def kernel(x, ctx_1024, mask_Bx1xSxS2_bf0, L0_attn_qkv_w, L0_attn_qkv_b, L0_attn_out_w, L0_attn_out_b,
           L0_xattn_wq_w, L0_xattn_wq_b, L0_xattn_wk_w, L0_xattn_wk_b, L0_xattn_wv_w, L0_xattn_wv_b,
           L0_xattn_wo_w, L0_xattn_wo_b, L0_xattn_ln_g, L0_xattn_ln_b, L0_ffn_centroids, L0_ffn_ln_g,
           L0_ffn_ln_b, L0_ffn_w1, L0_ffn_b1, L0_ffn_w2, L0_ffn_b2):
    import concourse.bacc as bacc
    from concourse.bass_utils import run_bass_kernel_spmd

    a = lambda v: np.asarray(v)
    qkv, qb = a(L0_attn_qkv_w), a(L0_attn_qkv_b)
    partner = np.arange(D) ^ (HD // 2)
    wq, wk, wv = qkv[:D], qkv[D:2 * D], qkv[2 * D:]
    bq, bk, bv = qb[:D], qb[D:2 * D], qb[2 * D:]
    wself = np.stack([w.T for w in (wq, wq[partner], wk, wk[partner], wv, a(L0_attn_out_w))], axis=1)
    wcross = np.stack([a(w).T for w in (L0_xattn_wq_w, L0_xattn_wk_w, L0_xattn_wv_w, L0_xattn_wo_w)], axis=1)
    bcol = np.stack([bq, bq[partner], bk, bk[partner], a(L0_xattn_wq_b), bv], axis=1)
    brow = np.concatenate([a(L0_attn_out_b), a(L0_xattn_wo_b), a(L0_xattn_ln_g), a(L0_xattn_ln_b),
                           a(L0_xattn_wk_b), a(L0_xattn_wv_b)])
    consts, negq, negk, pad = _constants(x.shape[0])
    arrays = {
        "x": a(x), "ctx": a(ctx_1024), "mask": a(mask_Bx1xSxS2_bf0).view(np.int32),
        "wself": wself, "wcross": wcross, "bcol": bcol, "brow": brow,
        "cent": a(L0_ffn_centroids).T,
        "w1t": a(L0_ffn_w1).transpose(2, 0, 1),
        "lngb": np.stack([a(L0_ffn_ln_g).T, a(L0_ffn_ln_b).T], axis=1),
        "b1c": a(L0_ffn_b1).reshape(E, FC, P).transpose(2, 0, 1),
        "w2t": a(L0_ffn_w2).reshape(E, D, FC, P).transpose(3, 0, 2, 1),
        "b2r": a(L0_ffn_b2).reshape(-1),
        "consts": consts, "negq": negq, "negk": negk, "padc": pad,
    }
    arrays = {f"in_{n}": np.ascontiguousarray(v) for n, v in arrays.items()}
    nc = bacc.Bacc("TRN2", target_bir_lowering=False, num_devices=1)
    args = [nc.dram_tensor(n, v.shape, mybir.dt.from_np(v.dtype), kind="ExternalInput").ap()
            for n, v in arrays.items()]
    args.append(nc.dram_tensor("out", x.shape, FP32, kind="ExternalOutput").ap())
    decoder_kernel(nc, *args)
    r = run_bass_kernel_spmd(nc, [arrays], core_ids=[0])
    return r.results[0]["out"]
```

```python
from contextlib import ExitStack

import numpy as np

import concourse.bass as bass
from concourse import mybir

FP32 = mybir.dt.float32
F32R = mybir.dt.float32r
BF16 = mybir.dt.bfloat16
I32 = mybir.dt.int32
U32 = mybir.dt.uint32
ALU = mybir.AluOpType
ACT = mybir.ActivationFunctionType
AX = mybir.AxisListType

P = 128
D = 128
H, HD = 16, 8
SQ = 64
J = 2
TG = J * P
E, F = 8, 512
FC = F // P
EPS = 1e-5
NEG = -1.0e30
ROW = 136
C_A, C_B, C_R, C_C, C_AL, C_ID = range(D, D + 6)


class Steps:

    def __init__(self, sem, names, total):
        self.sem, self.names, self.next, self.total = sem, names.split(), 0, total

    def at(self, n, name):
        if isinstance(n, int):
            n = min(n, self.total - 1)
        return n * len(self.names) + (self.names.index(name) + 1)

    def done(self, name):
        assert self.names[self.next] == name, (self.names[self.next], name)
        self.next = (self.next + 1) % len(self.names)
        return self.sem, 1


class Stage:

    def __init__(self, name, pieces, total, sem):
        self.piece = {}
        for p in pieces.split("|"):
            steps = Steps(sem(f"{name}_{p.split()[0]}"), p, total)
            self.piece.update({step: steps for step in p.split()})

    def done(self, name):
        return self.piece[name].done(name)


class Group:

    def __init__(self, c, it=None):
        self.c, self.it = c, it
        self.n = c if it is None else it * 2 + c
        self.half = c // 2 if it is None else it + c // 2
        self.par = c % 2

    def back(self, k):
        return Group(self.c - k, self.it)

    def within(self, total):
        return self.it is not None or 0 <= self.c < total


class Block:

    def __init__(self, c, it=None, step=0):
        self.c, self.it, self.step = c, it, step
        self.n = c if it is None else it * step + c
        self.half = c // 2 if it is None else it * (step // 2) + c // 2
        self.quarter = c // 4 if it is None or step < 4 else it * (step // 4) + c // 4

    def on(self, k):
        return Block(self.c + k, self.it, self.step)


class Waits:
    passed = None


def wait_for(eng, sem, v, alone=False):
    if not isinstance(v, int):
        eng.wait_ge(sem, v)
        if alone or eng.engine in (mybir.EngineType.Pool, mybir.EngineType.SP):
            eng.sem_inc(Waits.passed, 1)
    elif v > 0:
        eng.wait_ge(sem, v)


def wait(eng, steps, n, name, alone=False):
    if isinstance(steps, Stage):
        steps = steps.piece[name]
    wait_for(eng, steps.sem, steps.at(n, name), alone)




def wait_dma(eng, sems, g, count=1):
    wait_for(eng, sems[g.par], (g.half + 1) * (16 * count))


def decoder_kernel(nc, x, ctx, mask, wself, wcross, bcol, brow, cent, w1t, lngb, b1c, w2t, b2r,
                   consts, negq, negk, padc, out):
    NB = x.shape[0]
    T = NB * SQ
    NT = T // P
    NG = NT // J
    CAP = T + P
    NBLK = NT + E
    x_rows = x.rearrange("b s d -> (b s) d")
    c_rows = ctx.rearrange("b s d -> (b s) d")
    o_rows = out.rearrange("b s d -> (b s) d")
    m_rows = mask.rearrange("b o s k -> (b o s) k").rearrange("(t p) k -> p t k", p=P)
    rows = nc.dram_tensor("expert_rows", [E * CAP + P, ROW], FP32, kind="Internal").ap()

    es = ExitStack()
    with es:
        def sb(name, shape, dt=FP32):
            return es.enter_context(nc.sbuf_tensor(name, shape, dt))

        def two(name, shape, dt=FP32):
            return [sb(f"{name}_{i}", shape, dt) for i in range(2)]

        def sem(name):
            return es.enter_context(nc.semaphore(name))

        ws = sb("ws", [P, 6, D])
        WQ, WQR, WK, WKR, WV, WO = (ws[:, i, :] for i in range(6))
        wc = sb("wc", [P, 4, D])
        bc = sb("bc", [P, 6])
        br = sb("br", [P, 6, D])
        BO, BO2, LNG, LNB, BK2, BV2 = (br[:, i, :] for i in range(6))
        cT = sb("cT", [P, E])
        cf = sb("cf", [P, 4 * SQ + D + P + 4 + 4 + E + 2 + P + NBLK])
        o = 0
        rope = [cf[:, i * SQ:(i + 1) * SQ] for i in range(4)]
        o += 4 * SQ
        headmask = cf[:, o:o + D]
        o += D
        identf = cf[:, o:o + P]
        o += P
        own4, own4s = cf[:, o:o + 4], cf[:, o + 4:o + 8]
        o += 8
        iota8 = cf[:, o:o + E]
        o += E
        tok0 = cf[:, o:o + J]
        o += J
        trif = cf[:, o:o + P]
        o += P
        blkno = cf[:, o:o + NBLK]
        nqf = sb("nqf", [P, 512])
        nkf = sb("nkf", [P, 512])
        negq_b = sb("negq_b", [P, 512], BF16)
        negk_b = sb("negk_b", [P, 512], BF16)
        ident_b = sb("ident_b", [P, P], BF16)
        tri_b = sb("tri_b", [P, P], BF16)
        ones_b = sb("ones_b", [P, P], BF16)
        half = sb("half", [P, J])
        bvx = sb("bvx", [P, P])
        w1 = sb("w1", [P, E, F])
        w2 = sb("w2", [P, E, FC, D])
        gb = sb("gb", [P, 2, E])
        b1 = sb("b1", [P, E, FC])
        b2 = sb("b2", [P, E, D])
        mk = sb("mk", [P, NT, SQ // 4], I32)
        pen = sb("pen", [P, NT])
        tokid = sb("tokid", [P, J])
        xin = two("xin", [P, J, D])
        xn = two("xn", [P, J, D])
        xT = sb("xT", [P, TG])
        t1 = two("t1_", [P, TG])
        t2 = two("t2_", [P, TG])
        qf = sb("qf", [P, TG])
        kf = sb("kf", [P, TG])
        qhi = sb("qhi", [P, TG], F32R)
        qlo = sb("qlo", [P, TG], F32R)
        khi = sb("khi", [P, 2 * J, P], F32R)
        klo = sb("klo", [P, 2 * J, P], F32R)
        qst = two("qst", [P, 4, TG], F32R)
        qex = sb("qex", [P, 4, 4, TG], F32R)
        kst = two("kst", [P, 4, 2 * J, P], F32R)
        qz = two("qz", [P, 2 * J, P], F32R)
        kex = two("kex", [P, 4, TG], F32R)
        vau = two("vau", [P, J, H, 32])
        mx = sb("mx", [P, J, H])
        mt = sb("mt", [P, J, 4, 2, 4], BF16)
        prob = two("prob", [P, 512])
        ot = sb("ot", [P, J, 4, 2, 2, 16])
        rd = sb("rd", [P, J, 4, 2, 2])
        on = sb("on", [P, J, 2, 2, 4, HD])
        ont = two("ont", [P, J, 2, 2, 32])
        xr = two("xr", [P, J, D])
        cin = two("cin", [P, J, D])
        cxT = sb("cxT", [P, TG])
        x1 = two("x1", [P, J, D])
        xn1 = sb("xn1", [P, J, D])
        xT1 = sb("xT1", [P, TG])
        q2 = sb("q2", [P, TG])
        k2 = sb("k2", [P, J, 2, D])
        v2 = sb("v2", [P, J, D])
        mt2 = sb("mt2", [P, J, 2, D])
        r2s = sb("r2s", [P, J, 2, D])
        y1 = sb("y1", [P, J, D])
        yn = sb("yn", [P, J, D])
        pay = two("pay", [P, J, ROW])
        xp = sb("xp", [P, J, D])
        xpT = sb("xpT", [P, TG])
        stat = {s: sb(f"stat_{s}", [P, J, 6]) for s in "LTURQ"}
        mv = {s: sb(f"mv_{s}", [P, J, 2]) for s in "LTURQ"}
        ve = {s: sb(f"ve_{s}", [P, J]) for s in "LTURQ"}
        rs = {s: sb(f"rs_{s}", [P, J]) for s in "LTURQ"}
        nb = {s: sb(f"nb_{s}", [P, J]) for s in "LTU"}
        rc = sb("rc", [P, J])
        rm = sb("rm", [P, J])
        aff = sb("aff", [P, J, E])
        mx8 = sb("mx8", [P, J, 8])
        ix8 = sb("ix8", [P, J, 8], U32)
        idf = sb("idf", [P, J])
        ohb = sb("ohb", [P, J, E], BF16)
        ea = sb("ea", [P, J])
        ea1 = sb("ea1", [P, J])
        cnt = sb("cnt", [P, 2, E])
        rk = sb("rk", [P, J, E])
        slf = sb("slf", [P, J])
        sli = two("sli", [P, J], I32)
        ti = sb("ti", [P, E], I32)
        nbf = sb("nbf", [P, E])
        cum = sb("cum", [P, E])
        geb = sb("geb", [P, NBLK, E])
        gnb = sb("gnb", [P, NBLK, E])
        bex = sb("bex", [P, NBLK])
        bst = sb("bst", [P, NBLK])
        btf = sb("btf", [P, 2, NBLK])
        bti = sb("bti", [P, 2, NBLK], I32)
        prf = sb("prf", [P, E])
        pri = sb("pri", [P, E], I32)
        padt = sb("padt", [P, ROW])
        rb = [sb(f"rb{i}", [P, ROW]) for i in range(4)]
        idi = two("idi", [P, 1], I32)
        xh = two("xh", [P, D])
        bs = [sb(f"bs{i}", [P, D]) for i in range(4)]
        xhT = two("xhT", [P, P])
        hs = two("hs", [P, F])
        hT = two("hT", [P, FC, P])
        yb = two("yb", [P, D])
        yo = two("yo", [P, D])

        bank = [es.enter_context(nc.psum_tensor(f"bank{i}", [P, 512], FP32)) for i in range(8)]
        M = bank[0:3]
        B1 = bank[3:5]
        B2 = bank[5:7]
        BO_ = bank[7]

        def stage_steps(name, pieces):
            return Stage(name, pieces, NG, sem)

        pe_f = stage_steps("pe_front", "xT | QQ | KK | V")
        pe_s = stage_steps("pe_scores_for_max", "s0 | s1 | s2 | s3 | m0 m1")
        pe_a = stage_steps("pe_attention", "s0 | s1 | s2 | s3 | p0 | p1 | p2 | p3")
        pe_t = stage_steps("pe_cross", "cT | out | KV | xT | gram | Q2 | R | o2")
        pe_r = stage_steps("pe_route", "xT | aff | rank")
        ac_l = stage_steps("act_norm_x", "n")
        ac_f = stage_steps("act_front", "xT | V0 V1 | qhi | z0 z1 | khi | x0 x1 x2 x3")
        ac_s = stage_steps("act_maxima", "m0 m1 | e1 e2 e3")
        ac_a = stage_steps("act_exp", "e0 | e1 | e2 | e3")
        ac_t = stage_steps("act_cross", "cT | n | xT | Q2 | R | z")
        ac_r = stage_steps("act_route", "xT | ea")
        dv_l = stage_steps("dve_norm_x", "b0 b1 a0 a1")
        dv_f = stage_steps("dve_front", "q1 q2 | k1 k2")
        dv_s = stage_steps("dve_maxima", "m0 | m1 | m2 | m3 | hi lo | e0")
        dv_a = stage_steps("dve_attention", "ot | rd n0 n1 n2 n3 tr")
        dv_t = stage_steps("dve_cross", "x1 b0 b1 a0 a1 | k0 k1 v | mt | y0 y1 c0 c1 d0 d1")
        dv_r = stage_steps("dve_route", "b0 b1 a0 a1 | c p0 p1 | d0 d1 e0 e1 | cm A R C id tok B | "
                           "aff g0 g1 i0 i1 idf idm o0 o1 | al1 al | c1 rk tot pr sl nx s2 si")
        po_l = stage_steps("pool_norm_x", "eps pow mr nb")
        po_f = stage_steps("pool_front", "qf | qlo | kf | klo")
        po_t = stage_steps("pool_cross", "xb | eps pow mr nb | xnb x1b | eps2 pow2 mr2 nb2 | zg | x2")
        po_r = stage_steps("pool_route", "eps pow | eps2 pow2")
        d_x = [sem(f"dma_x{i}") for i in range(2)]
        d_xr = [sem(f"dma_x_again{i}") for i in range(2)]
        d_c = [sem(f"dma_ctx{i}") for i in range(2)]
        d_q = [sem(f"dma_q_stack{i}") for i in range(2)]
        d_k = [sem(f"dma_k_stack{i}") for i in range(2)]
        d_s = [sem(f"dma_scatter{i}") for i in range(2)]
        d_const = sem("dma_constants")
        d_weights = sem("dma_ffn_weights")
        d_pad = sem("dma_pad_rows")
        s_vec = sem("setup_vector")
        s_pool = sem("setup_pool")
        s_pe = sem("setup_tensor")
        s_tab = sem("block_table")
        s_zero = sem("setup_vector_zeros")
        s_pz = sem("setup_pool_zeros")
        s_mask = sem("setup_mask")
        s_chain = sem("block_table_chain")
        d_rb = [sem(f"dma_rows{i}") for i in range(4)]
        d_o = [sem(f"dma_out{i}") for i in range(2)]
        ffn = {k: Steps(sem(f"ffn_{k}"), k, NBLK) for k in
               ("pe_xT", "pe_h", "pe_hT", "pe_y", "act_xT", "act_relu", "dve_xh", "dve_h", 
                "dve_yb", "dve_yo", "pool_base", "pool_id")}

        Waits.passed = sem("waits_passed")

        def wait_b(eng, kind, n):
            wait(eng, ffn[kind], n, kind)

        def wait_rows(eng, b):
            wait_for(eng, d_rb[b.c % 4], (b.quarter + 1) * 16)

        def wait_out(eng, b):
            wait_for(eng, d_o[b.c % 2], b.half * 16)

        block = es.enter_context(nc.Block())

        DEPTH = 4
        FIRST, TOTAL = DEPTH + 2, NG + DEPTH
        LOOPS = (NG - 1 - FIRST) // 2

        def stage(g, back, op, *args):
            if g.back(back).within(NG):
                op(g.back(back), *args)

        def rounds(eng, one):
            for i in range(FIRST):
                one(Group(i))
            with eng.Fori(0, LOOPS) as it:
                one(Group(FIRST, it))
                one(Group(FIRST + 1, it))
            for i in range(FIRST + 2 * LOOPS, TOTAL):
                one(Group(i))

        BANK = {
            "x_turned": bank[0],
            "queries": bank[0],
            "max_scores0": bank[0],
            "max_scores2": bank[0],
            "max_rows0": bank[0],
            "projected": bank[0],
            "keys": bank[1],
            "max_scores1": bank[1],
            "max_rows1": bank[1],
            "ctx_turned": bank[1],
            "scores1": bank[1],
            "scores2": bank[1],
            "values": bank[2],
            "max_scores3": bank[2],
            "scores0": bank[2],
            "through_output": bank[2],
            "cross_queries": bank[2],
            "cross_keys_values": bank[3],
            "scores3": bank[3],
            "values_keys": bank[3],
            "weighted": bank[4],
            "x1_turned": bank[5],
            "cross_output": bank[5],
            "affinities": bank[5],
            "x2_turned": bank[6],
            "ranks": bank[6],
        }

        N_CONST = 13

        @block.sync
        def _(sp):
            for dst, src in ((ws[:, :, :], wself), (wc[:, :, :], wcross), (bc[:, :], bcol),
                             (cT[:, :], cent), (cf[:, :], consts), (nqf[:, :], negq), (nkf[:, :], negk),
                             (br[:, :, :].rearrange("p a d -> p (a d)"), brow.partition_broadcast(P)),
                             (gb[:, :, :], lngb), (b1[:, :, :], b1c), (padt[:, :], padc),
                             (b2[:, :, :].rearrange("p e d -> p (e d)"), b2r.partition_broadcast(P)),
                             (mk[:, :, :], m_rows)):
                sp.dma_start(dst, src).then_inc(d_const, 16)
            sp.dma_start(w1[:, :, :], w1t).then_inc(d_weights, 16)
            sp.dma_start(w2[:, :, :, :], w2t).then_inc(d_weights, 16)
            sp.wait_ge(d_const, 16 * N_CONST)
            sp.dma_start(rows[E * CAP:E * CAP + P, :], padt[:, :]).then_inc(d_pad, 16)
            sp.wait_ge(s_vec, 1)
            sp.wait_ge(s_pool, 1)

            def load_x(g):
                wait(sp, ac_l, g.n - 2, "n")
                sp.dma_start(xin[g.par][:, :, :],
                             x_rows[bass.ds(g.n * TG, TG), :].rearrange("(j p) d -> p j d", j=J)
                             ).then_inc(d_x[g.par], 16)

            def load_again(g):
                wait(sp, dv_t, g.n - 2, "x1")
                sp.dma_start(xr[g.par][:, :, :],
                             x_rows[bass.ds(g.n * TG, TG), :].rearrange("(j p) d -> p j d", j=J)
                             ).then_inc(d_xr[g.par], 16)
                wait(sp, pe_t, g.n - 2, "cT")
                sp.dma_start(cin[g.par][:, :, :],
                             c_rows[bass.ds(g.n * TG, TG), :].rearrange("(j p) d -> p j d", j=J)
                             ).then_inc(d_c[g.par], 16)

            def stack_q(g):
                wait(sp, dv_s, g.n - 2, "e0")
                wait(sp, ac_s, g.n - 2, "e3")
                wait(sp, ac_f, g.n, "qhi")
                wait(sp, po_f, g.n, "qlo")
                for s, src in enumerate((qhi, qhi, qlo)):
                    for r in range(4):
                        sp.dma_start(qst[g.par][32 * s:32 * s + 32, r, :].bitcast(FP32),
                                     src[32 * r:32 * r + 32, :].bitcast(FP32)).then_inc(d_q[g.par], 16)

            def stack_k(g):
                wait(sp, pe_a, g.n - 2, "s3")
                wait(sp, ac_f, g.n, "khi")
                wait(sp, po_f, g.n, "klo")
                for s, src in enumerate((khi, klo, khi)):
                    for r in range(4):
                        sp.dma_start(kst[g.par][32 * s:32 * s + 32, r, :, :].bitcast(FP32),
                                     src[32 * r:32 * r + 32, :, :].bitcast(FP32)).then_inc(d_k[g.par], 16)

            def one(g):
                stage(g, 0, load_x)
                stage(g, 1, load_again)
                stage(g, 1, stack_k)
                stage(g, 0, stack_q)

            rounds(nc.sync, one)

            sp.wait_ge(s_tab, 1)
            for e in range(E):
                at = nc.sync.value_load(pri[0:1, e:e + 1], min_val=0, max_val=(e + 1) * CAP - P)
                sp.dma_start(rows[bass.ds(at, P), :], padt[:, :]).then_inc(d_pad, 16)
            sp.wait_ge(d_pad, 16 * (E + 1))
            sp.wait_ge(d_s[0], 16 * J * ((NG + 1) // 2))
            sp.wait_ge(d_s[1], 16 * J * (NG // 2))

            def fetch(b):
                wait_b(sp, "pool_id", b.n - 4)
                wait_b(sp, "dve_yo", b.n - 4)
                at = nc.sync.value_load(bti[0:1, 1, bass.ds(b.n, 1)], min_val=0, max_val=E * CAP)
                sp.dma_start(rb[b.c % 4][:, :], rows[bass.ds(at, P), :]).then_inc(d_rb[b.c % 4], 16)

            for c in range(4):
                fetch(Block(c))
            with nc.sync.Fori(1, NBLK // 4) as it:
                for u in range(4):
                    fetch(Block(u, it, 4))
            for i in range(2):
                sp.wait_ge(d_o[i], 16 * NBLK // 2)

        @block.tensor
        def _(pe):
            mm, tr = nc.tensor.matmul, nc.tensor.transpose
            pe.wait_ge(d_const, 16 * N_CONST)
            pe.wait_ge(s_vec, 2)
            mm(M[0][:, 0:D], bvx[:, :], WO, start=True, stop=True).then_inc(s_pe, 1)
            pe.wait_ge(d_weights, 32)
            for e in range(E):
                for c in range(FC):
                    last = mm(M[1][:, e * FC + c:e * FC + c + 1], w1[:, e, c * P:(c + 1) * P],
                              gb[:, 1, e:e + 1], start=True, stop=True)
            last.then_inc(s_pe, 1)
            pe.wait_ge(s_vec, 4)

            BEFORE = {
                "x_turned": [(dv_t, "x1", -2), (ac_s, "m0", -1), (dv_s, "m2", -1), (dv_s, "m0", -1),
                    (dv_f, "q2", -1), (ac_f, "xT", -1)],
                "queries": [(ac_f, "xT", 0), (dv_t, "x1", -2), (ac_s, "m0", -1), (dv_s, "m2", -1),
                    (dv_s, "m0", -1), (dv_f, "q2", -1)],
                "max_scores0": [(dv_f, "q2", 0), (ac_f, "xT", 0), (dv_t, "x1", -2), (ac_s, "m0", -1),
                    (dv_s, "m2", -1), (dv_s, "m0", -1)],
                "max_scores2": [(dv_s, "m0", 0), (dv_f, "q2", 0), (ac_f, "xT", 0), (dv_t, "x1", -2),
                    (ac_s, "m0", -1), (dv_s, "m2", -1)],
                "max_rows0": [(dv_s, "m2", 0), (dv_s, "m0", 0), (dv_f, "q2", 0), (ac_f, "xT", 0),
                    (dv_t, "x1", -2), (ac_s, "m0", -1)],
                "projected": [(ac_s, "m0", 1), (dv_s, "m2", 1), (dv_s, "m0", 1), (dv_f, "q2", 1),
                    (ac_f, "xT", 1), (dv_t, "x1", -1)],
                "keys": [(ac_t, "cT", -1), (ac_s, "m1", -1), (ac_a, "e2", -2), (dv_s, "m1", -1),
                    (ac_a, "e1", -2), (dv_f, "k2", -1)],
                "max_scores1": [(ac_a, "e1", -1), (dv_f, "k2", 0), (ac_t, "cT", -1), (ac_s, "m1", -1),
                    (ac_a, "e2", -2), (dv_s, "m1", -1)],
                "max_rows1": [(ac_a, "e2", -1), (dv_s, "m1", 0), (ac_a, "e1", -1), (dv_f, "k2", 0),
                    (ac_t, "cT", -1), (ac_s, "m1", -1)],
                "ctx_turned": [(ac_s, "m1", 0), (ac_a, "e2", -1), (dv_s, "m1", 0), (ac_a, "e1", -1),
                    (dv_f, "k2", 0), (ac_t, "cT", -1)],
                "scores1": [(dv_f, "k2", 1), (ac_t, "cT", 0), (ac_s, "m1", 0), (ac_a, "e2", -1),
                    (dv_s, "m1", 0), (ac_a, "e1", -1)],
                "scores2": [(dv_s, "m1", 1), (ac_a, "e1", 0), (dv_f, "k2", 1), (ac_t, "cT", 0),
                    (ac_s, "m1", 0), (ac_a, "e2", -1)],
                "values": [(ac_t, "R", -2), (dv_s, "m3", -1), (ac_t, "Q2", -3), (ac_a, "e0", -2),
                    (ac_f, "V1", -1)],
                "max_scores3": [(ac_t, "Q2", -2), (ac_a, "e0", -1), (ac_f, "V1", 0), (ac_t, "R", -2),
                    (dv_s, "m3", -1)],
                "scores0": [(ac_f, "V1", 1), (ac_t, "R", -1), (dv_s, "m3", 0), (ac_t, "Q2", -2),
                    (ac_a, "e0", -1)],
                "through_output": [(dv_s, "m3", 1), (ac_t, "Q2", -1), (ac_a, "e0", 0), (ac_f, "V1", 1),
                    (ac_t, "R", -1)],
                "cross_queries": [(ac_a, "e0", 1), (ac_f, "V1", 2), (ac_t, "R", 0), (dv_s, "m3", 1),
                    (ac_t, "Q2", -1)],
                "cross_keys_values": [(ac_a, "e3", -1), (dv_t, "mt", -1), (dv_t, "v", -1)],
                "scores3": [(dv_t, "mt", 0), (dv_t, "v", 0), (ac_a, "e3", -1)],
                "values_keys": [(dv_t, "v", 0), (ac_a, "e3", -1), (dv_t, "mt", -1)],
                "weighted": [(dv_a, "ot", -1)],
                "x1_turned": [(dv_r, "aff", -2), (dv_t, "y1", -1), (ac_t, "xT", -1)],
                "cross_output": [(ac_t, "xT", 0), (dv_r, "aff", -2), (dv_t, "y1", -1)],
                "affinities": [(dv_t, "y1", 1), (ac_t, "xT", 1), (dv_r, "aff", -1)],
                "x2_turned": [(dv_r, "tot", -1), (ac_r, "xT", -1)],
                "ranks": [(ac_r, "xT", 0), (dv_r, "tot", -1)],
            }

            def free(g, use):
                for stage, name, ahead in BEFORE[use] if g.it is None else BEFORE[use][:1]:
                    wait(pe, stage, g.n + ahead, name)

            def x_turned(g):
                wait(pe, ac_l, g.n, "n")
                free(g, "x_turned")
                for j in range(J):
                    last = tr(BANK["x_turned"][:, j * P:(j + 1) * P], xn[g.par][:, j, :], identf)
                last.then_inc(*pe_f.done("xT"))

            def queries(g):
                wait(pe, ac_f, g.n, "xT")
                free(g, "queries")
                for i, w in enumerate((WQ, WQR)):
                    last = mm(BANK["queries"][:, i * TG:(i + 1) * TG], w, xT[:, :], start=True, stop=True)
                last.then_inc(*pe_f.done("QQ"))

            def keys(g):
                wait(pe, ac_f, g.n, "xT")
                free(g, "keys")
                for i, w in enumerate((WK, WKR)):
                    last = mm(BANK["keys"][:, i * TG:(i + 1) * TG], w, xT[:, :], start=True, stop=True)
                last.then_inc(*pe_f.done("KK"))

            def values(g):
                wait(pe, ac_f, g.n, "xT")
                free(g, "values")
                for j in range(J):
                    last = mm(BANK["values"][:, j * D:(j + 1) * D], xT[:, j * P:(j + 1) * P], WV,
                              start=True, stop=True)
                last.then_inc(*pe_f.done("V"))

            def max_scores(g, k):
                wait(pe, ac_f, g.n, "z1")
                wait(pe, ac_f, g.n, "x3")
                free(g, f"max_scores{k}")
                bank_, strip = BANK[f"max_scores{k}"], slice(32 * k, 32 * k + 32)
                mm(bank_[:, :], ident_b[:, :], negq_b[:, :], start=True, stop=False)
                for j in range(J):
                    for b in range(2):
                        q = 2 * j + b
                        last = mm(bank_[:, 256 * j:256 * j + 256], qz[g.par][strip, q, :],
                                  kex[g.par][strip, :, q * SQ:(q + 1) * SQ],
                                  start=False, stop=j == J - 1 and b == 1, tile_position=(32 * k, 0))
                last.then_inc(*pe_s.done(f"s{k}"))

            def max_rows(g):
                wait(pe, dv_s, g.n, "lo")
                for i in range(2):
                    free(g, f"max_rows{i}")
                    for h_ in range(2):
                        for j in range(J):
                            last = mm(BANK[f"max_rows{i}"][96:104, (2 * h_ + j) * P:(2 * h_ + j + 1) * P],
                                      mt[:, j, 2 * i + h_, :, :].rearrange("p t h -> p (t h)"),
                                      ident_b[:, :], start=True, stop=True, tile_position=(0, 96))
                    last.then_inc(*pe_s.done(f"m{i}"))

            def scores(g, k):
                j, c = k // 2, k % 2
                if k == 0:
                    wait_dma(pe, d_k, g, 12)
                    wait(pe, dv_s, g.n, "e0")
                    wait(pe, ac_s, g.n, "e3")
                free(g, f"scores{k}")
                bank_ = BANK[f"scores{k}"]
                mm(bank_[:, :], ident_b[:, :], negk_b[:, :], start=True, stop=False)
                for r_ in range(2):
                    for b in range(2):
                        q = 2 * j + b
                        last = mm(bank_[:, 256 * r_:256 * r_ + 256], kst[g.par][:, 2 * c + r_, q, :],
                                  qex[:, 2 * c + r_, :, q * SQ:(q + 1) * SQ],
                                  start=False, stop=r_ == 1 and b == 1)
                last.then_inc(*pe_a.done(f"s{k}"))

            def weighted(g, k):
                j, c = k // 2, k % 2
                wait(pe, ac_a, g.n, f"e{k}")
                if k == 0:
                    wait(pe, ac_f, g.n, "V1")
                    free(g, "weighted")
                for i in range(8):
                    h = 8 * c + i
                    o_ = BANK["weighted"][32 * (h // 4):32 * (h // 4) + 32,
                                          j * 256 + (h % 4) * SQ:j * 256 + (h % 4 + 1) * SQ]
                    last = mm(o_, vau[g.par][:, j, h, :], prob[k % 2][:, i * SQ:(i + 1) * SQ],
                              start=True, stop=True, tile_position=(0, 32 * (h // 4)))
                last.then_inc(*pe_a.done(f"p{k}"))

            def ctx_turned(g):
                wait_dma(pe, d_c, g)
                free(g, "ctx_turned")
                for j in range(J):
                    last = tr(BANK["ctx_turned"][:, j * P:(j + 1) * P], cin[g.par][:, j, :], identf)
                last.then_inc(*pe_t.done("cT"))

            def projected(g):
                wait(pe, dv_a, g.n, "tr")
                free(g, "projected")
                for j in range(J):
                    last = mm(BANK["projected"][:, j * D:(j + 1) * D],
                              ont[g.par][:, j, :, :, :].rearrange("p b q t -> p (b q t)"), WO,
                              start=True, stop=True)
                last.then_inc(*pe_t.done("out"))

            def x1_turned(g):
                wait(pe, ac_t, g.n, "n")
                free(g, "x1_turned")
                for j in range(J):
                    last = tr(BANK["x1_turned"][:, j * P:(j + 1) * P], xn1[:, j, :], identf)
                last.then_inc(*pe_t.done("xT"))

            def cross_keys_values(g):
                wait(pe, ac_t, g.n, "cT")
                free(g, "cross_keys_values")
                for j in range(J):
                    last = mm(BANK["cross_keys_values"][:, j * 256:(j + 1) * 256], cxT[:, j * P:(j + 1) * P],
                              wc[:, 1:3, :], start=True, stop=True)
                last.then_inc(*pe_t.done("KV"))

            def cross_queries(g):
                wait(pe, ac_t, g.n, "xT")
                free(g, "cross_queries")
                mm(BANK["cross_queries"][:, 0:TG], wc[:, 0, :], xT1[:, :], start=True, stop=True
                   ).then_inc(*pe_t.done("Q2"))

            def values_keys(g):
                wait(pe, dv_t, g.n, "v")
                free(g, "values_keys")
                for j in range(J):
                    last = mm(BANK["values_keys"][:, j * 256:(j + 1) * 256], v2[:, j, :], k2[:, j, :, :],
                              start=True, stop=True)
                last.then_inc(*pe_t.done("gram"))

            def through_output(g):
                wait(pe, dv_t, g.n, "mt")
                free(g, "through_output")
                for j in range(J):
                    for b in range(2):
                        last = mm(BANK["through_output"][:, (2 * j + b) * D:(2 * j + b + 1) * D],
                                  mt2[:, j, b, :], wc[:, 3, :], start=True, stop=True)
                last.then_inc(*pe_t.done("R"))

            def cross_output(g):
                wait(pe, ac_t, g.n, "R")
                wait(pe, ac_t, g.n, "Q2")
                free(g, "cross_output")
                for j in range(J):
                    last = mm(BANK["cross_output"][:, j * 256:(j + 1) * 256], q2[:, j * P:(j + 1) * P],
                              r2s[:, j, :, :], start=True, stop=True)
                last.then_inc(*pe_t.done("o2"))

            def x2_turned(g):
                wait(pe, dv_r, g.n, "p1")
                free(g, "x2_turned")
                for j in range(J):
                    last = tr(BANK["x2_turned"][:, j * P:(j + 1) * P], xp[:, j, :], identf)
                last.then_inc(*pe_r.done("xT"))

            def affinities(g):
                wait(pe, ac_r, g.n, "xT")
                free(g, "affinities")
                for j in range(J):
                    last = mm(BANK["affinities"][:, j * E:(j + 1) * E], xpT[:, j * P:(j + 1) * P], cT[:, :],
                              start=True, stop=True)
                last.then_inc(*pe_r.done("aff"))

            def ranks(g):
                wait(pe, dv_r, g.n, "o1")
                free(g, "ranks")
                mm(BANK["ranks"][:, 0:J * E], tri_b[:, :], ohb[:, :, :], start=True, stop=True)
                mm(BANK["ranks"][:, 16:16 + J * E], ones_b[:, :], ohb[:, :, :], start=True, stop=True
                   ).then_inc(*pe_r.done("rank"))

            def one(g):
                stage(g, 2, weighted, 3)
                stage(g, 2, through_output)
                stage(g, 4, affinities)
                stage(g, 2, projected)
                stage(g, 1, ctx_turned)
                stage(g, 0, x_turned)
                stage(g, 1, cross_keys_values)
                stage(g, 0, queries)
                stage(g, 0, keys)
                stage(g, 0, values)
                stage(g, 2, x1_turned)
                stage(g, 4, ranks)
                stage(g, 1, scores, 0)
                stage(g, 1, scores, 1)
                stage(g, 0, max_scores, 0)
                stage(g, 1, weighted, 0)
                stage(g, 1, values_keys)
                stage(g, 2, cross_queries)
                stage(g, 0, max_scores, 1)
                stage(g, 0, max_scores, 2)
                stage(g, 1, weighted, 1)
                stage(g, 0, max_scores, 3)
                stage(g, 1, scores, 2)
                stage(g, 1, scores, 3)
                stage(g, 2, cross_output)
                stage(g, 0, max_rows)
                stage(g, 3, x2_turned)
                stage(g, 1, weighted, 2)

            rounds(nc.tensor, one)

            fx, fy = [M[0], M[1]], [M[2], BO_]

            def expert(b):
                return nc.tensor.value_load(bti[0:1, 0, bass.ds(b.n, 1)], min_val=0, max_val=E - 1)

            def transposed(b):
                wait_b(pe, "dve_xh", b.n)
                wait_b(pe, "act_xT", b.n - 2)
                tr(fx[b.c % 2][:, 0:P], xh[b.c % 2][:, :], identf).then_inc(*ffn["pe_xT"].done("pe_xT"))

            def hidden(b, e):
                u = b.c % 2
                wait_b(pe, "act_xT", b.n)
                wait_b(pe, "dve_h", b.n - 2)
                mm(B1[u][:, :], xhT[u][:, :], w1[:, bass.ds(e, 1), :], start=True, stop=True
                   ).then_inc(*ffn["pe_h"].done("pe_h"))

            def turned(b):
                u = b.c % 2
                wait_b(pe, "dve_h", b.n)
                wait_b(pe, "act_relu", b.n - 2)
                for c in range(FC):
                    last = tr(B2[u][:, c * P:(c + 1) * P], hs[u][:, c * P:(c + 1) * P], identf)
                last.then_inc(*ffn["pe_hT"].done("pe_hT"))

            def second(b, e):
                u = b.c % 2
                wait_b(pe, "act_relu", b.n)
                wait_b(pe, "dve_yb", b.n - 2)
                for c in range(FC):
                    last = mm(fy[u][:, 0:D], hT[u][:, c, :], w2[:, bass.ds(e, 1), c, :],
                              start=c == 0, stop=c == FC - 1)
                last.then_inc(*ffn["pe_y"].done("pe_y"))

            pe.wait_ge(s_tab, 1)
            pe.wait_ge(s_pool, 2)
            transposed(Block(0))
            hidden(Block(0), expert(Block(0)))

            def step(b):
                transposed(b.on(1))
                turned(b)
                hidden(b.on(1), expert(b.on(1)))
                second(b, expert(b))

            step(Block(0))
            step(Block(1))
            with nc.tensor.Fori(1, NBLK // 2 - 1) as it:
                step(Block(0, it, 2))
                step(Block(1, it, 2))
            step(Block(NBLK - 2))
            turned(Block(NBLK - 1))
            second(Block(NBLK - 1), expert(Block(NBLK - 1)))

        @block.scalar
        def _(ac):
            act, cp = nc.scalar.activation, nc.scalar.copy

            def norm_x(g):
                wait(ac, po_l, g.n, "nb")
                wait(ac, pe_f, g.n - 2, "xT")
                for j in range(J):
                    last = act(xn[g.par][:, j, :], xin[g.par][:, j, :], ACT.Identity,
                               bias=nb["L"][:, j:j + 1], scale=rs["L"][:, j:j + 1])
                last.then_inc(*ac_l.done("n"))

            def x_turned(g):
                wait(ac, pe_f, g.n, "xT")
                wait(ac, pe_f, g.n - 1, "QQ")
                wait(ac, pe_f, g.n - 1, "KK")
                wait(ac, pe_f, g.n - 1, "V")
                cp(xT[:, :], BANK["x_turned"][:, 0:TG]).then_inc(*ac_f.done("xT"))

            def values(g):
                wait(ac, pe_f, g.n, "V")
                wait(ac, pe_a, g.n - 2, "p3")
                for b in range(2):
                    cp(vau[g.par][64 * b:64 * b + 64, :, :, 16 * b:16 * b + HD],
                       BANK["values"][64 * b:64 * b + 64, 0:TG].rearrange("p (j h d) -> p j h d", j=J, h=H)
                       ).then_inc(*ac_f.done(f"V{b}"))

            def q_high(g):
                wait(ac, po_f, g.n, "qf")
                wait_dma(ac, d_q, g.back(1), 12)
                cp(qhi[:, :], qf[:, :]).then_inc(*ac_f.done("qhi"))

            def q_padded(g):
                wait(ac, po_f, g.n, "qf")
                wait(ac, pe_s, g.n - 2, "s3")
                qd = qz[g.par][:, :, :].rearrange("p (j b) (c q) -> p j b c q", b=2, c=2)
                qs_ = qf[:, :].rearrange("p (j b q) -> p j b q", j=J, b=2)
                for b in range(2):
                    cp(qd[:, :, b, b, :], qs_[:, :, b, :]).then_inc(*ac_f.done(f"z{b}"))

            def k_high(g):
                wait(ac, po_f, g.n, "kf")
                wait_dma(ac, d_k, g.back(1), 12)
                diag = khi[:, :, :].rearrange("p (j b) (c k) -> p j b c k", b=2, c=2)
                for b in range(2):
                    last = cp(diag[:, :, b, b, :],
                              kf[:, :].rearrange("p (j b k) -> p j b k", j=J, b=2)[:, :, b, :])
                last.then_inc(*ac_f.done("khi"))

            def k_by_head(g):
                wait(ac, po_f, g.n, "kf")
                wait(ac, pe_s, g.n - 2, "s3")
                for i in range(4):
                    act(kex[g.par][:, i, :], kf[:, :], ACT.Copy, scale=own4[:, i:i + 1]
                        ).then_inc(*ac_f.done(f"x{i}"))

            def max_rows(g):
                wait_dma(ac, d_q, g, 12)
                wait(ac, ac_s, g.n - 2, "e3")
                wait(ac, dv_s, g.n - 2, "e0")
                for i in range(2):
                    wait(ac, pe_s, g.n, f"m{i}")
                    cp(qst[g.par][96:104, 2 * i:2 * i + 2, :].rearrange("p r t -> p (r t)"),
                       BANK[f"max_rows{i}"][96:104, :]).then_inc(*ac_s.done(f"m{i}"))

            def q_by_head(g):
                wait(ac, pe_a, g.n - 1, "s3")
                wait(ac, ac_s, g.n, "m1")
                for i in range(1, 4):
                    act(qex[:, :, i, :], qst[g.par][:, :, :].bitcast(FP32), ACT.Copy,
                        scale=own4s[:, i:i + 1]).then_inc(*ac_s.done(f"e{i}"))

            def exp(g, k):
                wait(ac, pe_a, g.n, f"s{k}")
                if k < 2:
                    wait(ac, pe_a, g.n - 1, f"p{k + 2}")
                else:
                    wait(ac, pe_a, g.n, f"p{k - 2}")
                act(prob[k % 2][:, :], BANK[f"scores{k}"][:, :], ACT.Exp).then_inc(*ac_a.done(f"e{k}"))

            def ctx_turned(g):
                wait(ac, pe_t, g.n, "cT")
                wait(ac, pe_t, g.n - 1, "KV")
                cp(cxT[:, :], BANK["ctx_turned"][:, 0:TG]).then_inc(*ac_t.done("cT"))

            def norm_x1(g):
                wait(ac, po_t, g.n, "nb")
                wait(ac, po_t, g.n - 1, "xnb")
                wait(ac, dv_t, g.n - 1, "y1")
                for j in range(J):
                    last = act(xn1[:, j, :], x1[g.par][:, j, :], ACT.Identity,
                               bias=nb["T"][:, j:j + 1], scale=rs["T"][:, j:j + 1])
                last.then_inc(*ac_t.done("n"))

            def x1_turned(g):
                wait(ac, pe_t, g.n, "xT")
                wait(ac, pe_t, g.n - 1, "Q2")
                cp(xT1[:, :], BANK["x1_turned"][:, 0:TG]).then_inc(*ac_t.done("xT"))

            def cross_queries(g):
                wait(ac, pe_t, g.n, "Q2")
                wait(ac, pe_t, g.n - 1, "o2")
                act(q2[:, :], BANK["cross_queries"][:, 0:TG], ACT.Identity, bias=bc[:, 4:5]
                    ).then_inc(*ac_t.done("Q2"))

            def through_output(g):
                wait(ac, pe_t, g.n, "R")
                wait(ac, pe_t, g.n - 1, "o2")
                cp(r2s[:, :, :, :].rearrange("p j b d -> p (j b d)"), BANK["through_output"][:, :]
                   ).then_inc(*ac_t.done("R"))

            def norm_y(g):
                wait(ac, po_t, g.n, "nb2")
                wait(ac, po_t, g.n - 1, "x2")
                for j in range(J):
                    last = act(yn[:, j, :], y1[:, j, :], ACT.Identity,
                               bias=nb["U"][:, j:j + 1], scale=rs["U"][:, j:j + 1])
                last.then_inc(*ac_t.done("z"))

            def x2_turned(g):
                wait(ac, pe_r, g.n, "xT")
                wait(ac, pe_r, g.n - 1, "aff")
                cp(xpT[:, :], BANK["x2_turned"][:, 0:TG]).then_inc(*ac_r.done("xT"))

            def exp_affinity(g):
                wait(ac, dv_r, g.n, "g1")
                wait(ac, dv_r, g.n - 1, "al1")
                act(ea[:, :], mx8[:, :, 0], ACT.Exp, scale=-1.0).then_inc(*ac_r.done("ea"))

            def one(g):
                stage(g, 1, max_rows)
                stage(g, 1, q_by_head)
                stage(g, 0, norm_x)
                stage(g, 1, ctx_turned)
                stage(g, 2, through_output)
                stage(g, 0, x_turned)
                stage(g, 3, norm_y)
                stage(g, 2, norm_x1)
                stage(g, 4, exp_affinity)
                stage(g, 0, values)
                stage(g, 0, q_high)
                stage(g, 0, q_padded)
                stage(g, 0, k_by_head)
                stage(g, 1, exp, 0)
                stage(g, 2, x1_turned)
                stage(g, 0, k_high)
                stage(g, 1, exp, 1)
                stage(g, 2, cross_queries)
                stage(g, 1, exp, 2)
                stage(g, 1, exp, 3)
                stage(g, 3, x2_turned)

            ac.wait_ge(d_const, 16 * N_CONST)
            ac.wait_ge(s_vec, 1)
            ac.wait_ge(s_pool, 1)
            rounds(nc.scalar, one)

            ac.wait_ge(s_tab, 1)

            def turned(b):
                u = b.c % 2
                wait_b(ac, "pe_xT", b.n)
                wait_b(ac, "pe_h", b.n - 2)
                cp(xhT[u][:, :], M[u][:, 0:P]).then_inc(*ffn["act_xT"].done("act_xT"))

            def relu(b):
                u = b.c % 2
                e = nc.scalar.value_load(bti[0:1, 0, bass.ds(b.n, 1)], min_val=0, max_val=E - 1)
                wait_b(ac, "pe_hT", b.n)
                wait_b(ac, "pe_y", b.n - 2)
                for c in range(FC):
                    last = act(hT[u][:, c, :], B2[u][:, c * P:(c + 1) * P], ACT.Relu,
                               bias=b1[:, bass.ds(e, 1), c])
                last.then_inc(*ffn["act_relu"].done("act_relu"))

            turned(Block(0))
            turned(Block(1))
            relu(Block(0))
            turned(Block(2))
            relu(Block(1))
            with nc.scalar.Fori(1, NBLK // 2 - 1) as it:
                turned(Block(1, it, 2))
                relu(Block(0, it, 2))
                turned(Block(2, it, 2))
                relu(Block(1, it, 2))
            turned(Block(NBLK - 1))
            relu(Block(NBLK - 2))
            relu(Block(NBLK - 1))

        @block.vector
        def _(dv):
            v = nc.vector

            def stats(stage, n, src, key, b, a):
                for j in range(J):
                    v.bn_stats(stat[key][:, j, :], src(j)).then_inc(*stage.done(f"{b}{j}"))
                wait(dv, stage, n, f"{b}1", alone=True)
                for j in range(J):
                    v.bn_aggr(mv[key][:, j, :], stat[key][:, j, :]).then_inc(*stage.done(f"{a}{j}"))

            def stats_x(g):
                wait(dv, po_l, g.n - 1, "nb")
                wait(dv, dv_l, g.n - 1, "a1")
                wait_dma(dv, d_x, g)
                stats(dv_l, g.n, lambda j: xin[g.par][:, j, :], "L", "b", "a")

            def rotate_q(g):
                wait(dv, pe_f, g.n, "QQ")
                wait(dv, po_f, g.n - 1, "qf")
                for i, buf in enumerate((t1, t2)):
                    v.scalar_tensor_tensor(
                        buf[0][:, :].rearrange("p (s t) -> p s t", t=SQ),
                        BANK["queries"][:, i * TG:(i + 1) * TG].rearrange("p (s t) -> p s t", t=SQ),
                        bc[:, i:i + 1], rope[i].unsqueeze(1).broadcast_to((P, 2 * J, SQ)), ALU.add, ALU.mult
                    ).then_inc(*dv_f.done(f"q{i + 1}"))

            def rotate_k(g):
                wait(dv, pe_f, g.n, "KK")
                wait(dv, po_f, g.n - 1, "kf")
                for i, buf in enumerate((t1, t2)):
                    v.scalar_tensor_tensor(
                        buf[1][:, :].rearrange("p (s t) -> p s t", t=SQ),
                        BANK["keys"][:, i * TG:(i + 1) * TG].rearrange("p (s t) -> p s t", t=SQ),
                        bc[:, 2 + i:3 + i], rope[2 + i].unsqueeze(1).broadcast_to((P, 2 * J, SQ)),
                        ALU.add, ALU.mult).then_inc(*dv_f.done(f"k{i + 1}"))

            def row_max(g, k):
                wait(dv, pe_s, g.n, f"s{k}")
                wait(dv, dv_s, g.n - 1, "lo")
                v.tensor_reduce(mx[:, :, 4 * k:4 * k + 4],
                                BANK[f"max_scores{k}"][:, :].rearrange("p (j h k) -> p j h k", j=J, k=SQ),
                                AX.X, ALU.max).then_inc(*dv_s.done(f"m{k}"))

            def max_parts(g):
                for k in range(4):
                    wait(dv, dv_s, g.n, f"m{k}")
                wait(dv, pe_s, g.n - 1, "m1")
                mxv = mx[:, :, :].rearrange("p j (r h) -> p (j r) h", h=4)
                mtv = mt[:, :, :, :, :].rearrange("p j r t h -> p (j r) t h")
                v.tensor_scalar(mtv[:, :, 0, :], mxv, -1.0, None, ALU.mult).then_inc(*dv_s.done("hi"))
                wait(dv, dv_s, g.n, "hi")
                v.scalar_tensor_tensor(mtv[:, :, 1, :], mxv, -1.0, mtv[:, :, 0, :],
                                       ALU.mult, ALU.subtract).then_inc(*dv_s.done("lo"))

            def q_by_head(g):
                wait(dv, ac_s, g.n, "m1")
                wait(dv, pe_a, g.n - 1, "s3")
                v.tensor_scalar(qex[:, :, 0, :], qst[g.par][:, :, :].bitcast(FP32),
                                own4s[:, 0:1], None, ALU.mult).then_inc(*dv_s.done("e0"))

            def weighted_turned(g):
                wait(dv, pe_a, g.n, "p3")
                wait(dv, dv_a, g.n - 1, "n3")
                v.transpose(ot[:, :, :, :, :, :].rearrange("p j g q b t -> p (j g q b t)"),
                            BANK["weighted"][:, :]).then_inc(*dv_a.done("ot"))

            def divide(g):
                wait(dv, dv_a, g.n, "ot")
                v.reciprocal(rd[:, :, :, :, :], ot[:, :, :, :, :, HD]).then_inc(*dv_a.done("rd"))
                wait(dv, dv_a, g.n, "rd")
                wait(dv, dv_a, g.n - 1, "tr")
                for j in range(J):
                    for b in range(2):
                        v.tensor_tensor(
                            on[:, j, b, :, :, :], ot[:, j, :, :, b, 0:HD].rearrange("p g q d -> p q g d"),
                            rd[:, j, :, :, b].rearrange("p g q -> p q g").unsqueeze(3)
                            .broadcast_to((P, 2, 4, HD)), ALU.mult).then_inc(*dv_a.done(f"n{2 * j + b}"))
                wait(dv, dv_a, g.n, "n3")
                wait(dv, pe_t, g.n - 2, "out")
                v.transpose(ont[g.par][:, :, :, :, :].rearrange("p j b q t -> p (j b q t)"),
                            on[:, :, :, :, :, :].rearrange("p j b q g d -> p (j b q g d)")
                            ).then_inc(*dv_a.done("tr"))

            def x1_sum(g):
                wait(dv, pe_t, g.n, "out")
                wait(dv, po_t, g.n, "xb")
                wait(dv, po_t, g.n - 2, "x2")
                wait(dv, po_t, g.n - 1, "nb")
                v.tensor_tensor(x1[g.par][:, :, :].rearrange("p j d -> p (j d)"), BANK["projected"][:, 0:TG],
                                xr[g.par][:, :, :].rearrange("p j d -> p (j d)"), ALU.add
                                ).then_inc(*dv_t.done("x1"))
                wait(dv, dv_t, g.n, "x1")
                stats(dv_t, g.n, lambda j: x1[g.par][:, j, :], "T", "b", "a")

            def cross_keys_values(g):
                wait(dv, pe_t, g.n, "KV")
                wait(dv, pe_t, g.n - 1, "gram")
                kv = BANK["cross_keys_values"][:, :].rearrange("p (j a d) -> p j a d", j=J, a=2)
                for b in range(2):
                    rows_ = slice(64 * b, 64 * b + 64)
                    v.tensor_tensor(k2[rows_, :, b, :], kv[rows_, :, 0, :],
                                    BK2[rows_].unsqueeze(1).broadcast_to((64, J, D)), ALU.add
                                    ).then_inc(*dv_t.done(f"k{b}"))
                v.tensor_tensor(v2[:, :, :], kv[:, :, 1, :], BV2.unsqueeze(1).broadcast_to((P, J, D)),
                                ALU.add).then_inc(*dv_t.done("v"))

            def own_head(g):
                wait(dv, pe_t, g.n, "gram")
                wait(dv, pe_t, g.n - 1, "R")
                v.tensor_tensor(mt2[:, :, :, :].rearrange("p j b d -> p (j b) d"),
                                BANK["values_keys"][:, :].rearrange("p (a d) -> p a d", d=D),
                                headmask.unsqueeze(1).broadcast_to((P, 2 * J, D)), ALU.mult
                                ).then_inc(*dv_t.done("mt"))

            def y_sum(g):
                wait(dv, pe_t, g.n, "o2")
                wait(dv, po_t, g.n, "xnb")
                wait(dv, ac_t, g.n - 1, "z")
                o2v = BANK["cross_output"][:, :].rearrange("p (j b d) -> p j b d", j=J, b=2)
                for b in range(2):
                    rows_ = slice(64 * b, 64 * b + 64)
                    v.tensor_tensor(y1[rows_, :, :], o2v[rows_, :, b, :], xn1[rows_, :, :], ALU.add
                                    ).then_inc(*dv_t.done(f"y{b}"))
                wait(dv, dv_t, g.n, "y1")
                stats(dv_t, g.n, lambda j: y1[:, j, :], "U", "c", "d")

            def stats_x2(g):
                wait(dv, po_t, g.n, "x2")
                wait(dv, dv_r, g.n - 1, "c")
                wait(dv, po_r, g.n - 1, "pow")
                stats(dv_r, g.n, lambda j: pay[g.par][:, j, 0:D], "R", "b", "a")

            def norm_x2(g):
                wait(dv, po_r, g.n, "pow")
                wait(dv, dv_r, g.n - 1, "C")
                wait(dv, dv_r, g.n - 1, "cm")
                v.scalar_tensor_tensor(rc[:, :], mv["R"][:, :, 0], -1.0, rs["R"][:, :],
                                       ALU.mult, ALU.mult).then_inc(*dv_r.done("c"))
                wait(dv, dv_r, g.n, "c")
                wait(dv, pe_r, g.n - 1, "xT")
                for j in range(J):
                    v.tensor_scalar(xp[:, j, :], pay[g.par][:, j, 0:D], rs["R"][:, j:j + 1], rc[:, j:j + 1],
                                    ALU.mult, ALU.add).then_inc(*dv_r.done(f"p{j}"))

            def stats_norm(g):
                wait(dv, dv_r, g.n, "p1")
                wait(dv, dv_r, g.n - 1, "B")
                wait(dv, po_r, g.n - 1, "pow2")
                stats(dv_r, g.n, lambda j: xp[:, j, :], "Q", "d", "e")

            def row_scalars(g):
                px = pay[g.par]
                wait(dv, po_r, g.n, "pow2")
                v.tensor_tensor(rm[:, :], rc[:, :], mv["Q"][:, :, 0], ALU.subtract
                                ).then_inc(*dv_r.done("cm"))
                v.tensor_tensor(px[:, :, C_A], rs["R"][:, :], rs["Q"][:, :], ALU.mult
                                ).then_inc(*dv_r.done("A"))
                v.tensor_scalar(px[:, :, C_R], rs["R"][:, :], 1.0, None, ALU.add
                                ).then_inc(*dv_r.done("R"))
                v.tensor_tensor(px[:, :, C_C], rc[:, :], pen[:, bass.ds(g.n * J, J)], ALU.add
                                ).then_inc(*dv_r.done("C"))
                wait(dv, dv_r, g.n - 1, "tok")
                v.tensor_copy(px[:, :, C_ID], tokid[:, :]).then_inc(*dv_r.done("id"))
                wait(dv, dv_r, g.n, "id")
                v.tensor_scalar(tokid[:, :], tokid[:, :], float(TG), None, ALU.add
                                ).then_inc(*dv_r.done("tok"))
                wait(dv, dv_r, g.n, "cm")
                v.tensor_tensor(px[:, :, C_B], rm[:, :], rs["Q"][:, :], ALU.mult
                                ).then_inc(*dv_r.done("B"))

            def choose(g):
                wait(dv, pe_r, g.n, "aff")
                v.tensor_copy(aff[:, :, :].rearrange("p j e -> p (j e)"), BANK["affinities"][:, 0:J * E]
                              ).then_inc(*dv_r.done("aff"))
                wait(dv, ac_r, g.n - 1, "ea")
                wait(dv, dv_r, g.n, "aff", alone=True)
                for j in range(J):
                    v.max(mx8[:, j, :], aff[:, j, :]).then_inc(*dv_r.done(f"g{j}"))
                wait(dv, dv_r, g.n, "g1", alone=True)
                for j in range(J):
                    v.max_index(ix8[:, j, :], mx8[:, j, :], aff[:, j, :]).then_inc(*dv_r.done(f"i{j}"))
                wait(dv, dv_r, g.n, "i1")
                wait(dv, dv_r, g.n - 1, "s2")
                v.tensor_copy(idf[:, :], ix8[:, :, 0]).then_inc(*dv_r.done("idf"))
                wait(dv, dv_r, g.n, "idf")
                v.tensor_scalar(idf[:, :], idf[:, :], float(E - 1), None, ALU.min
                                ).then_inc(*dv_r.done("idm"))
                wait(dv, dv_r, g.n, "idm")
                wait(dv, dv_r, g.n - 1, "pr")
                for j in range(J):
                    v.tensor_scalar(ohb[:, j, :], iota8, idf[:, j:j + 1], None, ALU.is_equal
                                    ).then_inc(*dv_r.done(f"o{j}"))

            def alpha(g):
                wait(dv, ac_r, g.n, "ea")
                v.tensor_scalar(ea1[:, :], ea[:, :], 1.0, None, ALU.add).then_inc(*dv_r.done("al1"))
                wait(dv, dv_r, g.n, "al1")
                v.reciprocal(pay[g.par][:, :, C_AL], ea1[:, :]).then_inc(*dv_r.done("al"))

            def place(g):
                bank_ = BANK["ranks"]
                wait(dv, pe_r, g.n, "rank")
                wait(dv, dv_r, g.n - 1, "nx")
                v.tensor_tensor(cnt[:, 1, :], cnt[:, 0, :], bank_[:, 16:16 + E], ALU.add
                                ).then_inc(*dv_r.done("c1"))
                wait(dv, dv_r, g.n, "c1")
                v.tensor_tensor(rk[:, :, :], bank_[:, 0:J * E].rearrange("p (j e) -> p j e", j=J),
                                cnt[:, :, :], ALU.add).then_inc(*dv_r.done("rk"))
                wait(dv, dv_r, g.n, "rk")
                v.tensor_tensor(cnt[:, 0, :], cnt[:, 1, :], bank_[:, 16 + E:16 + 2 * E], ALU.add
                                ).then_inc(*dv_r.done("tot"))
                v.tensor_tensor(rk[:, :, :], rk[:, :, :], ohb[:, :, :], ALU.mult
                                ).then_inc(*dv_r.done("pr"))
                wait(dv, dv_r, g.n, "pr")
                v.tensor_reduce(slf[:, :], rk[:, :, :], AX.X, ALU.add).then_inc(*dv_r.done("sl"))
                v.tensor_copy(cnt[:, 1, :], cnt[:, 0, :]).then_inc(*dv_r.done("nx"))
                wait(dv, dv_r, g.n, "sl")
                v.scalar_tensor_tensor(slf[:, :], idf[:, :], float(CAP), slf[:, :], ALU.mult, ALU.add
                                       ).then_inc(*dv_r.done("s2"))
                wait_dma(dv, d_s, g.back(2), J)
                wait(dv, dv_r, g.n, "s2")
                v.tensor_copy(sli[g.par][:, :], slf[:, :]).then_inc(*dv_r.done("si"))

            def one(g):
                stage(g, 2, weighted_turned)
                stage(g, 2, divide)
                stage(g, 0, stats_x)
                stage(g, 1, q_by_head)
                stage(g, 2, x1_sum)
                stage(g, 4, row_scalars)
                stage(g, 4, choose)
                stage(g, 0, rotate_q)
                stage(g, 0, rotate_k)
                stage(g, 1, cross_keys_values)
                stage(g, 3, stats_x2)
                stage(g, 4, place)
                stage(g, 4, alpha)
                stage(g, 0, row_max, 0)
                stage(g, 1, own_head)
                stage(g, 3, norm_x2)
                stage(g, 0, row_max, 1)
                stage(g, 0, row_max, 2)
                stage(g, 0, row_max, 3)
                stage(g, 0, max_parts)
                stage(g, 3, stats_norm)
                stage(g, 2, y_sum)

            for i in range(2):
                v.memset(qst[i][:, :, :].bitcast(FP32), 0.0)
                v.memset(qz[i][:, :, :].bitcast(FP32), 0.0)
                v.memset(vau[i][:, :, :, :], 0.0)
                v.memset(pay[i][:, :, :], 0.0)
            v.memset(khi[:, :, :].bitcast(FP32), 0.0)
            v.memset(klo[:, :, :].bitcast(FP32), 0.0)
            v.memset(cnt[:, :, :], 0.0)
            v.memset(ones_b[:, :], 1.0).then_inc(s_zero, 1)
            dv.wait_ge(s_zero, 1)
            dv.wait_ge(d_const, 16 * N_CONST)
            for i in range(2):
                for b in range(2):
                    v.memset(vau[i][64 * b:64 * b + 64, :, :, 16 * b + HD:16 * b + HD + 1], 1.0)
            v.tensor_copy(tokid[:, :], tok0)
            v.tensor_copy(negq_b[:, :], nqf[:, :])
            v.tensor_copy(negk_b[:, :], nkf[:, :])
            v.tensor_copy(ident_b[:, :], identf)
            v.tensor_copy(tri_b[:, :], trif).then_inc(s_vec, 1)
            v.tensor_copy(bvx[:, :], bc[:, 5:6].broadcast_to((P, P))).then_inc(s_vec, 1)
            dv.wait_ge(s_pe, 1)
            v.tensor_tensor(BO, M[0][:, 0:D], BO, ALU.add).then_inc(s_vec, 1)
            dv.wait_ge(s_vec, 3)
            v.tensor_reduce(pen[:, :], mk[:, :, :], AX.X, ALU.max).then_inc(s_mask, 1)
            dv.wait_ge(s_mask, 1)
            v.tensor_scalar(pen[:, :], pen[:, :], -3.0e38, 1.0e38, ALU.mult, ALU.mult).then_inc(s_mask, 1)
            dv.wait_ge(s_mask, 2)
            v.tensor_scalar(pen[:, :], pen[:, :], 0.0, None, ALU.mult).then_inc(s_mask, 1)
            dv.wait_ge(s_pe, 2)
            v.tensor_tensor(b1[:, :, :].rearrange("p e c -> p (e c)"), M[1][:, 0:E * FC],
                            b1[:, :, :].rearrange("p e c -> p (e c)"), ALU.add).then_inc(s_vec, 1)
            dv.wait_ge(s_vec, 4)
            dv.wait_ge(s_mask, 3)
            dv.wait_ge(s_pool, 1)

            rounds(nc.vector, one)

            cs = [0]

            def link(ins):
                cs[0] += 1
                ins.then_inc(s_chain, 1)
                dv.wait_ge(s_chain, cs[0])

            wait(dv, dv_r, NG - 1, "nx")
            link(v.tensor_scalar(nbf[:, :], cnt[:, 0, :], float(P - 1), None, ALU.add))
            link(v.tensor_copy(ti[:, :], nbf[:, :]))
            link(v.tensor_scalar(ti[:, :], ti[:, :], 7, None, ALU.logical_shift_right))
            link(v.tensor_copy(nbf[:, :], ti[:, :]))
            link(v.tensor_copy(cum[:, :], nbf[:, :]))
            for e in range(1, E):
                link(v.tensor_tensor(cum[:, e:e + 1], cum[:, e - 1:e], cum[:, e:e + 1], ALU.add))
            link(v.tensor_tensor(geb[:, :, :], blkno.unsqueeze(2).broadcast_to((P, NBLK, E)),
                                 cum[:, :].unsqueeze(1).broadcast_to((P, NBLK, E)), ALU.is_ge))
            link(v.tensor_tensor(gnb[:, :, :], geb[:, :, :],
                                 nbf[:, :].unsqueeze(1).broadcast_to((P, NBLK, E)), ALU.mult))
            link(v.tensor_reduce(bex[:, :], geb[:, :, :], AX.X, ALU.add))
            link(v.tensor_reduce(bst[:, :], gnb[:, :, :], AX.X, ALU.add))
            link(v.tensor_tensor(bst[:, :], blkno, bst[:, :], ALU.subtract))
            link(v.tensor_scalar(bst[:, :], bst[:, :], float(P), None, ALU.mult))
            link(v.scalar_tensor_tensor(bst[:, :], bex[:, :], float(CAP), bst[:, :], ALU.mult, ALU.add))
            link(v.tensor_scalar(btf[:, 1, :], bst[:, :], float(E * CAP), None, ALU.min))
            link(v.tensor_scalar(btf[:, 0, :], bex[:, :], float(E - 1), None, ALU.min))
            link(v.tensor_copy(bti[:, :, :], btf[:, :, :]))
            link(v.scalar_tensor_tensor(prf[:, :], iota8, float(CAP), cnt[:, 0, :], ALU.mult, ALU.add))
            v.tensor_copy(pri[:, :], prf[:, :]).then_inc(s_tab, 1)

            def rows_in(b):
                q = b.c % 4
                wait_rows(dv, b)
                wait_b(dv, "pe_xT", b.n - 2)
                v.tensor_scalar(xh[b.c % 2][:, :], rb[q][:, 0:D], rb[q][:, C_A:C_A + 1],
                                rb[q][:, C_B:C_B + 1], ALU.mult, ALU.add
                                ).then_inc(*ffn["dve_xh"].done("dve_xh"))

            def hidden(b):
                u = b.c % 2
                wait_b(dv, "pe_h", b.n)
                wait_b(dv, "pe_hT", b.n - 2)
                v.tensor_copy(hs[u][:, :], B1[u][:, :]).then_inc(*ffn["dve_h"].done("dve_h"))

            def finish(b, e):
                u, q = b.c % 2, b.c % 4
                wait_b(dv, "pe_y", b.n)
                v.tensor_tensor(yb[u][:, :], [M[2], BO_][u][:, 0:D], b2[:, bass.ds(e, 1), :], ALU.add
                                ).then_inc(*ffn["dve_yb"].done("dve_yb"))
                wait_b(dv, "dve_yb", b.n)
                wait_b(dv, "pool_base", b.n)
                wait_out(dv, b)
                v.scalar_tensor_tensor(yo[u][:, :], yb[u][:, :], rb[q][:, C_AL:C_AL + 1], bs[q][:, :],
                                       ALU.mult, ALU.add).then_inc(*ffn["dve_yo"].done("dve_yo"))

            def step(b):
                if b.it is not None or b.c + 2 < NBLK:
                    rows_in(b.on(2))
                e = nc.vector.value_load(bti[0:1, 0, bass.ds(b.n, 1)], min_val=0, max_val=E - 1)
                if b.it is not None or b.c + 1 < NBLK:
                    hidden(b.on(1))
                finish(b, e)

            rows_in(Block(0))
            rows_in(Block(1))
            hidden(Block(0))
            for c in range(4):
                step(Block(c))
            with nc.vector.Fori(1, NBLK // 4 - 1) as it:
                for u in range(4):
                    step(Block(u, it, 4))
            for c in range(NBLK - 4, NBLK):
                step(Block(c))

        @block.gpsimd
        def _(po):
            v = nc.gpsimd

            def inv_std(stage, n, key, tail=""):
                v.tensor_scalar(ve[key][:, :], mv[key][:, :, 1], EPS, None, ALU.add
                                ).then_inc(*stage.done("eps" + tail))
                wait(po, stage, n, "eps" + tail)
                v.tensor_tensor(rs[key][:, :], ve[key][:, :], half[:, :], ALU.pow
                                ).then_inc(*stage.done("pow" + tail))

            def offset(stage, n, key, tail=""):
                wait(po, stage, n, "pow" + tail)
                v.tensor_tensor(nb[key][:, :], mv[key][:, :, 0], rs[key][:, :], ALU.mult
                                ).then_inc(*stage.done("mr" + tail))
                wait(po, stage, n, "mr" + tail)
                v.tensor_scalar(nb[key][:, :], nb[key][:, :], -1.0, None, ALU.mult
                                ).then_inc(*stage.done("nb" + tail))

            def std_x(g):
                wait(po, dv_l, g.n, "a1")
                wait(po, ac_l, g.n - 1, "n")
                inv_std(po_l, g.n, "L")
                offset(po_l, g.n, "L")

            def q_sum(g):
                wait(po, dv_f, g.n, "q2")
                wait(po, po_f, g.n - 1, "qlo")
                wait(po, ac_f, g.n - 1, "z1")
                wait(po, ac_f, g.n - 1, "qhi")
                v.tensor_tensor(qf[:, :], t1[0][:, :], t2[0][:, :], ALU.add).then_inc(*po_f.done("qf"))

            def q_low(g):
                wait(po, ac_f, g.n, "qhi")
                wait_dma(po, d_q, g.back(1), 12)
                v.tensor_tensor(qlo[:, :], qf[:, :], qhi[:, :].bitcast(FP32), ALU.subtract
                                ).then_inc(*po_f.done("qlo"))

            def k_sum(g):
                wait(po, dv_f, g.n, "k2")
                wait(po, po_f, g.n - 1, "klo")
                wait(po, ac_f, g.n - 1, "x3")
                wait(po, ac_f, g.n - 1, "khi")
                v.tensor_tensor(kf[:, :], t1[1][:, :], t2[1][:, :], ALU.add).then_inc(*po_f.done("kf"))

            def k_low(g):
                wait(po, ac_f, g.n, "khi")
                wait_dma(po, d_k, g.back(1), 12)
                kl = klo[:, :, :].rearrange("p (j b) (c k) -> p j b c k", b=2, c=2)
                kh = khi[:, :, :].bitcast(FP32).rearrange("p (j b) (c k) -> p j b c k", b=2, c=2)
                kv = kf[:, :].rearrange("p (j b k) -> p j b k", j=J, b=2)
                for b in range(2):
                    last = v.tensor_tensor(kl[:, :, b, b, :], kv[:, :, b, :], kh[:, :, b, b, :], ALU.subtract)
                last.then_inc(*po_f.done("klo"))

            def x_bias(g):
                wait_dma(po, d_xr, g)
                v.tensor_tensor(xr[g.par][:, :, :], xr[g.par][:, :, :],
                                BO.unsqueeze(1).broadcast_to((P, J, D)), ALU.add
                                ).then_inc(*po_t.done("xb"))

            def std_x1(g):
                wait(po, dv_t, g.n, "a1")
                wait(po, ac_t, g.n - 1, "n")
                inv_std(po_t, g.n, "T")
                offset(po_t, g.n, "T")

            def sum_biases(g):
                wait(po, pe_t, g.n, "xT")
                wait(po, ac_t, g.n, "n")
                v.tensor_tensor(xn1[:, :, :], xn1[:, :, :], BO2.unsqueeze(1).broadcast_to((P, J, D)),
                                ALU.add).then_inc(*po_t.done("xnb"))
                v.tensor_tensor(x1[g.par][:, :, :], x1[g.par][:, :, :],
                                LNB.unsqueeze(1).broadcast_to((P, J, D)), ALU.add).then_inc(*po_t.done("x1b"))

            def std_y(g):
                wait(po, dv_t, g.n, "d1")
                wait(po, ac_t, g.n - 1, "z")
                inv_std(po_t, g.n, "U", "2")
                offset(po_t, g.n, "U", "2")

            def gain(g):
                wait(po, ac_t, g.n, "z")
                v.tensor_tensor(yn[:, :, :], yn[:, :, :], LNG.unsqueeze(1).broadcast_to((P, J, D)),
                                ALU.mult).then_inc(*po_t.done("zg"))

            def x2_sum(g):
                wait(po, po_t, g.n, "zg")
                wait(po, po_t, g.n, "x1b")
                wait_dma(po, d_s, g.back(2), J)
                v.tensor_tensor(pay[g.par][:, :, 0:D], yn[:, :, :], x1[g.par][:, :, :], ALU.add
                                ).then_inc(*po_t.done("x2"))

            def std_x2(g):
                wait(po, dv_r, g.n, "a1")
                wait(po, dv_r, g.n - 1, "R")
                wait(po, dv_r, g.n - 1, "p1")
                inv_std(po_r, g.n, "R")

            def std_norm(g):
                wait(po, dv_r, g.n, "e1")
                wait(po, dv_r, g.n - 1, "B")
                inv_std(po_r, g.n, "Q", "2")

            def scatter_rows(g):
                wait(po, dv_r, g.n, "B")
                wait(po, dv_r, g.n, "al")
                wait(po, dv_r, g.n, "si")
                for j in range(J):
                    v.indirect_dma_start(
                        out=rows, out_offset=bass.IndirectOffsetOnAxis(ap=sli[g.par][:, j:j + 1], axis=0),
                        in_=pay[g.par][:, j, :], in_offset=None).then_inc(d_s[g.par], 16)

            def one(g):
                stage(g, 3, std_y)
                stage(g, 0, std_x)
                stage(g, 1, x_bias)
                stage(g, 2, std_x1)
                stage(g, 3, gain)
                stage(g, 3, x2_sum)
                stage(g, 0, q_sum)
                stage(g, 0, k_sum)
                stage(g, 0, q_low)
                stage(g, 2, sum_biases)
                stage(g, 3, std_x2)
                stage(g, 4, scatter_rows)
                stage(g, 0, k_low)
                stage(g, 3, std_norm)

            v.memset(half[:, :], -0.5)
            for i in range(2):
                v.memset(kst[i][:, :, :, :].bitcast(FP32), 0.0)
            v.memset(k2[:, :, :, :], 0.0).then_inc(s_pz, 1)
            po.wait_ge(s_pz, 1)
            for i in range(2):
                kd = kst[i][96:104, :, :, :].bitcast(FP32).rearrange("p r (j b) (c k) -> p r j b c k", b=2, c=2)
                for r_ in range(4):
                    for b in range(2):
                        last = v.memset(kd[:, r_, :, b, b, :], 1.0)
            last.then_inc(s_pool, 1)
            po.wait_ge(s_pool, 1)
            po.wait_ge(d_weights, 32)
            po.wait_ge(d_const, 16 * N_CONST)
            po.wait_ge(s_pe, 2)
            for e in range(E):
                last = v.tensor_scalar(w1[:, e, :], w1[:, e, :], gb[:, 0, e:e + 1], None, ALU.mult)
            last.then_inc(s_pool, 1)
            po.wait_ge(s_vec, 4)

            rounds(nc.gpsimd, one)

            def step(b):
                u, q = b.c % 2, b.c % 4
                wait_rows(po, b)
                wait_b(po, "dve_yo", b.n - 4)
                v.tensor_scalar(bs[q][:, :], rb[q][:, 0:D], rb[q][:, C_R:C_R + 1], rb[q][:, C_C:C_C + 1],
                                ALU.mult, ALU.add).then_inc(*ffn["pool_base"].done("pool_base"))
                wait_out(po, b)
                v.tensor_copy(idi[u][:, :], rb[q][:, C_ID:C_ID + 1]).then_inc(*ffn["pool_id"].done("pool_id"))

            def scatter(b):
                u = b.c % 2
                wait_b(po, "pool_id", b.n)
                wait_b(po, "dve_yo", b.n)
                v.indirect_dma_start(
                    out=o_rows, out_offset=bass.IndirectOffsetOnAxis(ap=idi[u][:, 0:1], axis=0),
                    in_=yo[u][:, :], in_offset=None, bounds_check=T - 1, oob_is_err=False
                ).then_inc(d_o[u], 16)

            step(Block(0))
            for c in range(4):
                step(Block(c + 1))
                scatter(Block(c))
            with nc.gpsimd.Fori(1, NBLK // 4 - 1) as it:
                for u in range(4):
                    step(Block(u + 1, it, 4))
                    scatter(Block(u, it, 4))
            for c in range(NBLK - 4, NBLK):
                if c + 1 < NBLK:
                    step(Block(c + 1))
                scatter(Block(c))


def _constants(nb):
    t = nb * SQ
    p = np.arange(P)
    half = HD // 2
    inv = (1.0 / np.float32(10000.0) ** (np.arange(half, dtype=np.float32) / half)).astype(np.float32)
    ang = np.outer(np.arange(SQ, dtype=np.float32), inv).astype(np.float32)
    cos = np.cos(ang).T[p % half]
    sin = np.sin(ang).T[p % half] * np.where(p % HD < half, -1.0, 1.0)[:, None]
    scale = 1.0 / np.sqrt(np.float64(HD))
    dk = float(np.float32(np.sqrt(np.float16(HD))) + np.float32(1e-8))
    own = (p[:, None] // HD == p[None, :] // HD) / dk
    own4 = (p[:, None] % 32) // HD == np.arange(4)
    own4s = np.where(p[:, None] < 96, own4, p[:, None] % 4 == np.arange(4))
    nblk = t // P + E
    rep = lambda a: np.broadcast_to(a, (P, len(a)))
    cols = [cos * scale, sin * scale, cos, sin, own, np.eye(P), own4, own4s, rep(np.arange(E)),
            p[:, None] + P * np.arange(J), p[:, None] < p[None, :], rep(np.arange(nblk))]
    consts = np.concatenate([np.asarray(c, np.float32) for c in cols], axis=1)
    q = p % SQ
    later = np.arange(SQ)[None, :] > q[:, None]
    negq = np.tile(np.where(later, NEG, 0.0), (1, 8)).astype(np.float32)
    earlier = np.arange(SQ)[None, :] < q[:, None]
    negk = np.tile(np.where(earlier, NEG, 0.0), (1, 8)).astype(np.float32)
    pad = np.zeros((P, ROW), np.float32)
    pad[:, C_ID] = t + p
    return consts, negq, negk, pad


def kernel(x, ctx_1024, mask_Bx1xSxS2_bf0, L0_attn_qkv_w, L0_attn_qkv_b, L0_attn_out_w, L0_attn_out_b,
           L0_xattn_wq_w, L0_xattn_wq_b, L0_xattn_wk_w, L0_xattn_wk_b, L0_xattn_wv_w, L0_xattn_wv_b,
           L0_xattn_wo_w, L0_xattn_wo_b, L0_xattn_ln_g, L0_xattn_ln_b, L0_ffn_centroids, L0_ffn_ln_g,
           L0_ffn_ln_b, L0_ffn_w1, L0_ffn_b1, L0_ffn_w2, L0_ffn_b2):
    import concourse.bacc as bacc
    from concourse.bass_utils import run_bass_kernel_spmd

    a = lambda v: np.asarray(v)
    qkv, qb = a(L0_attn_qkv_w), a(L0_attn_qkv_b)
    partner = np.arange(D) ^ (HD // 2)
    wq, wk, wv = qkv[:D], qkv[D:2 * D], qkv[2 * D:]
    bq, bk, bv = qb[:D], qb[D:2 * D], qb[2 * D:]
    wself = np.stack([w.T for w in (wq, wq[partner], wk, wk[partner], wv, a(L0_attn_out_w))], axis=1)
    wcross = np.stack([a(w).T for w in (L0_xattn_wq_w, L0_xattn_wk_w, L0_xattn_wv_w, L0_xattn_wo_w)], axis=1)
    bcol = np.stack([bq, bq[partner], bk, bk[partner], a(L0_xattn_wq_b), bv], axis=1)
    brow = np.concatenate([a(L0_attn_out_b), a(L0_xattn_wo_b), a(L0_xattn_ln_g), a(L0_xattn_ln_b),
                           a(L0_xattn_wk_b), a(L0_xattn_wv_b)])
    consts, negq, negk, pad = _constants(x.shape[0])
    arrays = {
        "x": a(x), "ctx": a(ctx_1024), "mask": a(mask_Bx1xSxS2_bf0).view(np.int32),
        "wself": wself, "wcross": wcross, "bcol": bcol, "brow": brow,
        "cent": a(L0_ffn_centroids).T,
        "w1t": a(L0_ffn_w1).transpose(2, 0, 1),
        "lngb": np.stack([a(L0_ffn_ln_g).T, a(L0_ffn_ln_b).T], axis=1),
        "b1c": a(L0_ffn_b1).reshape(E, FC, P).transpose(2, 0, 1),
        "w2t": a(L0_ffn_w2).reshape(E, D, FC, P).transpose(3, 0, 2, 1),
        "b2r": a(L0_ffn_b2).reshape(-1),
        "consts": consts, "negq": negq, "negk": negk, "padc": pad,
    }
    arrays = {f"in_{n}": np.ascontiguousarray(v) for n, v in arrays.items()}
    nc = bacc.Bacc("TRN2", target_bir_lowering=False, num_devices=1)
    args = [nc.dram_tensor(n, v.shape, mybir.dt.from_np(v.dtype), kind="ExternalInput").ap()
            for n, v in arrays.items()]
    args.append(nc.dram_tensor("out", x.shape, FP32, kind="ExternalOutput").ap())
    decoder_kernel(nc, *args)
    r = run_bass_kernel_spmd(nc, [arrays], core_ids=[0])
    return r.results[0]["out"]
```

```python
from contextlib import ExitStack

import numpy as np

import concourse.bass as bass
from concourse import mybir

FP32 = mybir.dt.float32
F32R = mybir.dt.float32r
BF16 = mybir.dt.bfloat16
I32 = mybir.dt.int32
U32 = mybir.dt.uint32
ALU = mybir.AluOpType
ACT = mybir.ActivationFunctionType
AX = mybir.AxisListType

P = 128
D = 128
H, HD = 16, 8
SQ = 64
J = 2
TG = J * P
E, F = 8, 512
FC = F // P
EPS = 1e-5
NEG = -1.0e30
RB = 8
ROW = 136
C_A, C_B, C_R, C_C, C_AL, C_ID = range(D, D + 6)


class Steps:

    def __init__(self, sem, names, total):
        self.sem, self.names, self.next, self.total = sem, names.split(), 0, total

    def at(self, n, name):
        if isinstance(n, int):
            n = min(n, self.total - 1)
        return n * len(self.names) + (self.names.index(name) + 1)

    def done(self, name):
        assert self.names[self.next] == name, (self.names[self.next], name)
        self.next = (self.next + 1) % len(self.names)
        return self.sem, 1


class Stage:

    def __init__(self, name, pieces, total, sem):
        self.piece = {}
        for p in pieces.split("|"):
            steps = Steps(sem(f"{name}_{p.split()[0]}"), p, total)
            self.piece.update({step: steps for step in p.split()})

    def done(self, name):
        return self.piece[name].done(name)


class Group:

    def __init__(self, c, it=None):
        self.c, self.it = c, it
        self.n = c if it is None else it * 2 + c
        self.half = c // 2 if it is None else it + c // 2
        self.par = c % 2

    def back(self, k):
        return Group(self.c - k, self.it)

    def within(self, total):
        return self.it is not None or 0 <= self.c < total


class Block:

    def __init__(self, c, it=None, step=0):
        self.c, self.it, self.step = c, it, step
        self.n = c if it is None else it * step + c
        self.half = c // 2 if it is None else it * (step // 2) + c // 2
        self.quarter = c // 4 if it is None else it * (step // 4) + c // 4
        self.turn = c // RB if it is None or step < RB else it * (step // RB) + c // RB

    def within(self, total):
        return self.it is not None or 0 <= self.c < total

    def on(self, k):
        return Block(self.c + k, self.it, self.step)


class Waits:

    passed = None


def wait_for(eng, sem, v, alone=False):
    if not isinstance(v, int):
        eng.wait_ge(sem, v)
        if alone or eng.engine in (mybir.EngineType.Pool, mybir.EngineType.SP):
            eng.sem_inc(Waits.passed, 1)
    elif v > 0:
        eng.wait_ge(sem, v)


def wait(eng, steps, n, name, alone=False):
    if isinstance(steps, Stage):
        steps = steps.piece[name]
    wait_for(eng, steps.sem, steps.at(n, name), alone)


def wait_dma(eng, sems, g, count=1):
    wait_for(eng, sems[g.par], (g.half + 1) * (16 * count))


def decoder_kernel(nc, x, ctx, mask, wself, wcross, bcol, brow, cent, w1t, lngb, b1c, w2t, b2r,
                   consts, negq, negk, padc, out):
    NB = x.shape[0]
    T = NB * SQ
    NT = T // P
    NG = NT // J
    CAP = T + P
    NBLK = NT + E
    x_rows = x.rearrange("b s d -> (b s) d")
    c_rows = ctx.rearrange("b s d -> (b s) d")
    o_rows = out.rearrange("b s d -> (b s) d")
    m_rows = mask.rearrange("b o s k -> (b o s) k").rearrange("(t p) k -> p t k", p=P)
    rows = nc.dram_tensor("expert_rows", [E * CAP + P, ROW], FP32, kind="Internal").ap()

    es = ExitStack()
    with es:
        def sb(name, shape, dt=FP32):
            return es.enter_context(nc.sbuf_tensor(name, shape, dt))

        def two(name, shape, dt=FP32):
            return [sb(f"{name}_{i}", shape, dt) for i in range(2)]

        def sem(name):
            return es.enter_context(nc.semaphore(name))

        ws = sb("ws", [P, 6, D])
        WQ, WQR, WK, WKR, WV, WO = (ws[:, i, :] for i in range(6))
        wc = sb("wc", [P, 4, D])
        bc = sb("bc", [P, 6])
        br = sb("br", [P, 6, D])
        BO, BO2, LNG, LNB = (br[:, i, :] for i in range(4))
        cT = sb("cT", [P, E])
        cf = sb("cf", [P, 4 * SQ + D + P + 4 + 4 + E + NT + P + NBLK])
        o = 0
        rope = [cf[:, i * SQ:(i + 1) * SQ] for i in range(4)]
        o += 4 * SQ
        headmask = cf[:, o:o + D]
        o += D
        identf = cf[:, o:o + P]
        o += P
        own4, own4s = cf[:, o:o + 4], cf[:, o + 4:o + 8]
        o += 8
        iota8 = cf[:, o:o + E]
        o += E
        tokid = cf[:, o:o + NT]
        o += NT
        trif = cf[:, o:o + P]
        o += P
        blkno = cf[:, o:o + NBLK]
        nqf = sb("nqf", [P, SQ])
        nkf = sb("nkf", [P, SQ])
        negq_b = sb("negq_b", [P, 512], BF16)
        negk_b = sb("negk_b", [P, 512], BF16)
        ident_b = sb("ident_b", [P, P], BF16)
        tri_b = sb("tri_b", [P, P], BF16)
        ones_b = sb("ones_b", [P, P], BF16)
        bkv = sb("bkv", [P, 2 * D], BF16)
        part = [sb(f"part{i}", [P, 2 * D], BF16) for i in range(3)]
        rest = [sb(f"rest{i}", [P, 2 * D]) for i in range(2)]
        half = sb("half", [P, J])
        bvx = sb("bvx", [P, P])
        w1 = sb("w1", [P, E, F])
        w2 = sb("w2", [P, E, FC, D])
        gb = sb("gb", [P, 2, E])
        b1 = sb("b1", [P, E, FC])
        b2 = sb("b2", [P, E, D])
        mk = sb("mk", [P, NT, SQ // 4], I32)
        pen = sb("pen", [P, NT])
        xin = two("xin", [P, J, D])
        xn = two("xn", [P, J, D])
        xT = sb("xT", [P, TG])
        t1 = two("t1_", [P, TG])
        t2 = two("t2_", [P, TG])
        qf = sb("qf", [P, TG])
        kf = sb("kf", [P, TG])
        qhi = sb("qhi", [P, TG], F32R)
        qlo = sb("qlo", [P, TG], F32R)
        khi = sb("khi", [P, 2 * J, P], F32R)
        klo = sb("klo", [P, 2 * J, P], F32R)
        qst = two("qst", [P, 4, TG], F32R)
        qex = sb("qex", [P, 4, 4, TG], F32R)
        kst = two("kst", [P, 4, 2 * J, P], F32R)
        qz = two("qz", [P, 2 * J, P], F32R)
        kex = two("kex", [P, 4, TG], F32R)
        vau = two("vau", [P, J, H, 32])
        mx = sb("mx", [P, J, H])
        mt = sb("mt", [P, J, 4, 2, 4], BF16)
        prob = two("prob", [P, 512])
        ot = sb("ot", [P, J, 4, 2, 2, 16])
        rd = sb("rd", [P, J, 4, 2, 2])
        on = sb("on", [P, J, 2, 2, 4, HD])
        ont = two("ont", [P, J, 2, 2, 32])
        xr = two("xr", [P, J, D])
        cin = two("cin", [P, J, D])
        cxT = sb("cxT", [P, TG])
        x1 = two("x1", [P, J, D])
        xn1 = sb("xn1", [P, J, D])
        xT1 = sb("xT1", [P, TG])
        q2 = sb("q2", [P, TG])
        k2 = sb("k2", [P, J, 2, D])
        v2 = sb("v2", [P, J, D])
        mt2 = sb("mt2", [P, J, 2, D])
        r2s = two("r2s", [P, J, 2, D])
        y1 = sb("y1", [P, J, D])
        yn = sb("yn", [P, J, D])
        pay = two("pay", [P, J, ROW])
        xp = sb("xp", [P, J, D])
        xpT = sb("xpT", [P, TG])
        stat = {s: sb(f"stat_{s}", [P, J, 6]) for s in "LTURQ"}
        mv = {s: sb(f"mv_{s}", [P, J, 2]) for s in "LTURQ"}
        ve = {s: sb(f"ve_{s}", [P, J]) for s in "LTURQ"}
        rs = {s: sb(f"rs_{s}", [P, J]) for s in "LTURQ"}
        nb = {s: sb(f"nb_{s}", [P, J]) for s in "LTU"}
        rc = sb("rc", [P, J])
        rm = sb("rm", [P, J])
        mx8 = sb("mx8", [P, J, 8])
        ix8 = sb("ix8", [P, J, 8], U32)
        idf = sb("idf", [P, J])
        ohb = sb("ohb", [P, J, E], BF16)
        ea = sb("ea", [P, J])
        ea1 = sb("ea1", [P, J])
        cnt = sb("cnt", [P, E])
        rk = sb("rk", [P, J, E])
        slf = sb("slf", [P, J])
        sli = two("sli", [P, J], I32)
        ti = sb("ti", [P, E], I32)
        nbf = sb("nbf", [P, E])
        cum = sb("cum", [P, E])
        geb = sb("geb", [P, NBLK, E])
        gnb = sb("gnb", [P, NBLK, E])
        bex = sb("bex", [P, NBLK])
        bst = sb("bst", [P, NBLK])
        btf = sb("btf", [P, 2, NBLK])
        bti = sb("bti", [P, 2, NBLK], I32)
        pri = sb("pri", [P, E], I32)
        padt = sb("padt", [P, ROW])
        rb = [sb(f"rb{i}", [P, ROW]) for i in range(RB)]
        idi = [sb(f"idi{i}", [P, 1], I32) for i in range(4)]
        xh = two("xh", [P, D])
        bs = [sb(f"bs{i}", [P, D]) for i in range(RB)]
        xhT = two("xhT", [P, P])
        hs = two("hs", [P, F])
        hT = two("hT", [P, FC, P])
        yb = two("yb", [P, D])
        yo = [sb(f"yo{i}", [P, D]) for i in range(4)]

        bank = [es.enter_context(nc.psum_tensor(f"bank{i}", [P, 512], FP32)) for i in range(8)]
        M, B1 = bank[0:3], bank[3:5]
        HT = [[M[2], bank[5]], [bank[6], bank[7]]]

        def stage_steps(name, pieces):
            return Stage(name, pieces, NG, sem)

        pe_f = stage_steps("pe_front", "xT | QQ | KK | V")
        pe_s = stage_steps("pe_scores_for_max", "s0 | s1 | s2 | s3 | m0 m1")
        pe_a = stage_steps("pe_attention", "s0 | s1 | s2 | s3 | p0 | p1 | p2 | p3")
        pe_t = stage_steps("pe_cross", "cT | out | KV | xT | gram | Q2 | R | o2")
        pe_r = stage_steps("pe_route", "xT | aff | rank")
        ac_l = stage_steps("act_norm_x", "n")
        ac_f = stage_steps("act_front", "xT | V0 V1 | qhi | z0 z1 | khi | x0 x1 x2 x3")
        ac_s = stage_steps("act_maxima", "m0 m1 | e1 e2 e3")
        ac_a = stage_steps("act_exp", "e0 | e1 | e2 | e3")
        ac_t = stage_steps("act_cross", "cT | k0 k1 v | n | xT | Q2 | R | z")
        ac_r = stage_steps("act_route", "xT | id ea")
        dv_l = stage_steps("dve_norm_x", "b0 b1 a0 a1")
        dv_f = stage_steps("dve_front", "q1 q2 | k1 k2")
        dv_s = stage_steps("dve_maxima", "m0 | m1 | m2 | m3 | hi lo | e0")
        dv_a = stage_steps("dve_attention", "ot | rd n0 n1 n2 n3 tr")
        dv_t = stage_steps("dve_cross", "x1 b0 b1 a0 a1 | mt | y0 y1 c0 c1 d0 d1")
        dv_r = stage_steps("dve_route", "b0 b1 a0 a1 | c p0 p1 | d0 d1 e0 e1 | cm B | "
                           "g0 g1 i0 i1 idm o0 o1 | al1 al | rk tot pr sl si")
        po_l = stage_steps("pool_norm_x", "eps pow mr nb")
        po_f = stage_steps("pool_front", "qf | qlo | kf | klo")
        po_t = stage_steps("pool_cross", "xb | eps pow mr nb | xnb x1b | eps2 pow2 mr2 nb2 | zg | x2")
        po_r = stage_steps("pool_route", "eps pow | eps2 pow2 | A R C")
        d_x = [sem(f"dma_x{i}") for i in range(2)]
        d_xr = [sem(f"dma_x_again{i}") for i in range(2)]
        d_c = [sem(f"dma_ctx{i}") for i in range(2)]
        d_q = [sem(f"dma_q_stack{i}") for i in range(2)]
        d_k = [sem(f"dma_k_stack{i}") for i in range(2)]
        d_s = [sem(f"dma_scatter{i}") for i in range(2)]
        d_const = sem("dma_constants")
        d_late = sem("dma_late_constants")
        d_mask = sem("dma_mask")
        d_weights = sem("dma_ffn_weights")
        d_pad = sem("dma_pad_rows")
        s_vec = sem("setup_vector")
        s_pool = sem("setup_pool")
        s_pe = sem("setup_tensor")
        s_tab = sem("block_table")
        s_part = sem("setup_bias_parts")
        s_pads = sem("pad_rows_known")
        s_gain = sem("gain_in_weights")
        s_b1 = sem("offset_in_bias")
        s_zero = sem("setup_vector_zeros")
        s_pz = sem("setup_pool_zeros")
        s_mask = sem("setup_mask")
        s_chain = sem("block_table_chain")
        d_rb = [sem(f"dma_rows{i}") for i in range(RB)]
        d_o = [sem(f"dma_out{i}") for i in range(4)]
        ffn = {k: Steps(sem(f"ffn_{k}"), k, NBLK) for k in
               ("pe_xT", "pe_h", "pe_hT", "pe_y", "act_xT", "act_relu", "dve_xh", "dve_h", "dve_relu",
                "dve_yb", "dve_yo", "pool_base", "pool_id")}

        Waits.passed = sem("waits_passed")

        def wait_b(eng, kind, n):
            wait(eng, ffn[kind], n, kind)

        def wait_rows(eng, b):
            wait_for(eng, d_rb[b.c % RB], (b.turn + 1) * 16)

        def wait_out(eng, b):
            wait_for(eng, d_o[b.c % 4], b.quarter * 16)

        block = es.enter_context(nc.Block())

        DEPTH = 5
        FIRST, TOTAL = DEPTH + 2, NG + DEPTH
        QUIET = 2
        LOOPS = (NG - 1 - FIRST) // 2

        def stage(g, back, op, *args):
            if g.back(back).within(NG):
                op(g.back(back), *args)

        def rounds(eng, one, before_last=None, early=None):
            for i in range(FIRST):
                one(Group(i))
                if early:
                    early(i)
            with eng.Fori(0, LOOPS) as it:
                one(Group(FIRST, it))
                one(Group(FIRST + 1, it))
            for i in range(FIRST + 2 * LOOPS, TOTAL + 1):
                if i >= NG + QUIET - 1 and before_last:
                    before_last(i - (NG + QUIET - 1))
                one(Group(i))

        BANK = {
            "x_turned": bank[0],
            "queries": bank[0],
            "values": bank[0],
            "max_scores0": bank[0],
            "max_scores3": bank[0],
            "max_rows0": bank[0],
            "through_output": bank[0],
            "keys": bank[1],
            "max_scores2": bank[1],
            "max_rows1": bank[1],
            "scores3": bank[1],
            "max_scores1": bank[2],
            "ctx_turned": bank[2],
            "values_keys": bank[2],
            "x1_turned": bank[2],
            "x2_turned": bank[2],
            "affinities": bank[2],
            "cross_keys_values": bank[3],
            "scores2": bank[3],
            "cross_queries": bank[3],
            "scores0": bank[4],
            "weighted": bank[4],
            "projected": bank[4],
            "scores1": bank[5],
            "cross_output": bank[6],
            "ranks": bank[6],
        }

        N_CONST, N_LATE, N_WEIGHTS = 8, 4, 8

        @block.sync
        def _(sp):
            for dst, src in ((cf[:, :], consts), (ws[:, :, :], wself), (bc[:, :], bcol), (nqf[:, :], negq),
                             (nkf[:, :], negk), (br[:, :, :].rearrange("p a d -> p (a d)"),
                                                 brow.partition_broadcast(P)),
                             (wc[:, :, :], wcross), (cT[:, :], cent)):
                sp.dma_start(dst, src).then_inc(d_const, 16)

            def late_loads(i):
                if i == 0:
                    for dst, src in ((gb[:, :, :], lngb), (b1[:, :, :], b1c), (padt[:, :], padc)):
                        sp.dma_start(dst, src).then_inc(d_late, 16)
                if i == 1:
                    sp.dma_start(mk[:, :, :], m_rows).then_inc(d_mask, 16)
                if i == 2:
                    sp.dma_start(b2[:, :, :].rearrange("p e d -> p (e d)"),
                                 b2r.partition_broadcast(P)).then_inc(d_late, 16)
                if i < 4:
                    part = slice(i * E // 4, (i + 1) * E // 4)
                    sp.dma_start(w1[:, part, :], w1t[:, part, :]).then_inc(d_weights, 16)
                    sp.dma_start(w2[:, part, :, :], w2t[:, part, :, :]).then_inc(d_weights, 16)

            def load_x(g):
                wait(sp, ac_l, g.n - 2, "n")
                sp.dma_start(xin[g.par][:, :, :],
                             x_rows[bass.ds(g.n * TG, TG), :].rearrange("(j p) d -> p j d", j=J)
                             ).then_inc(d_x[g.par], 16)

            def load_again(g):
                wait(sp, dv_t, g.n - 2, "x1")
                sp.dma_start(xr[g.par][:, :, :],
                             x_rows[bass.ds(g.n * TG, TG), :].rearrange("(j p) d -> p j d", j=J)
                             ).then_inc(d_xr[g.par], 16)
                wait(sp, pe_t, g.n - 2, "cT")
                sp.dma_start(cin[g.par][:, :, :],
                             c_rows[bass.ds(g.n * TG, TG), :].rearrange("(j p) d -> p j d", j=J)
                             ).then_inc(d_c[g.par], 16)

            def stack_q(g):
                if g.it is None and g.n == 0:
                    sp.wait_ge(s_vec, 1)
                    sp.wait_ge(s_pool, 1)
                wait(sp, dv_s, g.n - 2, "e0")
                wait(sp, ac_s, g.n - 2, "e3")
                wait(sp, ac_f, g.n, "qhi")
                wait(sp, po_f, g.n, "qlo")
                for s, src in enumerate((qhi, qhi, qlo)):
                    for r in range(4):
                        sp.dma_start(qst[g.par][32 * s:32 * s + 32, r, :].bitcast(FP32),
                                     src[32 * r:32 * r + 32, :].bitcast(FP32)).then_inc(d_q[g.par], 16)

            def stack_k(g):
                if g.it is None and g.n == 0:
                    sp.wait_ge(s_vec, 1)
                    sp.wait_ge(s_pool, 1)
                wait(sp, pe_a, g.n - 2, "s3")
                wait(sp, ac_f, g.n, "khi")
                wait(sp, po_f, g.n, "klo")
                for s, src in enumerate((khi, klo, khi)):
                    for r in range(4):
                        sp.dma_start(kst[g.par][32 * s:32 * s + 32, r, :, :].bitcast(FP32),
                                     src[32 * r:32 * r + 32, :, :].bitcast(FP32)).then_inc(d_k[g.par], 16)

            def one(g):
                stage(g, 0, load_x)
                stage(g, 1, load_again)
                stage(g, 1, stack_k)
                stage(g, 0, stack_q)

            rounds(nc.sync, one, early=late_loads)

            sp.wait_ge(d_late, 16 * N_LATE)
            sp.dma_start(rows[E * CAP:E * CAP + P, :], padt[:, :]).then_inc(d_pad, 16)
            sp.wait_ge(s_pads, 1)
            for e in range(E // 2):
                at = nc.sync.value_load(pri[0:1, e:e + 1], min_val=0, max_val=(e + 1) * CAP - P)
                sp.dma_start(rows[bass.ds(at, P), :], padt[:, :]).then_inc(d_pad, 16)
            sp.wait_ge(d_pad, 16 * (E + 1))
            sp.wait_ge(s_tab, 1)
            sp.wait_ge(d_s[0], 16 * J * ((NG + 1) // 2))
            sp.wait_ge(d_s[1], 16 * J * (NG // 2))

            def fetch(b):
                wait_b(sp, "pool_id", b.n - RB)
                wait_b(sp, "dve_yo", b.n - RB)
                at = nc.sync.value_load(bti[0:1, 1, bass.ds(b.n, 1)], min_val=0, max_val=E * CAP)
                sp.dma_start(rb[b.c % RB][:, :], rows[bass.ds(at, P), :]).then_inc(d_rb[b.c % RB], 16)

            for c in range(RB):
                fetch(Block(c))
            with nc.sync.Fori(1, NBLK // RB) as it:
                for u in range(RB):
                    fetch(Block(u, it, RB))
            for i in range(4):
                sp.wait_ge(d_o[i], 16 * NBLK // RB)

        @block.tensor
        def _(pe):
            mm, tr = nc.tensor.matmul, nc.tensor.transpose
            pe.wait_ge(d_const, 16 * N_CONST)
            pe.wait_ge(s_vec, 2)
            mm(M[0][:, 0:D], bvx[:, :], WO, start=True, stop=True).then_inc(s_pe, 1)
            BEFORE = {
                "x_turned": [(ac_s, "m0", -1), (ac_t, "R", -2), (dv_s, "m3", -1), (dv_s, "m0", -1),
                    (ac_f, "V1", -1), (dv_f, "q2", -1), (ac_f, "xT", -1)],
                "queries": [(ac_f, "xT", 0), (ac_s, "m0", -1), (ac_t, "R", -2), (dv_s, "m3", -1),
                    (dv_s, "m0", -1), (ac_f, "V1", -1), (dv_f, "q2", -1)],
                "values": [(dv_f, "q2", 0), (ac_f, "xT", 0), (ac_s, "m0", -1), (ac_t, "R", -2),
                    (dv_s, "m3", -1), (dv_s, "m0", -1), (ac_f, "V1", -1)],
                "max_scores0": [(ac_f, "V1", 0), (dv_f, "q2", 0), (ac_f, "xT", 0), (ac_s, "m0", -1),
                    (ac_t, "R", -2), (dv_s, "m3", -1), (dv_s, "m0", -1)],
                "max_scores3": [(dv_s, "m0", 0), (ac_f, "V1", 0), (dv_f, "q2", 0), (ac_f, "xT", 0),
                    (ac_s, "m0", -1), (ac_t, "R", -2), (dv_s, "m3", -1)],
                "max_rows0": [(ac_t, "R", -1), (dv_s, "m3", 0), (dv_s, "m0", 0), (ac_f, "V1", 0),
                    (dv_f, "q2", 0), (ac_f, "xT", 0), (ac_s, "m0", -1)],
                "through_output": [(dv_s, "m3", 1), (dv_s, "m0", 1), (ac_f, "V1", 1), (dv_f, "q2", 1),
                    (ac_f, "xT", 1), (ac_s, "m0", 0), (ac_t, "R", -1)],
                "keys": [(ac_s, "m1", -1), (ac_a, "e3", -2), (dv_s, "m2", -1), (dv_f, "k2", -1)],
                "max_scores2": [(dv_f, "k2", 0), (ac_s, "m1", -1), (ac_a, "e3", -2), (dv_s, "m2", -1)],
                "max_rows1": [(ac_a, "e3", -1), (dv_s, "m2", 0), (dv_f, "k2", 0), (ac_s, "m1", -1)],
                "scores3": [(dv_s, "m2", 1), (dv_f, "k2", 1), (ac_s, "m1", 0), (ac_a, "e3", -1)],
                "max_scores1": [(dv_r, "i1", -4), (ac_r, "xT", -4), (ac_t, "cT", -1), (ac_t, "xT", -3),
                    (dv_t, "mt", -2), (dv_s, "m1", -1)],
                "ctx_turned": [(ac_t, "xT", -2), (dv_t, "mt", -1), (dv_s, "m1", 0), (dv_r, "i1", -4),
                    (ac_r, "xT", -4), (ac_t, "cT", -1)],
                "values_keys": [(dv_s, "m1", 1), (dv_r, "i1", -3), (ac_r, "xT", -3), (ac_t, "cT", 0),
                    (ac_t, "xT", -2), (dv_t, "mt", -1)],
                "x1_turned": [(dv_t, "mt", 1), (dv_s, "m1", 2), (dv_r, "i1", -2), (ac_r, "xT", -2),
                    (ac_t, "cT", 1), (ac_t, "xT", -1)],
                "x2_turned": [(ac_t, "cT", 3), (ac_t, "xT", 1), (dv_t, "mt", 2), (dv_s, "m1", 3),
                    (dv_r, "i1", -1), (ac_r, "xT", -1)],
                "affinities": [(ac_r, "xT", 0), (ac_t, "cT", 3), (ac_t, "xT", 1), (dv_t, "mt", 2),
                    (dv_s, "m1", 3), (dv_r, "i1", -1)],
                "cross_keys_values": [(ac_t, "Q2", -2), (ac_a, "e2", -1), (ac_t, "v", -1)],
                "scores2": [(ac_t, "v", 0), (ac_t, "Q2", -2), (ac_a, "e2", -1)],
                "cross_queries": [(ac_a, "e2", 1), (ac_t, "v", 1), (ac_t, "Q2", -1)],
                "scores0": [(dv_t, "x1", -1), (dv_a, "ot", -1), (ac_a, "e0", -1)],
                "weighted": [(ac_a, "e0", 0), (dv_t, "x1", -1), (dv_a, "ot", -1)],
                "projected": [(dv_a, "ot", 0), (ac_a, "e0", 0), (dv_t, "x1", -1)],
                "scores1": [(ac_a, "e1", -1)],
                "cross_output": [(dv_r, "tot", -2), (dv_t, "y1", -1)],
                "ranks": [(dv_t, "y1", 1), (dv_r, "tot", -1)],
            }

            def free(g, use):
                for stage, name, ahead in BEFORE[use] if g.it is None else BEFORE[use][:1]:
                    wait(pe, stage, g.n + ahead, name)

            def x_turned(g):
                wait(pe, ac_l, g.n, "n")
                free(g, "x_turned")
                for j in range(J):
                    last = tr(BANK["x_turned"][:, j * P:(j + 1) * P], xn[g.par][:, j, :], identf)
                last.then_inc(*pe_f.done("xT"))

            def queries(g):
                wait(pe, ac_f, g.n, "xT")
                free(g, "queries")
                for i, w in enumerate((WQ, WQR)):
                    last = mm(BANK["queries"][:, i * TG:(i + 1) * TG], w, xT[:, :], start=True, stop=True)
                last.then_inc(*pe_f.done("QQ"))

            def keys(g):
                wait(pe, ac_f, g.n, "xT")
                free(g, "keys")
                for i, w in enumerate((WK, WKR)):
                    last = mm(BANK["keys"][:, i * TG:(i + 1) * TG], w, xT[:, :], start=True, stop=True)
                last.then_inc(*pe_f.done("KK"))

            def values(g):
                wait(pe, ac_f, g.n, "xT")
                free(g, "values")
                for j in range(J):
                    last = mm(BANK["values"][:, j * D:(j + 1) * D], xT[:, j * P:(j + 1) * P], WV,
                              start=True, stop=True)
                last.then_inc(*pe_f.done("V"))

            def max_scores(g, k):
                wait(pe, ac_f, g.n, "z1")
                wait(pe, ac_f, g.n, "x3")
                free(g, f"max_scores{k}")
                bank_, strip = BANK[f"max_scores{k}"], slice(32 * k, 32 * k + 32)
                mm(bank_[:, :], ident_b[:, :], negq_b[:, :], start=True, stop=False)
                for j in range(J):
                    for b in range(2):
                        q = 2 * j + b
                        last = mm(bank_[:, 256 * j:256 * j + 256], qz[g.par][strip, q, :],
                                  kex[g.par][strip, :, q * SQ:(q + 1) * SQ],
                                  start=False, stop=j == J - 1 and b == 1, tile_position=(32 * k, 0))
                last.then_inc(*pe_s.done(f"s{k}"))

            def max_rows(g):
                wait(pe, dv_s, g.n, "lo")
                for i in range(2):
                    free(g, f"max_rows{i}")
                    for h_ in range(2):
                        for j in range(J):
                            last = mm(BANK[f"max_rows{i}"][96:104, (2 * h_ + j) * P:(2 * h_ + j + 1) * P],
                                      mt[:, j, 2 * i + h_, :, :].rearrange("p t h -> p (t h)"),
                                      ident_b[:, :], start=True, stop=True, tile_position=(0, 96))
                    last.then_inc(*pe_s.done(f"m{i}"))

            def scores(g, k):
                j, c = k // 2, k % 2
                if k == 0:
                    wait_dma(pe, d_k, g, 12)
                    wait(pe, dv_s, g.n, "e0")
                    wait(pe, ac_s, g.n, "e3")
                free(g, f"scores{k}")
                bank_ = BANK[f"scores{k}"]
                mm(bank_[:, :], ident_b[:, :], negk_b[:, :], start=True, stop=False)
                for r_ in range(2):
                    for b in range(2):
                        q = 2 * j + b
                        last = mm(bank_[:, 256 * r_:256 * r_ + 256], kst[g.par][:, 2 * c + r_, q, :],
                                  qex[:, 2 * c + r_, :, q * SQ:(q + 1) * SQ],
                                  start=False, stop=r_ == 1 and b == 1)
                last.then_inc(*pe_a.done(f"s{k}"))

            def weighted(g, k):
                j, c = k // 2, k % 2
                wait(pe, ac_a, g.n, f"e{k}")
                if k == 0:
                    wait(pe, ac_f, g.n, "V1")
                    free(g, "weighted")
                for i in range(8):
                    h = 8 * c + i
                    o_ = BANK["weighted"][32 * (h // 4):32 * (h // 4) + 32,
                                          j * 256 + (h % 4) * SQ:j * 256 + (h % 4 + 1) * SQ]
                    last = mm(o_, vau[g.par][:, j, h, :], prob[k % 2][:, i * SQ:(i + 1) * SQ],
                              start=True, stop=True, tile_position=(0, 32 * (h // 4)))
                last.then_inc(*pe_a.done(f"p{k}"))

            def ctx_turned(g):
                wait_dma(pe, d_c, g)
                free(g, "ctx_turned")
                for j in range(J):
                    last = tr(BANK["ctx_turned"][:, j * P:(j + 1) * P], cin[g.par][:, j, :], identf)
                last.then_inc(*pe_t.done("cT"))

            def projected(g):
                wait(pe, dv_a, g.n, "tr")
                free(g, "projected")
                for j in range(J):
                    last = mm(BANK["projected"][:, j * D:(j + 1) * D],
                              ont[g.par][:, j, :, :, :].rearrange("p b q t -> p (b q t)"), WO,
                              start=True, stop=True)
                last.then_inc(*pe_t.done("out"))

            def x1_turned(g):
                wait(pe, ac_t, g.n, "n")
                free(g, "x1_turned")
                for j in range(J):
                    last = tr(BANK["x1_turned"][:, j * P:(j + 1) * P], xn1[:, j, :], identf)
                last.then_inc(*pe_t.done("xT"))

            def cross_keys_values(g):
                wait(pe, ac_t, g.n, "cT")
                free(g, "cross_keys_values")
                for j in range(J):
                    o_ = BANK["cross_keys_values"][:, j * 256:(j + 1) * 256]
                    mm(o_, ones_b[:, :], bkv[:, :], start=True, stop=False)
                    last = mm(o_, cxT[:, j * P:(j + 1) * P], wc[:, 1:3, :], start=False, stop=True)
                last.then_inc(*pe_t.done("KV"))

            def cross_queries(g):
                wait(pe, ac_t, g.n, "xT")
                free(g, "cross_queries")
                mm(BANK["cross_queries"][:, 0:TG], wc[:, 0, :], xT1[:, :], start=True, stop=True
                   ).then_inc(*pe_t.done("Q2"))

            def values_keys(g):
                wait(pe, ac_t, g.n, "v")
                free(g, "values_keys")
                for j in range(J):
                    last = mm(BANK["values_keys"][:, j * 256:(j + 1) * 256], v2[:, j, :], k2[:, j, :, :],
                              start=True, stop=True)
                last.then_inc(*pe_t.done("gram"))

            def through_output(g):
                wait(pe, dv_t, g.n, "mt")
                free(g, "through_output")
                for j in range(J):
                    for b in range(2):
                        last = mm(BANK["through_output"][:, (2 * j + b) * D:(2 * j + b + 1) * D],
                                  mt2[:, j, b, :], wc[:, 3, :], start=True, stop=True)
                last.then_inc(*pe_t.done("R"))

            def cross_output(g):
                wait(pe, ac_t, g.n, "R")
                wait(pe, ac_t, g.n, "Q2")
                free(g, "cross_output")
                for j in range(J):
                    last = mm(BANK["cross_output"][:, j * 256:(j + 1) * 256], q2[:, j * P:(j + 1) * P],
                              r2s[g.par][:, j, :, :], start=True, stop=True)
                last.then_inc(*pe_t.done("o2"))

            def x2_turned(g):
                wait(pe, dv_r, g.n, "p1")
                free(g, "x2_turned")
                for j in range(J):
                    last = tr(BANK["x2_turned"][:, j * P:(j + 1) * P], xp[:, j, :], identf)
                last.then_inc(*pe_r.done("xT"))

            def affinities(g):
                wait(pe, ac_r, g.n, "xT")
                free(g, "affinities")
                for j in range(J):
                    last = mm(BANK["affinities"][:, j * E:(j + 1) * E], xpT[:, j * P:(j + 1) * P], cT[:, :],
                              start=True, stop=True)
                last.then_inc(*pe_r.done("aff"))

            def ranks(g):
                wait(pe, dv_r, g.n, "o1")
                free(g, "ranks")
                bank_ = BANK["ranks"]
                for j in range(J + 1):
                    for i in range(min(j + 1, J)):
                        last = mm(bank_[:, j * E:(j + 1) * E], tri_b[:, :] if i == j else ones_b[:, :],
                                  ohb[:, i, :], start=i == 0, stop=i == min(j, J - 1))
                last.then_inc(*pe_r.done("rank"))

            def expert_offsets(part):
                count = -(-E // (TOTAL + 2 - NG - QUIET))
                if part * count >= E:
                    return
                for stage_, name, _ in BEFORE["scores1"]:
                    wait(pe, stage_, NG - 1, name)
                pe.wait_ge(d_weights, 16 * N_WEIGHTS)
                pe.wait_ge(d_late, 16 * N_LATE)
                for e in range(part * count, min(E, (part + 1) * count)):
                    for c in range(FC):
                        last = mm(BANK["scores1"][:, e * FC + c:e * FC + c + 1],
                                  w1[:, e, c * P:(c + 1) * P], gb[:, 1, e:e + 1], start=True, stop=True)
                if e == E - 1:
                    last.then_inc(s_pe, 1)

            def one(g):
                stage(g, 2, weighted, 2)
                stage(g, 2, through_output)
                stage(g, 2, weighted, 3)
                stage(g, 3, cross_queries)
                stage(g, 1, max_rows)
                stage(g, 1, ctx_turned)
                stage(g, 3, cross_output)
                stage(g, 0, x_turned)
                stage(g, 4, x2_turned)
                stage(g, 0, queries)
                stage(g, 0, keys)
                stage(g, 2, projected)
                stage(g, 0, values)
                stage(g, 1, cross_keys_values)
                stage(g, 4, affinities)
                stage(g, 1, scores, 0)
                stage(g, 1, scores, 1)
                stage(g, 0, max_scores, 0)
                stage(g, 4, ranks)
                stage(g, 0, max_scores, 1)
                stage(g, 0, max_scores, 2)
                stage(g, 1, scores, 2)
                stage(g, 0, max_scores, 3)
                stage(g, 1, weighted, 0)
                stage(g, 1, values_keys)
                stage(g, 1, weighted, 1)
                stage(g, 1, scores, 3)
                stage(g, 2, x1_turned)

            rounds(nc.tensor, one, expert_offsets)

            wait(pe, dv_r, NG - 1, "tot")

            def expert(b):
                return nc.tensor.value_load(bti[0:1, 0, bass.ds(b.n, 1)], min_val=0, max_val=E - 1)

            def transposed(b):
                wait_b(pe, "dve_xh", b.n)
                wait_b(pe, "act_xT", b.n - 1)
                tr(M[0][:, 0:P], xh[b.c % 2][:, :], identf).then_inc(*ffn["pe_xT"].done("pe_xT"))

            def hidden(b, e):
                u = b.c % 2
                wait_b(pe, "act_xT", b.n)
                wait_b(pe, "dve_h", b.n - 2)
                mm(B1[u][:, :], xhT[u][:, :], w1[:, bass.ds(e, 1), :], start=True, stop=True
                   ).then_inc(*ffn["pe_h"].done("pe_h"))

            def turned(b):
                u = b.c % 2
                wait_b(pe, "dve_h", b.n)
                wait_b(pe, "act_relu", b.n - 2)
                wait_b(pe, "dve_relu", b.n - 2)
                for c in range(FC):
                    last = tr(HT[u][c // 2][:, (c % 2) * P:(c % 2 + 1) * P], hs[u][:, c * P:(c + 1) * P],
                              identf)
                last.then_inc(*ffn["pe_hT"].done("pe_hT"))

            def second(b, e):
                u = b.c % 2
                wait_b(pe, "act_relu", b.n)
                wait_b(pe, "dve_relu", b.n)
                wait_b(pe, "dve_yb", b.n - 1)
                for c in range(FC):
                    last = mm(M[1][:, 0:D], hT[u][:, c, :], w2[:, bass.ds(e, 1), c, :],
                              start=c == 0, stop=c == FC - 1)
                last.then_inc(*ffn["pe_y"].done("pe_y"))

            pe.wait_ge(s_gain, 1)
            pe.wait_ge(s_tab, 1)

            def steps(blocks):
                e = expert(blocks[0])
                for b in blocks:
                    if b.within(NBLK):
                        hidden(b, e)
                    if b is blocks[0]:
                        e2, e1 = (expert(b.on(k)) if b.on(k).within(NBLK) else None for k in (-2, -1))
                    if b.on(-1).within(NBLK):
                        turned(b.on(-1))
                    if b.on(-2).within(NBLK):
                        second(b.on(-2), e2)
                    e2, e1, e = e1, e, None
                    if b is not blocks[-1] and b.on(1).within(NBLK):
                        e = expert(b.on(1))
                    if b.on(2).within(NBLK):
                        transposed(b.on(2))

            transposed(Block(0))
            transposed(Block(1))
            steps([Block(c) for c in range(RB)])
            with nc.tensor.Fori(1, NBLK // RB - 1) as it:
                steps([Block(u, it, RB) for u in range(RB)])
            steps([Block(c) for c in range(NBLK - RB, NBLK + 2)])

        @block.scalar
        def _(ac):
            act, cp = nc.scalar.activation, nc.scalar.copy

            def norm_x(g):
                wait(ac, po_l, g.n, "nb")
                wait(ac, pe_f, g.n - 2, "xT")
                for j in range(J):
                    last = act(xn[g.par][:, j, :], xin[g.par][:, j, :], ACT.Identity,
                               bias=nb["L"][:, j:j + 1], scale=rs["L"][:, j:j + 1])
                last.then_inc(*ac_l.done("n"))

            def x_turned(g):
                wait(ac, pe_f, g.n, "xT")
                wait(ac, pe_f, g.n - 1, "QQ")
                wait(ac, pe_f, g.n - 1, "KK")
                wait(ac, pe_f, g.n - 1, "V")
                cp(xT[:, :], BANK["x_turned"][:, 0:TG]).then_inc(*ac_f.done("xT"))

            def values(g):
                wait(ac, pe_f, g.n, "V")
                wait(ac, pe_a, g.n - 2, "p3")
                for b in range(2):
                    cp(vau[g.par][64 * b:64 * b + 64, :, :, 16 * b:16 * b + HD],
                       BANK["values"][64 * b:64 * b + 64, 0:TG].rearrange("p (j h d) -> p j h d", j=J, h=H)
                       ).then_inc(*ac_f.done(f"V{b}"))

            def q_high(g):
                wait(ac, po_f, g.n, "qf")
                wait_dma(ac, d_q, g.back(1), 12)
                cp(qhi[:, :], qf[:, :]).then_inc(*ac_f.done("qhi"))

            def q_padded(g):
                wait(ac, po_f, g.n, "qf")
                wait(ac, pe_s, g.n - 2, "s3")
                qd = qz[g.par][:, :, :].rearrange("p (j b) (c q) -> p j b c q", b=2, c=2)
                qs_ = qf[:, :].rearrange("p (j b q) -> p j b q", j=J, b=2)
                for b in range(2):
                    cp(qd[:, :, b, b, :], qs_[:, :, b, :]).then_inc(*ac_f.done(f"z{b}"))

            def k_high(g):
                wait(ac, po_f, g.n, "kf")
                wait_dma(ac, d_k, g.back(1), 12)
                diag = khi[:, :, :].rearrange("p (j b) (c k) -> p j b c k", b=2, c=2)
                for b in range(2):
                    last = cp(diag[:, :, b, b, :],
                              kf[:, :].rearrange("p (j b k) -> p j b k", j=J, b=2)[:, :, b, :])
                last.then_inc(*ac_f.done("khi"))

            def k_by_head(g):
                wait(ac, po_f, g.n, "kf")
                wait(ac, pe_s, g.n - 2, "s3")
                for i in range(4):
                    act(kex[g.par][:, i, :], kf[:, :], ACT.Copy, scale=own4[:, i:i + 1]
                        ).then_inc(*ac_f.done(f"x{i}"))

            def max_rows(g):
                wait_dma(ac, d_q, g, 12)
                wait(ac, ac_s, g.n - 2, "e3")
                wait(ac, dv_s, g.n - 2, "e0")
                for i in range(2):
                    wait(ac, pe_s, g.n, f"m{i}")
                    cp(qst[g.par][96:104, 2 * i:2 * i + 2, :].rearrange("p r t -> p (r t)"),
                       BANK[f"max_rows{i}"][96:104, :]).then_inc(*ac_s.done(f"m{i}"))

            def q_by_head(g):
                wait(ac, pe_a, g.n - 1, "s3")
                wait(ac, ac_s, g.n, "m1")
                for i in range(1, 4):
                    act(qex[:, :, i, :], qst[g.par][:, :, :].bitcast(FP32), ACT.Copy,
                        scale=own4s[:, i:i + 1]).then_inc(*ac_s.done(f"e{i}"))

            def exp(g, k):
                wait(ac, pe_a, g.n, f"s{k}")
                if k < 2:
                    wait(ac, pe_a, g.n - 1, f"p{k + 2}")
                else:
                    wait(ac, pe_a, g.n, f"p{k - 2}")
                act(prob[k % 2][:, :], BANK[f"scores{k}"][:, :], ACT.Exp).then_inc(*ac_a.done(f"e{k}"))

            def ctx_turned(g):
                wait(ac, pe_t, g.n, "cT")
                wait(ac, pe_t, g.n - 1, "KV")
                cp(cxT[:, :], BANK["ctx_turned"][:, 0:TG]).then_inc(*ac_t.done("cT"))

            def cross_keys_values(g):
                wait(ac, pe_t, g.n, "KV")
                wait(ac, pe_t, g.n - 1, "gram")
                kv = BANK["cross_keys_values"][:, :].rearrange("p (j a d) -> p j a d", j=J, a=2)
                for b in range(2):
                    rows_ = slice(64 * b, 64 * b + 64)
                    cp(k2[rows_, :, b, :], kv[rows_, :, 0, :]).then_inc(*ac_t.done(f"k{b}"))
                cp(v2[:, :, :], kv[:, :, 1, :]).then_inc(*ac_t.done("v"))

            def norm_x1(g):
                wait(ac, po_t, g.n, "nb")
                wait(ac, po_t, g.n - 1, "xnb")
                wait(ac, dv_t, g.n - 1, "y1")
                for j in range(J):
                    last = act(xn1[:, j, :], x1[g.par][:, j, :], ACT.Identity,
                               bias=nb["T"][:, j:j + 1], scale=rs["T"][:, j:j + 1])
                last.then_inc(*ac_t.done("n"))

            def x1_turned(g):
                wait(ac, pe_t, g.n, "xT")
                wait(ac, pe_t, g.n - 1, "Q2")
                cp(xT1[:, :], BANK["x1_turned"][:, 0:TG]).then_inc(*ac_t.done("xT"))

            def cross_queries(g):
                wait(ac, pe_t, g.n, "Q2")
                wait(ac, pe_t, g.n - 1, "o2")
                act(q2[:, :], BANK["cross_queries"][:, 0:TG], ACT.Identity, bias=bc[:, 4:5]
                    ).then_inc(*ac_t.done("Q2"))

            def through_output(g):
                wait(ac, pe_t, g.n, "R")
                wait(ac, pe_t, g.n - 2, "o2")
                cp(r2s[g.par][:, :, :, :].rearrange("p j b d -> p (j b d)"), BANK["through_output"][:, :]
                   ).then_inc(*ac_t.done("R"))

            def norm_y(g):
                wait(ac, po_t, g.n, "nb2")
                wait(ac, po_t, g.n - 1, "x2")
                for j in range(J):
                    last = act(yn[:, j, :], y1[:, j, :], ACT.Identity,
                               bias=nb["U"][:, j:j + 1], scale=rs["U"][:, j:j + 1])
                last.then_inc(*ac_t.done("z"))

            def x2_turned(g):
                wait(ac, pe_r, g.n, "xT")
                wait(ac, pe_r, g.n - 1, "aff")
                cp(xpT[:, :], BANK["x2_turned"][:, 0:TG]).then_inc(*ac_r.done("xT"))

            def exp_affinity(g):
                wait(ac, po_t, g.n, "x2")
                cp(pay[g.par][:, :, C_ID], tokid[:, bass.ds(g.n * J, J)]).then_inc(*ac_r.done("id"))
                wait(ac, dv_r, g.n, "g1")
                wait(ac, dv_r, g.n - 1, "al1")
                act(ea[:, :], mx8[:, :, 0], ACT.Exp, scale=-1.0).then_inc(*ac_r.done("ea"))

            def one(g):
                stage(g, 2, exp, 3)
                stage(g, 2, through_output)
                stage(g, 3, x1_turned)
                stage(g, 3, cross_queries)
                stage(g, 1, max_rows)
                stage(g, 0, norm_x)
                stage(g, 1, ctx_turned)
                stage(g, 0, x_turned)
                stage(g, 1, q_by_head)
                stage(g, 4, x2_turned)
                stage(g, 0, q_high)
                stage(g, 0, q_padded)
                stage(g, 0, values)
                stage(g, 0, k_by_head)
                stage(g, 0, k_high)
                stage(g, 1, cross_keys_values)
                stage(g, 1, exp, 0)
                stage(g, 1, exp, 1)
                stage(g, 2, norm_x1)
                stage(g, 3, norm_y)
                stage(g, 4, exp_affinity)
                stage(g, 1, exp, 2)

            ac.wait_ge(d_const, 16 * N_CONST)
            ac.wait_ge(s_vec, 1)
            ac.wait_ge(s_pool, 1)
            rounds(nc.scalar, one)

            ac.wait_ge(d_late, 16 * N_LATE)
            ac.wait_ge(s_pe, 2)
            for e in range(E):
                last = act(w1[:, e, :], w1[:, e, :], ACT.Copy, scale=gb[:, 0, e:e + 1])
            last.then_inc(s_gain, 1)
            ac.wait_ge(s_pads, 1)
            for e in range(E // 2, E):
                at = nc.scalar.value_load(pri[0:1, e:e + 1], min_val=0, max_val=(e + 1) * CAP - P)
                ac.dma_start(rows[bass.ds(at, P), :], padt[:, :]).then_inc(d_pad, 16)
            ac.wait_ge(s_tab, 1)
            ac.wait_ge(s_b1, 1)

            def turned(b):
                wait_b(ac, "pe_xT", b.n)
                wait_b(ac, "pe_h", b.n - 2)
                cp(xhT[b.c % 2][:, :], M[0][:, 0:P]).then_inc(*ffn["act_xT"].done("act_xT"))

            def relu(b, e):
                u = b.c % 2
                wait_b(ac, "pe_hT", b.n)
                wait_b(ac, "pe_y", b.n - 2)
                for c in range(2):
                    last = act(hT[u][:, c, :], HT[u][0][:, c * P:(c + 1) * P], ACT.Relu,
                               bias=b1[:, bass.ds(e, 1), c])
                last.then_inc(*ffn["act_relu"].done("act_relu"))

            def expert(b):
                return nc.scalar.value_load(bti[0:1, 0, bass.ds(b.n, 1)], min_val=0, max_val=E - 1)

            def steps(blocks):
                e = expert(blocks[0].on(-1)) if blocks[0].on(-1).within(NBLK) else None
                for b in blocks:
                    if b.on(-1).within(NBLK):
                        relu(b.on(-1), e)
                    e = expert(b) if b is not blocks[-1] and b.within(NBLK) else None
                    if b.on(2).within(NBLK):
                        turned(b.on(2))

            turned(Block(0))
            turned(Block(1))
            steps([Block(c) for c in range(RB)])
            with nc.scalar.Fori(1, NBLK // RB - 1) as it:
                steps([Block(u, it, RB) for u in range(RB)])
            steps([Block(c) for c in range(NBLK - RB, NBLK + 1)])

        @block.vector
        def _(dv):
            v = nc.vector

            def stats(stage, n, src, key, b, a):
                for j in range(J):
                    v.bn_stats(stat[key][:, j, :], src(j)).then_inc(*stage.done(f"{b}{j}"))
                wait(dv, stage, n, f"{b}1", alone=True)
                for j in range(J):
                    v.bn_aggr(mv[key][:, j, :], stat[key][:, j, :]).then_inc(*stage.done(f"{a}{j}"))

            def stats_x(g):
                wait(dv, po_l, g.n - 1, "nb")
                wait(dv, dv_l, g.n - 1, "a1")
                wait_dma(dv, d_x, g)
                stats(dv_l, g.n, lambda j: xin[g.par][:, j, :], "L", "b", "a")

            def rotate_q(g):
                wait(dv, pe_f, g.n, "QQ")
                wait(dv, po_f, g.n - 1, "qf")
                for i, buf in enumerate((t1, t2)):
                    v.scalar_tensor_tensor(
                        buf[0][:, :].rearrange("p (s t) -> p s t", t=SQ),
                        BANK["queries"][:, i * TG:(i + 1) * TG].rearrange("p (s t) -> p s t", t=SQ),
                        bc[:, i:i + 1], rope[i].unsqueeze(1).broadcast_to((P, 2 * J, SQ)), ALU.add, ALU.mult
                    ).then_inc(*dv_f.done(f"q{i + 1}"))

            def rotate_k(g):
                wait(dv, pe_f, g.n, "KK")
                wait(dv, po_f, g.n - 1, "kf")
                for i, buf in enumerate((t1, t2)):
                    v.scalar_tensor_tensor(
                        buf[1][:, :].rearrange("p (s t) -> p s t", t=SQ),
                        BANK["keys"][:, i * TG:(i + 1) * TG].rearrange("p (s t) -> p s t", t=SQ),
                        bc[:, 2 + i:3 + i], rope[2 + i].unsqueeze(1).broadcast_to((P, 2 * J, SQ)),
                        ALU.add, ALU.mult).then_inc(*dv_f.done(f"k{i + 1}"))

            def row_max(g, k):
                wait(dv, pe_s, g.n, f"s{k}")
                wait(dv, dv_s, g.n - 1, "lo")
                v.tensor_reduce(mx[:, :, 4 * k:4 * k + 4],
                                BANK[f"max_scores{k}"][:, :].rearrange("p (j h k) -> p j h k", j=J, k=SQ),
                                AX.X, ALU.max).then_inc(*dv_s.done(f"m{k}"))

            def max_parts(g):
                for k in range(4):
                    wait(dv, dv_s, g.n, f"m{k}")
                wait(dv, pe_s, g.n - 1, "m1")
                mxv = mx[:, :, :].rearrange("p j (r h) -> p (j r) h", h=4)
                mtv = mt[:, :, :, :, :].rearrange("p j r t h -> p (j r) t h")
                v.tensor_scalar(mtv[:, :, 0, :], mxv, -1.0, None, ALU.mult).then_inc(*dv_s.done("hi"))
                wait(dv, dv_s, g.n, "hi")
                v.scalar_tensor_tensor(mtv[:, :, 1, :], mxv, -1.0, mtv[:, :, 0, :],
                                       ALU.mult, ALU.subtract).then_inc(*dv_s.done("lo"))

            def q_by_head(g):
                wait(dv, ac_s, g.n, "m1")
                wait(dv, pe_a, g.n - 1, "s3")
                v.tensor_scalar(qex[:, :, 0, :], qst[g.par][:, :, :].bitcast(FP32),
                                own4s[:, 0:1], None, ALU.mult).then_inc(*dv_s.done("e0"))

            def weighted_turned(g):
                wait(dv, pe_a, g.n, "p3")
                wait(dv, dv_a, g.n - 1, "n3")
                v.transpose(ot[:, :, :, :, :, :].rearrange("p j g q b t -> p (j g q b t)"),
                            BANK["weighted"][:, :]).then_inc(*dv_a.done("ot"))

            def divide(g):
                wait(dv, dv_a, g.n, "ot")
                v.reciprocal(rd[:, :, :, :, :], ot[:, :, :, :, :, HD]).then_inc(*dv_a.done("rd"))
                wait(dv, dv_a, g.n, "rd")
                wait(dv, dv_a, g.n - 1, "tr")
                for j in range(J):
                    for b in range(2):
                        v.tensor_tensor(
                            on[:, j, b, :, :, :], ot[:, j, :, :, b, 0:HD].rearrange("p g q d -> p q g d"),
                            rd[:, j, :, :, b].rearrange("p g q -> p q g").unsqueeze(3)
                            .broadcast_to((P, 2, 4, HD)), ALU.mult).then_inc(*dv_a.done(f"n{2 * j + b}"))
                wait(dv, dv_a, g.n, "n3")
                wait(dv, pe_t, g.n - 2, "out")
                v.transpose(ont[g.par][:, :, :, :, :].rearrange("p j b q t -> p (j b q t)"),
                            on[:, :, :, :, :, :].rearrange("p j b q g d -> p (j b q g d)")
                            ).then_inc(*dv_a.done("tr"))

            def x1_sum(g):
                wait(dv, pe_t, g.n, "out")
                wait(dv, po_t, g.n, "xb")
                wait(dv, po_t, g.n - 2, "x2")
                wait(dv, po_t, g.n - 1, "nb")
                v.tensor_tensor(x1[g.par][:, :, :].rearrange("p j d -> p (j d)"), BANK["projected"][:, 0:TG],
                                xr[g.par][:, :, :].rearrange("p j d -> p (j d)"), ALU.add
                                ).then_inc(*dv_t.done("x1"))
                wait(dv, dv_t, g.n, "x1")
                stats(dv_t, g.n, lambda j: x1[g.par][:, j, :], "T", "b", "a")

            def own_head(g):
                wait(dv, pe_t, g.n, "gram")
                wait(dv, pe_t, g.n - 1, "R")
                v.tensor_tensor(mt2[:, :, :, :].rearrange("p j b d -> p (j b) d"),
                                BANK["values_keys"][:, :].rearrange("p (a d) -> p a d", d=D),
                                headmask.unsqueeze(1).broadcast_to((P, 2 * J, D)), ALU.mult
                                ).then_inc(*dv_t.done("mt"))

            def y_sum(g):
                wait(dv, pe_t, g.n, "o2")
                wait(dv, po_t, g.n, "xnb")
                wait(dv, ac_t, g.n - 1, "z")
                o2v = BANK["cross_output"][:, :].rearrange("p (j b d) -> p j b d", j=J, b=2)
                for b in range(2):
                    rows_ = slice(64 * b, 64 * b + 64)
                    v.tensor_tensor(y1[rows_, :, :], o2v[rows_, :, b, :], xn1[rows_, :, :], ALU.add
                                    ).then_inc(*dv_t.done(f"y{b}"))
                wait(dv, dv_t, g.n, "y1")
                stats(dv_t, g.n, lambda j: y1[:, j, :], "U", "c", "d")

            def stats_x2(g):
                wait(dv, po_t, g.n, "x2")
                wait(dv, dv_r, g.n - 1, "c")
                wait(dv, po_r, g.n - 1, "pow")
                stats(dv_r, g.n, lambda j: pay[g.par][:, j, 0:D], "R", "b", "a")

            def norm_x2(g):
                wait(dv, po_r, g.n, "pow")
                wait(dv, po_r, g.n - 1, "C")
                wait(dv, dv_r, g.n - 1, "cm")
                v.scalar_tensor_tensor(rc[:, :], mv["R"][:, :, 0], -1.0, rs["R"][:, :],
                                       ALU.mult, ALU.mult).then_inc(*dv_r.done("c"))
                wait(dv, dv_r, g.n, "c")
                wait(dv, pe_r, g.n - 1, "xT")
                for j in range(J):
                    v.tensor_scalar(xp[:, j, :], pay[g.par][:, j, 0:D], rs["R"][:, j:j + 1], rc[:, j:j + 1],
                                    ALU.mult, ALU.add).then_inc(*dv_r.done(f"p{j}"))

            def stats_norm(g):
                wait(dv, dv_r, g.n, "p1")
                wait(dv, dv_r, g.n - 1, "B")
                wait(dv, po_r, g.n - 1, "pow2")
                stats(dv_r, g.n, lambda j: xp[:, j, :], "Q", "d", "e")

            def row_scalars(g):
                wait(dv, po_r, g.n, "pow2")
                v.tensor_tensor(rm[:, :], rc[:, :], mv["Q"][:, :, 0], ALU.subtract
                                ).then_inc(*dv_r.done("cm"))
                wait(dv, dv_r, g.n, "cm")
                v.tensor_tensor(pay[g.par][:, :, C_B], rm[:, :], rs["Q"][:, :], ALU.mult
                                ).then_inc(*dv_r.done("B"))

            def choose(g):
                aff = BANK["affinities"][:, 0:J * E].rearrange("p (j e) -> p j e", j=J)
                wait(dv, pe_r, g.n, "aff")
                wait(dv, ac_r, g.n - 1, "ea", alone=True)
                for j in range(J):
                    v.max(mx8[:, j, :], aff[:, j, :]).then_inc(*dv_r.done(f"g{j}"))
                wait(dv, dv_r, g.n, "g1", alone=True)
                for j in range(J):
                    v.max_index(ix8[:, j, :], mx8[:, j, :], aff[:, j, :]).then_inc(*dv_r.done(f"i{j}"))
                wait(dv, dv_r, g.n, "i1")
                v.tensor_scalar(idf[:, :], ix8[:, :, 0], float(E - 1), None, ALU.min
                                ).then_inc(*dv_r.done("idm"))
                wait(dv, dv_r, g.n, "idm")
                wait(dv, dv_r, g.n - 1, "pr")
                for j in range(J):
                    v.tensor_scalar(ohb[:, j, :], iota8, idf[:, j:j + 1], None, ALU.is_equal
                                    ).then_inc(*dv_r.done(f"o{j}"))

            def alpha(g):
                wait(dv, ac_r, g.n, "ea")
                v.tensor_scalar(ea1[:, :], ea[:, :], 1.0, None, ALU.add).then_inc(*dv_r.done("al1"))
                wait(dv, dv_r, g.n, "al1")
                v.reciprocal(pay[g.par][:, :, C_AL], ea1[:, :]).then_inc(*dv_r.done("al"))

            def place(g):
                bank_ = BANK["ranks"][:, 0:3 * E].rearrange("p (j e) -> p j e", e=E)
                wait(dv, pe_r, g.n, "rank")
                wait(dv, dv_r, g.n - 1, "tot")
                wait(dv, dv_r, g.n - 1, "si")
                v.tensor_tensor(rk[:, :, :], bank_[:, 0:J, :],
                                cnt[:, :].unsqueeze(1).broadcast_to((P, J, E)), ALU.add
                                ).then_inc(*dv_r.done("rk"))
                wait(dv, dv_r, g.n, "rk")
                v.tensor_tensor(cnt[:, :], cnt[:, :], bank_[:, J, :], ALU.add
                                ).then_inc(*dv_r.done("tot"))
                v.tensor_tensor(rk[:, :, :], rk[:, :, :], ohb[:, :, :], ALU.mult
                                ).then_inc(*dv_r.done("pr"))
                wait(dv, dv_r, g.n, "pr")
                v.tensor_reduce(slf[:, :], rk[:, :, :], AX.X, ALU.add).then_inc(*dv_r.done("sl"))
                wait_dma(dv, d_s, g.back(2), J)
                wait(dv, dv_r, g.n, "sl")
                v.tensor_copy(sli[g.par][:, :], slf[:, :]).then_inc(*dv_r.done("si"))

            def one(g):
                stage(g, 4, stats_x2)
                stage(g, 1, max_parts)
                stage(g, 5, alpha)
                stage(g, 0, stats_x)
                stage(g, 2, weighted_turned)
                stage(g, 4, norm_x2)
                stage(g, 1, q_by_head)
                stage(g, 2, divide)
                stage(g, 4, stats_norm)
                stage(g, 0, rotate_q)
                stage(g, 0, rotate_k)
                stage(g, 2, x1_sum)
                stage(g, 3, y_sum)
                stage(g, 4, choose)
                stage(g, 4, row_scalars)
                stage(g, 0, row_max, 0)
                stage(g, 0, row_max, 1)
                stage(g, 4, place)
                stage(g, 0, row_max, 2)
                stage(g, 1, own_head)
                stage(g, 0, row_max, 3)

            for i in range(2):
                v.memset(qst[i][:, :, :].bitcast(FP32), 0.0)
                v.memset(qz[i][:, :, :].bitcast(FP32), 0.0)
                v.memset(vau[i][:, :, :, :], 0.0)
                v.memset(pay[i][:, :, :], 0.0)
            v.memset(khi[:, :, :].bitcast(FP32), 0.0)
            v.memset(klo[:, :, :].bitcast(FP32), 0.0)
            v.memset(ones_b[:, :], 1.0).then_inc(s_zero, 1)
            dv.wait_ge(s_zero, 1)
            dv.wait_ge(d_const, 16 * N_CONST)
            for i in range(2):
                for b in range(2):
                    v.memset(vau[i][64 * b:64 * b + 64, :, :, 16 * b + HD:16 * b + HD + 1], 1.0)
            v.tensor_scalar(cnt[:, :], iota8, float(CAP), None, ALU.mult)
            v.tensor_copy(negq_b[:, :].rearrange("p (h k) -> p h k", k=SQ),
                          nqf[:, :].unsqueeze(1).broadcast_to((P, 512 // SQ, SQ)))
            v.tensor_copy(negk_b[:, :].rearrange("p (h k) -> p h k", k=SQ),
                          nkf[:, :].unsqueeze(1).broadcast_to((P, 512 // SQ, SQ)))
            v.tensor_copy(ident_b[:, :], identf)
            v.tensor_copy(tri_b[:, :], trif).then_inc(s_vec, 1)
            both = br[:, 4:6, :].rearrange("p a d -> p (a d)")
            v.tensor_copy(part[0][:, :], both).then_inc(s_part, 1)
            dv.wait_ge(s_part, 1)
            v.tensor_tensor(rest[0][:, :], both, part[0][:, :], ALU.subtract).then_inc(s_part, 1)
            dv.wait_ge(s_part, 2)
            v.tensor_copy(part[1][:, :], rest[0][:, :]).then_inc(s_part, 1)
            dv.wait_ge(s_part, 3)
            v.tensor_tensor(rest[1][:, :], rest[0][:, :], part[1][:, :], ALU.subtract).then_inc(s_part, 1)
            dv.wait_ge(s_part, 4)
            v.tensor_copy(part[2][:, :], rest[1][:, :])
            v.tensor_scalar(bkv[:, :], part[0][:, :], identf[:, 0:1], None, ALU.mult).then_inc(s_part, 1)
            for i in range(1, 3):
                dv.wait_ge(s_part, 4 + i)
                v.scalar_tensor_tensor(bkv[:, :], part[i][:, :], identf[:, i:i + 1], bkv[:, :],
                                       ALU.mult, ALU.add).then_inc(s_part, 1)
            v.tensor_copy(bvx[:, :], bc[:, 5:6].broadcast_to((P, P))).then_inc(s_vec, 1)
            dv.wait_ge(s_pe, 1)
            v.tensor_tensor(BO, M[0][:, 0:D], BO, ALU.add).then_inc(s_vec, 1)
            def penalties(i):
                if i != 2:
                    return
                dv.wait_ge(d_mask, 16)
                v.tensor_reduce(pen[:, :], mk[:, :, :], AX.X, ALU.max).then_inc(s_mask, 1)
                dv.wait_ge(s_mask, 1)
                v.tensor_scalar(pen[:, :], pen[:, :], -3.0e38, 1.0e38, ALU.mult, ALU.mult
                                ).then_inc(s_mask, 1)
                dv.wait_ge(s_mask, 2)
                v.tensor_scalar(pen[:, :], pen[:, :], 0.0, None, ALU.mult).then_inc(s_mask, 1)

            dv.wait_ge(s_vec, 3)
            dv.wait_ge(s_pool, 1)

            rounds(nc.vector, one, early=penalties)

            cs = [0]

            def link(ins):
                cs[0] += 1
                ins.then_inc(s_chain, 1)
                dv.wait_ge(s_chain, cs[0])

            wait(dv, dv_r, NG - 1, "tot")
            v.tensor_copy(pri[:, :], cnt[:, :]).then_inc(s_pads, 1)
            link(v.scalar_tensor_tensor(nbf[:, :], iota8, -float(CAP), cnt[:, :], ALU.mult, ALU.add))
            link(v.tensor_scalar(nbf[:, :], nbf[:, :], float(P - 1), None, ALU.add))
            link(v.tensor_copy(ti[:, :], nbf[:, :]))
            link(v.tensor_scalar(ti[:, :], ti[:, :], 7, None, ALU.logical_shift_right))
            link(v.tensor_copy(nbf[:, :], ti[:, :]))
            link(v.tensor_copy(cum[:, :], nbf[:, :]))
            for e in range(1, E):
                link(v.tensor_tensor(cum[:, e:e + 1], cum[:, e - 1:e], cum[:, e:e + 1], ALU.add))
            link(v.tensor_tensor(geb[:, :, :], blkno.unsqueeze(2).broadcast_to((P, NBLK, E)),
                                 cum[:, :].unsqueeze(1).broadcast_to((P, NBLK, E)), ALU.is_ge))
            link(v.tensor_tensor(gnb[:, :, :], geb[:, :, :],
                                 nbf[:, :].unsqueeze(1).broadcast_to((P, NBLK, E)), ALU.mult))
            link(v.tensor_reduce(bex[:, :], geb[:, :, :], AX.X, ALU.add))
            link(v.tensor_reduce(bst[:, :], gnb[:, :, :], AX.X, ALU.add))
            link(v.tensor_tensor(bst[:, :], blkno, bst[:, :], ALU.subtract))
            link(v.tensor_scalar(bst[:, :], bst[:, :], float(P), None, ALU.mult))
            link(v.scalar_tensor_tensor(bst[:, :], bex[:, :], float(CAP), bst[:, :], ALU.mult, ALU.add))
            link(v.tensor_scalar(btf[:, 1, :], bst[:, :], float(E * CAP), None, ALU.min))
            link(v.tensor_scalar(btf[:, 0, :], bex[:, :], float(E - 1), None, ALU.min))
            v.tensor_copy(bti[:, :, :], btf[:, :, :]).then_inc(s_tab, 1)

            def rows_in(b):
                q = b.c % RB
                wait_rows(dv, b)
                wait_b(dv, "pe_xT", b.n - 2)
                v.tensor_scalar(xh[b.c % 2][:, :], rb[q][:, 0:D], rb[q][:, C_A:C_A + 1],
                                rb[q][:, C_B:C_B + 1], ALU.mult, ALU.add
                                ).then_inc(*ffn["dve_xh"].done("dve_xh"))

            def hidden(b):
                u = b.c % 2
                wait_b(dv, "pe_h", b.n)
                wait_b(dv, "pe_hT", b.n - 2)
                v.tensor_copy(hs[u][:, :], B1[u][:, :]).then_inc(*ffn["dve_h"].done("dve_h"))

            def relu(b, e):
                u = b.c % 2
                wait_b(dv, "pe_hT", b.n)
                wait_b(dv, "pe_y", b.n - 2)
                for c in range(2, FC):
                    last = v.tensor_scalar(hT[u][:, c, :], HT[u][1][:, (c - 2) * P:(c - 1) * P],
                                           b1[:, bass.ds(e, 1), c], 0.0, ALU.add, ALU.max)
                last.then_inc(*ffn["dve_relu"].done("dve_relu"))

            def finish(b, e):
                u, q = b.c % 2, b.c % RB
                wait_b(dv, "pe_y", b.n)
                v.tensor_tensor(yb[u][:, :], M[1][:, 0:D], b2[:, bass.ds(e, 1), :], ALU.add
                                ).then_inc(*ffn["dve_yb"].done("dve_yb"))
                wait_b(dv, "dve_yb", b.n)
                wait_b(dv, "pool_base", b.n)
                wait_out(dv, b)
                v.scalar_tensor_tensor(yo[b.c % 4][:, :], yb[u][:, :], rb[q][:, C_AL:C_AL + 1], bs[q][:, :],
                                       ALU.mult, ALU.add).then_inc(*ffn["dve_yo"].done("dve_yo"))

            def expert(b):
                return nc.vector.value_load(bti[0:1, 0, bass.ds(b.n, 1)], min_val=0, max_val=E - 1)

            def steps(blocks):
                for b in blocks:
                    if b.within(NBLK):
                        hidden(b)
                    if b.on(3).within(NBLK):
                        rows_in(b.on(3))
                    if b is blocks[0]:
                        e2, e1 = (expert(b.on(k)) if b.on(k).within(NBLK) else None for k in (-2, -1))
                    if b.on(-1).within(NBLK):
                        relu(b.on(-1), e1)
                    if b.on(-2).within(NBLK):
                        finish(b.on(-2), e2)
                    e2, e1 = e1, None
                    if b is not blocks[-1] and b.within(NBLK):
                        e1 = expert(b)

            dv.wait_ge(d_late, 16 * N_LATE)
            dv.wait_ge(s_pe, 2)
            v.tensor_tensor(b1[:, :, :].rearrange("p e c -> p (e c)"), BANK["scores1"][:, 0:E * FC],
                            b1[:, :, :].rearrange("p e c -> p (e c)"), ALU.add).then_inc(s_b1, 1)
            dv.wait_ge(s_b1, 1)
            for c in range(3):
                rows_in(Block(c))
            steps([Block(c) for c in range(RB)])
            with nc.vector.Fori(1, NBLK // RB - 1) as it:
                steps([Block(u, it, RB) for u in range(RB)])
            steps([Block(c) for c in range(NBLK - RB, NBLK + 2)])

        @block.gpsimd
        def _(po):
            v = nc.gpsimd

            def inv_std(stage, n, key, tail=""):
                v.tensor_scalar(ve[key][:, :], mv[key][:, :, 1], EPS, None, ALU.add
                                ).then_inc(*stage.done("eps" + tail))
                wait(po, stage, n, "eps" + tail)
                v.tensor_tensor(rs[key][:, :], ve[key][:, :], half[:, :], ALU.pow
                                ).then_inc(*stage.done("pow" + tail))

            def offset(stage, n, key, tail=""):
                wait(po, stage, n, "pow" + tail)
                v.tensor_tensor(nb[key][:, :], mv[key][:, :, 0], rs[key][:, :], ALU.mult
                                ).then_inc(*stage.done("mr" + tail))
                wait(po, stage, n, "mr" + tail)
                v.tensor_scalar(nb[key][:, :], nb[key][:, :], -1.0, None, ALU.mult
                                ).then_inc(*stage.done("nb" + tail))

            def std_x(g):
                wait(po, dv_l, g.n, "a1")
                wait(po, ac_l, g.n - 1, "n")
                inv_std(po_l, g.n, "L")
                offset(po_l, g.n, "L")

            def q_sum(g):
                wait(po, dv_f, g.n, "q2")
                wait(po, po_f, g.n - 1, "qlo")
                wait(po, ac_f, g.n - 1, "z1")
                wait(po, ac_f, g.n - 1, "qhi")
                v.tensor_tensor(qf[:, :], t1[0][:, :], t2[0][:, :], ALU.add).then_inc(*po_f.done("qf"))

            def q_low(g):
                wait(po, ac_f, g.n, "qhi")
                wait_dma(po, d_q, g.back(1), 12)
                v.tensor_tensor(qlo[:, :], qf[:, :], qhi[:, :].bitcast(FP32), ALU.subtract
                                ).then_inc(*po_f.done("qlo"))

            def k_sum(g):
                wait(po, dv_f, g.n, "k2")
                wait(po, po_f, g.n - 1, "klo")
                wait(po, ac_f, g.n - 1, "x3")
                wait(po, ac_f, g.n - 1, "khi")
                v.tensor_tensor(kf[:, :], t1[1][:, :], t2[1][:, :], ALU.add).then_inc(*po_f.done("kf"))

            def k_low(g):
                wait(po, ac_f, g.n, "khi")
                wait_dma(po, d_k, g.back(1), 12)
                kl = klo[:, :, :].rearrange("p (j b) (c k) -> p j b c k", b=2, c=2)
                kh = khi[:, :, :].bitcast(FP32).rearrange("p (j b) (c k) -> p j b c k", b=2, c=2)
                kv = kf[:, :].rearrange("p (j b k) -> p j b k", j=J, b=2)
                for b in range(2):
                    last = v.tensor_tensor(kl[:, :, b, b, :], kv[:, :, b, :], kh[:, :, b, b, :], ALU.subtract)
                last.then_inc(*po_f.done("klo"))

            def x_bias(g):
                wait_dma(po, d_xr, g)
                v.tensor_tensor(xr[g.par][:, :, :], xr[g.par][:, :, :],
                                BO.unsqueeze(1).broadcast_to((P, J, D)), ALU.add
                                ).then_inc(*po_t.done("xb"))

            def std_x1(g):
                wait(po, dv_t, g.n, "a1")
                wait(po, ac_t, g.n - 1, "n")
                inv_std(po_t, g.n, "T")
                offset(po_t, g.n, "T")

            def sum_biases(g):
                wait(po, pe_t, g.n, "xT")
                wait(po, ac_t, g.n, "n")
                v.tensor_tensor(xn1[:, :, :], xn1[:, :, :], BO2.unsqueeze(1).broadcast_to((P, J, D)),
                                ALU.add).then_inc(*po_t.done("xnb"))
                v.tensor_tensor(x1[g.par][:, :, :], x1[g.par][:, :, :],
                                LNB.unsqueeze(1).broadcast_to((P, J, D)), ALU.add).then_inc(*po_t.done("x1b"))

            def std_y(g):
                wait(po, dv_t, g.n, "d1")
                wait(po, ac_t, g.n - 1, "z")
                inv_std(po_t, g.n, "U", "2")
                offset(po_t, g.n, "U", "2")

            def gain(g):
                wait(po, ac_t, g.n, "z")
                v.tensor_tensor(yn[:, :, :], yn[:, :, :], LNG.unsqueeze(1).broadcast_to((P, J, D)),
                                ALU.mult).then_inc(*po_t.done("zg"))

            def x2_sum(g):
                wait(po, po_t, g.n, "zg")
                wait(po, po_t, g.n, "x1b")
                wait_dma(po, d_s, g.back(2), J)
                v.tensor_tensor(pay[g.par][:, :, 0:D], yn[:, :, :], x1[g.par][:, :, :], ALU.add
                                ).then_inc(*po_t.done("x2"))

            def std_x2(g):
                wait(po, dv_r, g.n, "a1")
                wait(po, po_r, g.n - 1, "C")
                wait(po, dv_r, g.n - 1, "p1")
                inv_std(po_r, g.n, "R")

            def std_norm(g):
                wait(po, dv_r, g.n, "e1")
                wait(po, dv_r, g.n - 1, "B")
                wait(po, po_r, g.n - 1, "C")
                inv_std(po_r, g.n, "Q", "2")

            def row_scalars(g):
                px = pay[g.par]
                if g.it is None and g.n == 0:
                    po.wait_ge(s_mask, 3)
                wait(po, po_t, g.n, "x2")
                wait(po, dv_r, g.n, "c")
                wait(po, po_r, g.n, "pow2")
                v.tensor_tensor(px[:, :, C_A], rs["R"][:, :], rs["Q"][:, :], ALU.mult
                                ).then_inc(*po_r.done("A"))
                v.tensor_scalar(px[:, :, C_R], rs["R"][:, :], 1.0, None, ALU.add
                                ).then_inc(*po_r.done("R"))
                v.tensor_tensor(px[:, :, C_C], rc[:, :], pen[:, bass.ds(g.n * J, J)], ALU.add
                                ).then_inc(*po_r.done("C"))

            def scatter_rows(g):
                wait(po, dv_r, g.n, "B")
                wait(po, po_r, g.n, "C")
                wait(po, ac_r, g.n, "id")
                wait(po, dv_r, g.n, "al")
                wait(po, dv_r, g.n, "si")
                for j in range(J):
                    v.indirect_dma_start(
                        out=rows, out_offset=bass.IndirectOffsetOnAxis(ap=sli[g.par][:, j:j + 1], axis=0),
                        in_=pay[g.par][:, j, :], in_offset=None).then_inc(d_s[g.par], 16)

            def one(g):
                stage(g, 3, sum_biases)
                stage(g, 4, std_x2)
                stage(g, 0, std_x)
                stage(g, 1, x_bias)
                stage(g, 5, scatter_rows)
                stage(g, 0, q_sum)
                stage(g, 0, k_sum)
                stage(g, 0, q_low)
                stage(g, 2, std_x1)
                stage(g, 4, std_norm)
                stage(g, 0, k_low)
                stage(g, 3, std_y)
                stage(g, 4, row_scalars)
                stage(g, 3, gain)
                stage(g, 3, x2_sum)

            v.memset(half[:, :], -0.5)
            for i in range(2):
                v.memset(kst[i][:, :, :, :].bitcast(FP32), 0.0)
            v.memset(k2[:, :, :, :], 0.0).then_inc(s_pz, 1)
            po.wait_ge(s_pz, 1)
            for i in range(2):
                kd = kst[i][96:104, :, :, :].bitcast(FP32).rearrange("p r (j b) (c k) -> p r j b c k", b=2, c=2)
                for r_ in range(4):
                    for b in range(2):
                        last = v.memset(kd[:, r_, :, b, b, :], 1.0)
            last.then_inc(s_pool, 1)
            po.wait_ge(d_const, 16 * N_CONST)
            po.wait_ge(s_pool, 1)
            po.wait_ge(s_vec, 3)

            rounds(nc.gpsimd, one)

            def step(b):
                u, q = b.c % 2, b.c % RB
                wait_rows(po, b)
                wait_b(po, "dve_yo", b.n - RB)
                v.tensor_scalar(bs[q][:, :], rb[q][:, 0:D], rb[q][:, C_R:C_R + 1], rb[q][:, C_C:C_C + 1],
                                ALU.mult, ALU.add).then_inc(*ffn["pool_base"].done("pool_base"))
                wait_out(po, b)
                v.tensor_copy(idi[b.c % 4][:, :], rb[q][:, C_ID:C_ID + 1]).then_inc(*ffn["pool_id"].done("pool_id"))

            def scatter(b):
                u = b.c % 2
                wait_b(po, "pool_id", b.n)
                wait_b(po, "dve_yo", b.n)
                v.indirect_dma_start(
                    out=o_rows, out_offset=bass.IndirectOffsetOnAxis(ap=idi[b.c % 4][:, 0:1], axis=0),
                    in_=yo[b.c % 4][:, :], in_offset=None, bounds_check=T - 1, oob_is_err=False
                ).then_inc(d_o[b.c % 4], 16)

            step(Block(0))
            for c in range(RB):
                step(Block(c + 1))
                scatter(Block(c))
            with nc.gpsimd.Fori(1, NBLK // RB - 1) as it:
                for u in range(RB):
                    step(Block(u + 1, it, RB))
                    scatter(Block(u, it, RB))
            for c in range(NBLK - RB, NBLK):
                if c + 1 < NBLK:
                    step(Block(c + 1))
                scatter(Block(c))


def _constants(nb):
    t = nb * SQ
    p = np.arange(P)
    half = HD // 2
    inv = (1.0 / np.float32(10000.0) ** (np.arange(half, dtype=np.float32) / half)).astype(np.float32)
    ang = np.outer(np.arange(SQ, dtype=np.float32), inv).astype(np.float32)
    cos = np.cos(ang).T[p % half]
    sin = np.sin(ang).T[p % half] * np.where(p % HD < half, -1.0, 1.0)[:, None]
    scale = 1.0 / np.sqrt(np.float64(HD))
    dk = float(np.float32(np.sqrt(np.float16(HD))) + np.float32(1e-8))
    own = (p[:, None] // HD == p[None, :] // HD) / dk
    own4 = (p[:, None] % 32) // HD == np.arange(4)
    own4s = np.where(p[:, None] < 96, own4, p[:, None] % 4 == np.arange(4))
    nblk = t // P + E
    rep = lambda a: np.broadcast_to(a, (P, len(a)))
    cols = [cos * scale, sin * scale, cos, sin, own, np.eye(P), own4, own4s, rep(np.arange(E)),
            p[:, None] + P * np.arange(t // P), p[:, None] < p[None, :], rep(np.arange(nblk))]
    consts = np.concatenate([np.asarray(c, np.float32) for c in cols], axis=1)
    q = p % SQ
    later = np.arange(SQ)[None, :] > q[:, None]
    negq = np.where(later, NEG, 0.0).astype(np.float32)
    earlier = np.arange(SQ)[None, :] < q[:, None]
    negk = np.where(earlier, NEG, 0.0).astype(np.float32)
    pad = np.zeros((P, ROW), np.float32)
    pad[:, C_ID] = t + p
    return consts, negq, negk, pad


def kernel(x, ctx_1024, mask_Bx1xSxS2_bf0, L0_attn_qkv_w, L0_attn_qkv_b, L0_attn_out_w, L0_attn_out_b,
           L0_xattn_wq_w, L0_xattn_wq_b, L0_xattn_wk_w, L0_xattn_wk_b, L0_xattn_wv_w, L0_xattn_wv_b,
           L0_xattn_wo_w, L0_xattn_wo_b, L0_xattn_ln_g, L0_xattn_ln_b, L0_ffn_centroids, L0_ffn_ln_g,
           L0_ffn_ln_b, L0_ffn_w1, L0_ffn_b1, L0_ffn_w2, L0_ffn_b2):
    import concourse.bacc as bacc
    from concourse.bass_utils import run_bass_kernel_spmd

    a = lambda v: np.asarray(v)
    qkv, qb = a(L0_attn_qkv_w), a(L0_attn_qkv_b)
    partner = np.arange(D) ^ (HD // 2)
    wq, wk, wv = qkv[:D], qkv[D:2 * D], qkv[2 * D:]
    bq, bk, bv = qb[:D], qb[D:2 * D], qb[2 * D:]
    wself = np.stack([w.T for w in (wq, wq[partner], wk, wk[partner], wv, a(L0_attn_out_w))], axis=1)
    wcross = np.stack([a(w).T for w in (L0_xattn_wq_w, L0_xattn_wk_w, L0_xattn_wv_w, L0_xattn_wo_w)], axis=1)
    bcol = np.stack([bq, bq[partner], bk, bk[partner], a(L0_xattn_wq_b), bv], axis=1)
    brow = np.concatenate([a(L0_attn_out_b), a(L0_xattn_wo_b), a(L0_xattn_ln_g), a(L0_xattn_ln_b),
                           a(L0_xattn_wk_b), a(L0_xattn_wv_b)])
    consts, negq, negk, pad = _constants(x.shape[0])
    arrays = {
        "x": a(x), "ctx": a(ctx_1024), "mask": a(mask_Bx1xSxS2_bf0).view(np.int32),
        "wself": wself, "wcross": wcross, "bcol": bcol, "brow": brow,
        "cent": a(L0_ffn_centroids).T,
        "w1t": a(L0_ffn_w1).transpose(2, 0, 1),
        "lngb": np.stack([a(L0_ffn_ln_g).T, a(L0_ffn_ln_b).T], axis=1),
        "b1c": a(L0_ffn_b1).reshape(E, FC, P).transpose(2, 0, 1),
        "w2t": a(L0_ffn_w2).reshape(E, D, FC, P).transpose(3, 0, 2, 1),
        "b2r": a(L0_ffn_b2).reshape(-1),
        "consts": consts, "negq": negq, "negk": negk, "padc": pad,
    }
    arrays = {f"in_{n}": np.ascontiguousarray(v) for n, v in arrays.items()}
    nc = bacc.Bacc("TRN2", target_bir_lowering=False, num_devices=1)
    args = [nc.dram_tensor(n, v.shape, mybir.dt.from_np(v.dtype), kind="ExternalInput").ap()
            for n, v in arrays.items()]
    args.append(nc.dram_tensor("out", x.shape, FP32, kind="ExternalOutput").ap())
    decoder_kernel(nc, *args)
    r = run_bass_kernel_spmd(nc, [arrays], core_ids=[0])
    return r.results[0]["out"]
```
